# Optimizing a Trainium2 kernel written in Bass

```python
import numpy as np
import jax
import jax.numpy as jnp

def _softmax(x, axis=-1):
    return jax.nn.softmax(x, axis=axis)

def _gelu(x):
    return jax.nn.gelu(x, approximate=True)

def _silu(x):
    return jax.nn.silu(x)

def _sigmoid(x):
    return jax.nn.sigmoid(x)

def _layernorm(x, axis=-1, eps=1e-05):
    m = jnp.mean(x, axis=axis, keepdims=True)
    v = jnp.var(x, axis=axis, keepdims=True)
    return (x - m) / jnp.sqrt(v + eps)

def _scatter_add(tgt, idx, src, axis=0):
    return tgt.at[idx].add(src)

def _segment_sum(src, seg, n):
    return jax.ops.segment_sum(src, seg, n)
kernel_name = 'mk_gps_d2_gnn_r8_3ec615'

def setup_inputs(seed: int=0):
    np.random.seed(seed)
    _w = jnp.asarray

    def _rec_inputs():
        import jax
        import jax.numpy as jnp
        _gk = jax.random.key(seed)
        x = -0.0003713 + 1 * jax.random.normal(jax.random.fold_in(_gk, 1), (6250, 256), jnp.float32)
        src = jax.random.randint(jax.random.fold_in(_gk, 2), (200000,), 0, 6250, jnp.int32)
        dst = jnp.minimum((6250 * jax.random.uniform(jax.random.fold_in(_gk, 3), (200000,)) ** 2.0).astype(jnp.int32), 49999)
        _o = jnp.argsort(dst, stable=True)
        src = src[_o]
        dst = dst[_o]
        return (x, src, dst)
    x, src, dst = _rec_inputs()

    def _L0_gnn_setup():
        import jax, jax.numpy as jnp
        import numpy as np
        N = 6250
        E = 100000
        H = 8
        C = 32
        HS = H * C
        NEG_SLOPE = 0.2
        EPS = 1e-16
        key = jax.random.key(seed)
        ks = jax.random.split(key, 6)
        x = jax.random.normal(ks[0], (N, HS), dtype=jnp.float32)
        edge_index = jax.random.randint(ks[1], (2, E), 0, N, dtype=jnp.int64)
        W = jax.random.normal(ks[2], (HS, HS), dtype=jnp.float32) * (1.0 / np.sqrt(HS))
        att_src = jax.random.normal(ks[3], (H, C), dtype=jnp.float32) * (1.0 / np.sqrt(C))
        att_dst = jax.random.normal(ks[4], (H, C), dtype=jnp.float32) * (1.0 / np.sqrt(C))
        bias = jax.random.normal(ks[5], (HS,), dtype=jnp.float32) * 0.02
        return {'x': x, 'edge_index': edge_index, 'W': W, 'att_src': att_src, 'att_dst': att_dst, 'bias': bias}
    _L0_gnn_all = _L0_gnn_setup()
    _L0_gnn_in = {k: v for k, v in _L0_gnn_all.items() if k in ('W', 'att_src', 'att_dst', 'bias')}
    del _L0_gnn_all

    def _L0_mix_setup():
        import jax, jax.numpy as jnp
        import numpy as np
        BN_EPS = 1e-05
        key = jax.random.key(seed)
        ks = jax.random.split(key, 4)
        B, N, D = (8, 1024, 256)
        outD = 256
        s = 1.0 / np.sqrt(D)
        return {'feature': jax.random.normal(ks[0], (B, N, D), dtype=jnp.float32), 'W_qk': jax.random.normal(ks[1], (2, D, D), dtype=jnp.float32) * s, 'b_qk': jnp.zeros((2, D), dtype=jnp.float32), 'W_v': jax.random.normal(ks[2], (D, outD), dtype=jnp.float32) * s, 'b_v': jnp.zeros((outD,), dtype=jnp.float32), 'gamma': jnp.ones((D,), dtype=jnp.float32), 'beta': jnp.zeros((D,), dtype=jnp.float32)}
    _L0_mix_all = _L0_mix_setup()
    _L0_mix_in = {k: v for k, v in _L0_mix_all.items() if k in ('W_qk', 'b_qk', 'W_v', 'b_v', 'gamma', 'beta')}
    del _L0_mix_all

    def _L0_ffn_setup():
        import jax, jax.numpy as jnp
        import numpy as np
        N_EXPERTS = 8
        TOP_K = 2
        key = jax.random.key(seed)
        ks = jax.random.split(key, 5)
        B, T, C, E, H = (8, 256, 256, 8, 682)
        scale = 1.0 / np.sqrt(C)
        return {'x': jax.random.normal(ks[0], (B, T, C), dtype=jnp.float32), 'router_w': jax.random.normal(ks[1], (E, C), dtype=jnp.float32) * scale, 'w1': jax.random.normal(ks[2], (E, H, C), dtype=jnp.float32) * scale, 'w2': jax.random.normal(ks[3], (E, C, H), dtype=jnp.float32) * (1.0 / np.sqrt(H)), 'w3': jax.random.normal(ks[4], (E, H, C), dtype=jnp.float32) * scale}
    _L0_ffn_all = _L0_ffn_setup()
    _L0_ffn_in = {k: v for k, v in _L0_ffn_all.items() if k in ('router_w', 'w1', 'w2', 'w3')}
    del _L0_ffn_all

    def _L1_gnn_setup():
        import jax, jax.numpy as jnp
        import numpy as np
        ALPHA = 0.2

        def _gat_head(node_feats, W, a, src, dst, N):
            h = node_feats @ W
            C = W.shape[1]
            a_l, a_r = (a[0, :C], a[0, C:])
            s_l = h @ a_l
            s_r = h @ a_r
            logits = s_l[src] + s_r[dst]
            e = jnp.exp(-jax.nn.leaky_relu(logits, negative_slope=ALPHA))
            row_sum = jax.ops.segment_sum(e, src, num_segments=N)
            h_prime = jax.ops.segment_sum(e[:, None] * h[dst], src, num_segments=N)
            return jax.nn.elu(h_prime / row_sum[:, None])
        key = jax.random.key(seed)
        k1, k2, k3, k4, k5, k6 = jax.random.split(key, 6)
        N, E, c_in, c_head = (6250, 100000, 256, 128)
        node_feats = jax.random.normal(k1, (N, c_in), dtype=jnp.float32)
        edge_index = jax.random.randint(k2, (2, E), 0, N, dtype=jnp.int64)
        std_W = 1.414 * np.sqrt(2.0 / (c_in + c_head))
        std_a = 1.414 * np.sqrt(2.0 / (1 + 2 * c_head))
        W1 = jax.random.normal(k3, (c_in, c_head), dtype=jnp.float32) * std_W
        a1 = jax.random.normal(k4, (1, 2 * c_head), dtype=jnp.float32) * std_a
        W2 = jax.random.normal(k5, (c_in, c_head), dtype=jnp.float32) * std_W
        a2 = jax.random.normal(k6, (1, 2 * c_head), dtype=jnp.float32) * std_a
        return {'node_feats': node_feats, 'W1': W1, 'a1': a1, 'W2': W2, 'a2': a2, 'edge_index': edge_index, 'N': N}
    _L1_gnn_all = _L1_gnn_setup()
    _L1_gnn_in = {k: v for k, v in _L1_gnn_all.items() if k in ('W1', 'a1', 'W2', 'a2')}
    del _L1_gnn_all

    def _L1_mix_setup():
        import jax, jax.numpy as jnp
        import numpy as np
        MIDC = 256
        HEADS = 8
        HEADC = MIDC // HEADS
        EPS = 1e-05

        def _ln(x, gamma, beta):
            mu = jnp.mean(x, axis=-1, keepdims=True)
            var = jnp.var(x, axis=-1, keepdims=True)
            return (x - mu) * jax.lax.rsqrt(var + EPS) * gamma + beta
        key = jax.random.key(seed)
        ks = jax.random.split(key, 8)
        B, HW, C = (8, 512, MIDC)
        s = 1.0 / np.sqrt(C)
        return {'x': jax.random.normal(ks[0], (B, HW, C), jnp.float32), 'w_qkv': jax.random.normal(ks[1], (C, 3 * C), jnp.float32) * s, 'b_qkv': jnp.zeros((3 * C,), jnp.float32), 'kln_g': jnp.ones((HEADC,), jnp.float32), 'kln_b': jnp.zeros((HEADC,), jnp.float32), 'vln_g': jnp.ones((HEADC,), jnp.float32), 'vln_b': jnp.zeros((HEADC,), jnp.float32), 'w1': jax.random.normal(ks[2], (C, C), jnp.float32) * s, 'b1': jnp.zeros((C,), jnp.float32), 'w2': jax.random.normal(ks[3], (C, C), jnp.float32) * s, 'b2': jnp.zeros((C,), jnp.float32)}
    _L1_mix_all = _L1_mix_setup()
    _L1_mix_in = {k: v for k, v in _L1_mix_all.items() if k in ('w_qkv', 'b_qkv', 'kln_g', 'kln_b', 'vln_g', 'vln_b', 'w1', 'b1', 'w2', 'b2')}
    del _L1_mix_all

    def _L1_ffn_setup():
        import jax, jax.numpy as jnp
        import numpy as np
        DIM = 256
        H = 8
        D = 64
        G = 64
        INNER = H * D
        SCALE = D ** (-0.5)
        key = jax.random.key(seed)
        ks = jax.random.split(key, 12)
        B, N = (4, 2048)
        x = jax.random.normal(ks[0], (B, N, DIM), dtype=jnp.float32)
        s = lambda fan_in: 1.0 / np.sqrt(fan_in)
        W_fx = jax.random.normal(ks[1], (DIM, INNER), dtype=jnp.float32) * s(DIM)
        b_fx = jnp.zeros((INNER,), dtype=jnp.float32)
        W_x = jax.random.normal(ks[2], (DIM, INNER), dtype=jnp.float32) * s(DIM)
        b_x = jnp.zeros((INNER,), dtype=jnp.float32)
        A = jax.random.normal(ks[3], (G, D), dtype=jnp.float32)
        Q, _ = jnp.linalg.qr(A.T)
        W_slice = Q[:, :G].astype(jnp.float32)
        b_slice = jnp.zeros((G,), dtype=jnp.float32)
        W_q = jax.random.normal(ks[4], (D, D), dtype=jnp.float32) * s(D)
        W_k = jax.random.normal(ks[5], (D, D), dtype=jnp.float32) * s(D)
        W_v = jax.random.normal(ks[6], (D, D), dtype=jnp.float32) * s(D)
        W_out = jax.random.normal(ks[7], (INNER, DIM), dtype=jnp.float32) * s(INNER)
        b_out = jnp.zeros((DIM,), dtype=jnp.float32)
        temperature = jnp.ones((1, H, 1, 1), dtype=jnp.float32) * 0.5
        return {'x': x, 'W_fx': W_fx, 'b_fx': b_fx, 'W_x': W_x, 'b_x': b_x, 'W_slice': W_slice, 'b_slice': b_slice, 'W_q': W_q, 'W_k': W_k, 'W_v': W_v, 'W_out': W_out, 'b_out': b_out, 'temperature': temperature}
    _L1_ffn_all = _L1_ffn_setup()
    _L1_ffn_in = {k: v for k, v in _L1_ffn_all.items() if k in ('W_fx', 'b_fx', 'W_x', 'b_x', 'W_slice', 'b_slice', 'W_q', 'W_k', 'W_v', 'W_out', 'b_out', 'temperature')}
    del _L1_ffn_all
    return {'x': x, 'src': src, 'dst': dst, 'L0_gnn_W': _L0_gnn_in['W'], 'L0_gnn_att_src': _L0_gnn_in['att_src'], 'L0_gnn_att_dst': _L0_gnn_in['att_dst'], 'L0_gnn_bias': _L0_gnn_in['bias'], 'L0_mix_W_qk': _L0_mix_in['W_qk'], 'L0_mix_b_qk': _L0_mix_in['b_qk'], 'L0_mix_W_v': _L0_mix_in['W_v'], 'L0_mix_b_v': _L0_mix_in['b_v'], 'L0_mix_gamma': _L0_mix_in['gamma'], 'L0_mix_beta': _L0_mix_in['beta'], 'L0_ffn_router_w': _L0_ffn_in['router_w'], 'L0_ffn_w1': _L0_ffn_in['w1'], 'L0_ffn_w2': _L0_ffn_in['w2'], 'L0_ffn_w3': _L0_ffn_in['w3'], 'L1_gnn_W1': _L1_gnn_in['W1'], 'L1_gnn_a1': _L1_gnn_in['a1'], 'L1_gnn_W2': _L1_gnn_in['W2'], 'L1_gnn_a2': _L1_gnn_in['a2'], 'L1_mix_w_qkv': _L1_mix_in['w_qkv'], 'L1_mix_b_qkv': _L1_mix_in['b_qkv'], 'L1_mix_kln_g': _L1_mix_in['kln_g'], 'L1_mix_kln_b': _L1_mix_in['kln_b'], 'L1_mix_vln_g': _L1_mix_in['vln_g'], 'L1_mix_vln_b': _L1_mix_in['vln_b'], 'L1_mix_w1': _L1_mix_in['w1'], 'L1_mix_b1': _L1_mix_in['b1'], 'L1_mix_w2': _L1_mix_in['w2'], 'L1_mix_b2': _L1_mix_in['b2'], 'L1_ffn_W_fx': _L1_ffn_in['W_fx'], 'L1_ffn_b_fx': _L1_ffn_in['b_fx'], 'L1_ffn_W_x': _L1_ffn_in['W_x'], 'L1_ffn_b_x': _L1_ffn_in['b_x'], 'L1_ffn_W_slice': _L1_ffn_in['W_slice'], 'L1_ffn_b_slice': _L1_ffn_in['b_slice'], 'L1_ffn_W_q': _L1_ffn_in['W_q'], 'L1_ffn_W_k': _L1_ffn_in['W_k'], 'L1_ffn_W_v': _L1_ffn_in['W_v'], 'L1_ffn_W_out': _L1_ffn_in['W_out'], 'L1_ffn_b_out': _L1_ffn_in['b_out'], 'L1_ffn_temperature': _L1_ffn_in['temperature']}

def reference(x, src, dst, L0_gnn_W, L0_gnn_att_src, L0_gnn_att_dst, L0_gnn_bias, L0_mix_W_qk, L0_mix_b_qk, L0_mix_W_v, L0_mix_b_v, L0_mix_gamma, L0_mix_beta, L0_ffn_router_w, L0_ffn_w1, L0_ffn_w2, L0_ffn_w3, L1_gnn_W1, L1_gnn_a1, L1_gnn_W2, L1_gnn_a2, L1_mix_w_qkv, L1_mix_b_qkv, L1_mix_kln_g, L1_mix_kln_b, L1_mix_vln_g, L1_mix_vln_b, L1_mix_w1, L1_mix_b1, L1_mix_w2, L1_mix_b2, L1_ffn_W_fx, L1_ffn_b_fx, L1_ffn_W_x, L1_ffn_b_x, L1_ffn_W_slice, L1_ffn_b_slice, L1_ffn_W_q, L1_ffn_W_k, L1_ffn_W_v, L1_ffn_W_out, L1_ffn_b_out, L1_ffn_temperature):
    import jax
    import jax.numpy as jnp

    def _L0_gnn_ref(x, edge_index, W, att_src, att_dst, bias):
        import jax, jax.numpy as jnp
        import numpy as np
        N = 6250
        E = 100000
        H = 8
        C = 32
        HS = H * C
        NEG_SLOPE = 0.2
        EPS = 1e-16
        src, dst = (edge_index[0], edge_index[1])
        xw = (x @ W).reshape(N, H, C)
        a_src = jnp.einsum('nhc,hc->nh', xw, att_src)
        a_dst = jnp.einsum('nhc,hc->nh', xw, att_dst)
        e = a_src[src] + a_dst[dst]
        e = jax.nn.leaky_relu(e, NEG_SLOPE)
        m = jax.ops.segment_max(e, dst, num_segments=N)
        m = jnp.where(jnp.isfinite(m), m, 0.0)
        ex = jnp.exp(e - m[dst])
        denom = jax.ops.segment_sum(ex, dst, num_segments=N)
        alpha = ex / (denom[dst] + EPS)
        msg = xw[src] * alpha[:, :, None]
        out = jax.ops.segment_sum(msg, dst, num_segments=N)
        out = out.reshape(N, HS) + bias
        return jax.nn.relu(out)

    def _L0_mix_ref(feature, W_qk, b_qk, W_v, b_v, gamma, beta):
        import jax, jax.numpy as jnp
        import numpy as np
        BN_EPS = 1e-05
        QK = jnp.einsum('bnd,kde->bkne', feature, W_qk) + b_qk[None, :, None, :]
        value = jnp.einsum('bnd,de->bne', feature, W_v) + b_v
        query = QK[:, 0]
        key = QK[:, 1]
        sm = jax.nn.softmax(key, axis=1)
        lam = jnp.einsum('bnd,bne->bde', sm, value)
        mean = jnp.mean(lam, axis=(0, 2), keepdims=True)
        var = jnp.var(lam, axis=(0, 2), keepdims=True)
        bn = (lam - mean) * jax.lax.rsqrt(var + BN_EPS)
        bn = bn * gamma[None, :, None] + beta[None, :, None]
        return jnp.einsum('bnd,bde->bne', query, bn)

    def _L0_ffn_ref(x, router_w, w1, w2, w3):
        import jax, jax.numpy as jnp
        import numpy as np
        N_EXPERTS = 8
        TOP_K = 2
        B, T, C = x.shape
        flat = x.reshape(-1, C)
        logits = flat @ router_w.T
        probs = jax.nn.softmax(logits, axis=-1)
        topk_probs, topk_idx = jax.lax.top_k(probs, TOP_K)
        topk_probs = topk_probs / (jnp.sum(topk_probs, axis=-1, keepdims=True) + 1e-09)
        onehot = jax.nn.one_hot(topk_idx, N_EXPERTS, dtype=flat.dtype)
        gates = jnp.einsum('nk,nke->ne', topk_probs, onehot)
        h1 = jnp.einsum('nc,ehc->neh', flat, w1)
        h3 = jnp.einsum('nc,ehc->neh', flat, w3)
        h = jax.nn.silu(h1) * h3
        y = jnp.einsum('neh,ech->nec', h, w2)
        out = jnp.einsum('ne,nec->nc', gates, y)
        return out.reshape(B, T, C)

    def _L1_gnn_ref(node_feats, W1, a1, W2, a2, edge_index, N):
        import jax, jax.numpy as jnp
        import numpy as np
        ALPHA = 0.2

        def _gat_head(node_feats, W, a, src, dst, N):
            h = node_feats @ W
            C = W.shape[1]
            a_l, a_r = (a[0, :C], a[0, C:])
            s_l = h @ a_l
            s_r = h @ a_r
            logits = s_l[src] + s_r[dst]
            e = jnp.exp(-jax.nn.leaky_relu(logits, negative_slope=ALPHA))
            row_sum = jax.ops.segment_sum(e, src, num_segments=N)
            h_prime = jax.ops.segment_sum(e[:, None] * h[dst], src, num_segments=N)
            return jax.nn.elu(h_prime / row_sum[:, None])
        src, dst = (edge_index[0], edge_index[1])
        out1 = _gat_head(node_feats, W1, a1, src, dst, N)
        out2 = _gat_head(node_feats, W2, a2, src, dst, N)
        return jnp.concatenate([out1, out2], axis=1)

    def _L1_mix_ref(x, w_qkv, b_qkv, kln_g, kln_b, vln_g, vln_b, w1, b1, w2, b2):
        import jax, jax.numpy as jnp
        import numpy as np
        MIDC = 256
        HEADS = 8
        HEADC = MIDC // HEADS
        EPS = 1e-05

        def _ln(x, gamma, beta):
            mu = jnp.mean(x, axis=-1, keepdims=True)
            var = jnp.var(x, axis=-1, keepdims=True)
            return (x - mu) * jax.lax.rsqrt(var + EPS) * gamma + beta
        B, HW, C = x.shape
        bias = x
        qkv = (x @ w_qkv + b_qkv).reshape(B, HW, HEADS, 3 * HEADC)
        qkv = qkv.transpose(0, 2, 1, 3)
        q, k, v = jnp.split(qkv, 3, axis=-1)
        k = _ln(k, kln_g, kln_b)
        v = _ln(v, vln_g, vln_b)
        kv = jnp.einsum('bhnd,bhne->bhde', k, v) / HW
        out = jnp.einsum('bhnd,bhde->bhne', q, kv)
        out = out.transpose(0, 2, 1, 3).reshape(B, HW, C)
        ret = out + bias
        h = jax.nn.gelu(ret @ w1 + b1, approximate=False)
        return h @ w2 + b2 + bias

    def _L1_ffn_ref(x, W_fx, b_fx, W_x, b_x, W_slice, b_slice, W_q, W_k, W_v, W_out, b_out, temperature):
        import jax, jax.numpy as jnp
        import numpy as np
        DIM = 256
        H = 8
        D = 64
        G = 64
        INNER = H * D
        SCALE = D ** (-0.5)
        B, N, _ = x.shape
        fx_mid = (x @ W_fx + b_fx).reshape(B, N, H, D).transpose(0, 2, 1, 3)
        x_mid = (x @ W_x + b_x).reshape(B, N, H, D).transpose(0, 2, 1, 3)
        temp = jnp.clip(temperature, 0.1, 5.0)
        slice_weights = jax.nn.softmax((x_mid @ W_slice + b_slice) / temp, axis=-1)
        slice_norm = slice_weights.sum(axis=2)
        slice_token = jnp.einsum('bhnc,bhng->bhgc', fx_mid, slice_weights)
        slice_token = slice_token / (slice_norm[..., None] + 1e-05)
        q = slice_token @ W_q
        k = slice_token @ W_k
        v = slice_token @ W_v
        attn = jax.nn.softmax(jnp.einsum('bhgc,bhkc->bhgk', q, k) * SCALE, axis=-1)
        out_slice = jnp.einsum('bhgk,bhkc->bhgc', attn, v)
        out_x = jnp.einsum('bhgc,bhng->bhnc', out_slice, slice_weights)
        out_x = out_x.transpose(0, 2, 1, 3).reshape(B, N, INNER)
        return out_x @ W_out + b_out
    edge_index = jnp.stack([src, dst])
    xn = _layernorm(x, axis=-1)
    x = x + _L0_gnn_ref(xn, edge_index, L0_gnn_W, L0_gnn_att_src, L0_gnn_att_dst, L0_gnn_bias) + _L0_mix_ref(xn[None], L0_mix_W_qk, L0_mix_b_qk, L0_mix_W_v, L0_mix_b_v, L0_mix_gamma, L0_mix_beta)[0]
    x = x + _L0_ffn_ref(_layernorm(x, axis=-1)[None], L0_ffn_router_w, L0_ffn_w1, L0_ffn_w2, L0_ffn_w3)[0]
    xn = _layernorm(x, axis=-1)
    x = x + _L1_gnn_ref(xn, L1_gnn_W1, L1_gnn_a1, L1_gnn_W2, L1_gnn_a2, edge_index, 6250) + _L1_mix_ref(xn[None], L1_mix_w_qkv, L1_mix_b_qkv, L1_mix_kln_g, L1_mix_kln_b, L1_mix_vln_g, L1_mix_vln_b, L1_mix_w1, L1_mix_b1, L1_mix_w2, L1_mix_b2)[0]
    x = x + _L1_ffn_ref(_layernorm(x, axis=-1)[None], L1_ffn_W_fx, L1_ffn_b_fx, L1_ffn_W_x, L1_ffn_b_x, L1_ffn_W_slice, L1_ffn_b_slice, L1_ffn_W_q, L1_ffn_W_k, L1_ffn_W_v, L1_ffn_W_out, L1_ffn_b_out, L1_ffn_temperature)[0]
    return x

_drawn_inputs = setup_inputs


def setup_inputs(seed=0):
    import zlib

    import numpy as np

    out = dict(_drawn_inputs(seed))
    spreads = {'L0_mix_b_qk': (0.0, 0.1),
     'L0_mix_b_v': (0.0, 0.1),
     'L0_mix_gamma': (1.0, 0.2),
     'L0_mix_beta': (0.0, 0.8),
     'L1_mix_b_qkv': (0.0, 0.49),
     'L1_mix_kln_g': (1.0, 0.6),
     'L1_mix_kln_b': (0.0, 0.8),
     'L1_mix_vln_g': (1.0, 0.6),
     'L1_mix_vln_b': (0.0, 0.8),
     'L1_mix_b1': (0.0, 0.8),
     'L1_mix_b2': (0.0, 0.8),
     'L1_ffn_b_fx': (0.0, 0.8),
     'L1_ffn_b_x': (0.0, 0.8),
     'L1_ffn_b_slice': (0.0, 0.8),
     'L1_ffn_b_out': (0.0, 2.0),
     'L1_ffn_temperature': (0.5, 0.6)}
    factors = {'L0_gnn_W': 5.701,
     'L0_gnn_att_src': 7.442,
     'L0_gnn_att_dst': 8.0,
     'L0_gnn_bias': 8.0,
     'L1_gnn_W1': 2.687,
     'L1_gnn_W2': 3.555,
     'L1_gnn_a2': 4.276,
     'L1_ffn_W_fx': 6.769,
     'L1_ffn_W_x': 8.0,
     'L1_ffn_W_slice': 8.0,
     'L1_ffn_W_q': 8.0,
     'L1_ffn_W_k': 8.0,
     'L1_ffn_W_v': 5.569,
     'L1_ffn_W_out': 5.486}
    for name, (base, spread) in spreads.items():
        noise = np.random.default_rng([zlib.crc32(name.encode()), seed]).standard_normal(out[name].shape)
        drawn = base * np.exp(spread * noise) if base else spread * noise
        out[name] = jnp.asarray(drawn.astype(out[name].dtype))
    for name, factor in factors.items():
        out[name] = (out[name] * factor).astype(out[name].dtype)
    return out
```

```python
from contextlib import ExitStack

import concourse.bass as bass
from concourse import mybir

F32 = mybir.dt.float32
I32 = mybir.dt.int32
ALU = mybir.AluOpType
ACT = mybir.ActivationFunctionType
AX = mybir.AxisListType.X

N = 6250
D = 256
E = 200000
P = 125
NT = N // P
KC = D // 128
EJ = E // P
TILE = 128
TILES = -(-(E // TILE + NT) // 16) * 16
SEG = -(-TILES // 128)
TPAD = SEG * 128
BATCH = 8
CH = 2 * P
NCH = N // CH
BIG = 1e30
SEND = 32
TURNS = EJ // SEND


class Link:

    def __init__(self, eng, sem, start=0):
        self.eng, self.sem, self.base, self.k = eng, sem, start, 0

    def begin(self, per):
        self.start, self.per, self.k = self.base + self.k, per, 0

    def turn(self, i):
        assert self.k in (0, self.per), (self.k, self.per)
        self.base, self.k = i * self.per + self.start, 0

    def close(self, turns):
        assert self.k == self.per, (self.k, self.per)
        self.base, self.k = self.start + turns * self.per, 0

    def put(self, ins):
        self.k += 1
        return ins.then_inc(self.sem, 1)

    def __call__(self, ins, hold=False):
        self.put(ins)
        self.eng.wait_ge(self.sem, self.base + self.k)
        if hold:
            self.eng.nop(nofuse=True)


def turns(eng, n):
    yield 0, True
    with eng.Fori(1, n) as i:
        yield i, False


def bc(ap, axis, n):
    a = ap.unsqueeze(axis)
    shape = list(a.shape)
    shape[axis] = n
    return a.broadcast_to(shape)


def numbers(nc, engine, ap, top):
    _, values = nc.values_load_multi_w_load_instructions(
        ap, engines=[engine], min_val=0, max_val=top,
        skip_runtime_bounds_check_because="they are counts of blocks, below NT by their making")
    return values


class Room:

    def __init__(self, nc, tag):
        self.nc, self.tag, self.stack, self.sems = nc, tag, ExitStack(), []

    def __enter__(self):
        self.stack.__enter__()
        return self

    def __exit__(self, *a):
        with self.nc.Block() as block:

            @block.sync
            def _(sp):
                for sem in self.sems:
                    sp.sem_clear(sem)
        return self.stack.__exit__(*a)

    def sb(self, name, shape, dt=F32):
        return self.stack.enter_context(self.nc.sbuf_tensor(f"{self.tag}_{name}", shape, dt))

    def ps(self, name, shape, dt=F32):
        return self.stack.enter_context(self.nc.psum_tensor(f"{self.tag}_{name}", shape, dt))

    def own_sems(self, name):
        return [self.nc.alloc_semaphore(name=f"{self.tag}_{name}{u}") for u in range(2)]

    def sem(self, name):
        self.sems.append(self.stack.enter_context(self.nc.semaphore(f"{self.tag}_{name}")))
        return self.sems[-1]


def constants(nc, room):
    c = {
        "ident": room.sb("ident", [128, 128]),
        "ones": room.sb("ones", [128, 128]),
        "before": room.sb("before", [P, P]),
        "count": room.sb("count", [128, 128]),
        "zero": room.sb("zero", [128, 128]),
    }
    count_i = room.sb("count_i", [128, 128], I32)
    filled, made = room.sem("filled"), room.sem("made")
    with nc.Block() as block:

        @block.gpsimd
        def _(pool):
            pool.memset(c["ident"][:, :], 0.0).then_inc(filled, 1)
            pool.memset(c["ones"][:, :], 1.0).then_inc(filled, 1)
            pool.memset(c["before"][:, :], 1.0).then_inc(filled, 1)
            pool.memset(c["zero"][:, :], 0.0).then_inc(filled, 1)
            pool.iota(count_i[:, :], pattern=[[1, 128]], base=0, channel_multiplier=0).then_inc(filled, 1)
            pool.wait_ge(filled, 5)
            pool.affine_select(out=c["ident"][:, :], in_=c["ident"][:, :], compare_op=ALU.not_equal, fill=1.0,
                               base=0, pattern=[[-1, 128]], channel_multiplier=1).then_inc(made, 1)
            pool.affine_select(out=c["before"][:, :], in_=c["before"][:, :], compare_op=ALU.is_gt, fill=0.0,
                               base=0, pattern=[[1, P]], channel_multiplier=-1).then_inc(made, 1)

        @block.vector
        def _(dve):
            dve.wait_ge(filled, 5)
            dve.tensor_copy(c["count"][:, :], count_i[:, :]).then_inc(made, 1)
    return c


class Sender:

    def __init__(self, nc, room, rec):
        self.nc, self.rec = nc, rec
        self.rec3 = room.sb("rec3", [P, EJ, 3])
        self.stage = room.sb("stage", [P, SEND, 3])
        self.staged, self.sent = room.own_sems("staged")[0], room.own_sems("sent")

    def send(self, pool, lo, hi):
        with pool.Fori(lo, hi) as i:
            pool.tensor_copy(self.stage[:, :, :], self.rec3[:, bass.ds(i * SEND, SEND), :]).then_inc(self.staged, 1)
            pool.wait_ge(self.staged, i + 1)
            pool.nop(nofuse=True)
            for k in range(SEND):
                pool.indirect_dma_start(
                    out=self.rec[:, :], out_offset=bass.IndirectOffsetOnAxis(ap=self.stage[:, k, 0:1].bitcast(I32), axis=0),
                    in_=self.stage[:, k, 1:3], in_offset=None).then_inc(self.sent[k // (SEND // 2)], 16)
            for h in range(2):
                pool.wait_ge(self.sent[h], i * (8 * SEND) + 8 * SEND)
            pool.nop(nofuse=True)


def place_edges(nc, c, tag, key, other, sender, tile_end, beside=None):
    rec, rec3 = sender.rec, sender.rec3
    with Room(nc, tag) as room:
        key_i = room.sb("key_i", [P, EJ], I32)
        oth_i = room.sb("oth_i", [P, EJ], I32)
        keyf = room.sb("keyf", [P, EJ])
        blk = room.sb("blk", [P, EJ])
        blk_i = room.sb("blk_i", [P, EJ], I32)
        hit = room.sb("hit", [P, EJ])
        upto = room.sb("upto", [P, EJ])
        pos = room.sb("pos", [P, EJ])
        zeros = room.sb("zeros", [P, EJ])
        cnt = room.sb("cnt", [P, NT])
        tot_i = room.sb("tot_i", [128, NT], I32)
        tiles = room.sb("tiles", [128, NT])
        ends = room.sb("ends", [128, NT])
        base = room.sb("base", [128, NT])
        blank = room.sb("blank", [128, SEG * TILE, 2])
        tot = room.ps("tot", [128, NT])
        pre = room.ps("pre", [128, NT])
        loaded, step, counted, summed = (room.sem(s) for s in ("loaded", "step", "counted", "summed"))
        placed, blanked, blank_set = (room.sem(s) for s in ("placed", "blanked", "blank_set"))
        ended = room.sem("ended")
        rec_rows = rec.rearrange("(q s) w -> q (s w)", q=128)
        with nc.Block() as block:

            @block.sync
            def _(sp):
                sp.dma_start(key_i[:, :], key.rearrange("(p j) -> p j", p=P)).then_inc(loaded, 16)
                sp.dma_start(oth_i[:, :], other.rearrange("(p j) -> p j", p=P)).then_inc(loaded, 16)
                sp.wait_ge(blank_set, 2)
                sp.dma_start(rec_rows, blank[:, :, :].rearrange("p s w -> p (s w)")).then_inc(blanked, 16)
                sp.wait_ge(placed, 1)
                sp.dma_start(tile_end, ends[0:1, :]).then_inc(ended, 16)
                sp.wait_ge(ended, 16)
                sp.wait_ge(blanked, 16)

            @block.vector
            def _(dve):
                link = Link(dve, step)
                link.put(dve.memset(zeros[:, :], 0.0))
                link.put(dve.memset(pos[:, :], 0.0))
                dve.wait_ge(loaded, 32)
                link.put(dve.tensor_copy(rec3[:, :, 1], oth_i[:, :]))
                link(dve.tensor_copy(keyf[:, :], key_i[:, :]))
                link.put(dve.tensor_copy(rec3[:, :, 2], keyf[:, :]))
                link(dve.tensor_scalar(blk[:, :], keyf[:, :], 0.5, 1.0 / P, ALU.add, ALU.mult))
                link(dve.tensor_copy(blk_i[:, :], blk[:, :]))
                link(dve.tensor_copy(blk[:, :], blk_i[:, :]))
                link(dve.scalar_tensor_tensor(hit[:, :], blk[:, :], float(P), keyf[:, :], ALU.mult, ALU.is_gt))
                link(dve.tensor_tensor(blk[:, :], blk[:, :], hit[:, :], ALU.subtract))
                link.begin(1)
                with dve.Fori(0, NT) as b:
                    link.turn(b)
                    link(dve.tensor_scalar(hit[:, :], blk[:, :], c["count"][0:P, bass.ds(b, 1)], 0.0,
                                           ALU.is_equal, ALU.add, accum_out=cnt[:, bass.ds(b, 1)]))
                link.close(NT)
                dve.nop().then_inc(counted, 1)
                dve.wait_ge(summed, 2)
                link(dve.tensor_scalar(tiles[:, :], tot[:, :], float(TILE - 1), None, ALU.add))
                link(dve.tensor_copy(tot_i[:, :], tiles[:, :]))
                link(dve.tensor_scalar(tot_i[:, :], tot_i[:, :], 7, None, ALU.logical_shift_right))
                link(dve.tensor_copy(tiles[:, :], tot_i[:, :]))
                link(dve.tensor_tensor_scan(ends[:, :], tiles[:, :], c["zero"][:, 0:NT],
                                            0.0, ALU.add, ALU.add))
                dve.nop().then_inc(placed, 1)
                link(dve.tensor_tensor(base[:, :], ends[:, :], tiles[:, :], ALU.subtract))
                link(dve.tensor_scalar(base[:, :], base[:, :], float(TILE), -1.0, ALU.mult, ALU.add))
                link(dve.tensor_tensor(base[0:P, :], base[0:P, :], pre[0:P, :], ALU.add))
                link.begin(4)
                with dve.Fori(0, NT) as b:
                    link.turn(b)
                    link(dve.tensor_scalar(hit[:, :], blk[:, :], c["count"][0:P, bass.ds(b, 1)], None, ALU.is_equal))
                    link(dve.tensor_tensor_scan(upto[:, :], hit[:, :], zeros[:, :], base[0:P, bass.ds(b, 1)],
                                                ALU.add, ALU.add))
                    link(dve.scalar_tensor_tensor(upto[:, :], blk[:, :], c["count"][0:P, bass.ds(b, 1)], upto[:, :],
                                                  ALU.is_equal, ALU.mult))
                    link(dve.tensor_tensor(pos[:, :], pos[:, :], upto[:, :], ALU.add))
                link.close(NT)
                link(dve.tensor_copy(rec3[:, :, 0].bitcast(I32), pos[:, :]))
                dve.nop().then_inc(placed, 1)

            @block.tensor
            def _(pe):
                pe.wait_ge(counted, 1)
                pe.matmul(tot[:, :], c["ones"][0:P, :], cnt[:, :], start=True, stop=True).then_inc(summed, 1)
                pe.matmul(pre[0:P, :], c["before"][:, :], cnt[:, :], start=True, stop=True).then_inc(summed, 1)

            @block.gpsimd
            def _(pool):
                pool.memset(blank[:, :, 0], 0.0).then_inc(blank_set, 1)
                pool.memset(blank[:, :, 1], -1.0).then_inc(blank_set, 1)
                if beside is not None:
                    beside(pool)


def lay_slots(nc, c, tag, rec, tile_end, idx, loc, flat_loc, blk, blk_off, width):
    with Room(nc, tag) as room:
        rows = room.sb("rows", [128, SEG, TILE, 2])
        oth = room.sb("oth", [128, TPAD])
        key = room.sb("key", [128, TPAD])
        idx_i = room.sb("idx_i", [128, TPAD], I32)
        locs = room.sb("locs", [128, TPAD])
        minus_first = room.sb("minus_first", [128, SEG])
        flat = room.sb("flat", [128, SEG, TILE])
        blk_i = room.sb("blk_i", [1, TPAD], I32)
        off = room.sb("off", [1, TPAD], I32)
        tcount_i = room.sb("tcount_i", [NT, TPAD], I32)
        tcount = room.sb("tcount", [NT, TPAD])
        end_row = room.sb("end_row", [1, NT])
        end_col = room.sb("end_col", [NT, 1])
        turned = [room.ps(f"turned{i}", [128, 2, 128]) for i in range(2)]
        col = room.ps("col", [128, 1 + SEG])
        blks = [room.ps(f"blk{i}", [128, TPAD // 4]) for i in range(4)]
        loaded, step, turn, copied = (room.sem(s) for s in ("loaded", "step", "turn", "copied"))
        tiled, blocks, col_made, stored = (room.sem(s) for s in ("tiled", "blocks", "col_made", "stored"))
        Q = TPAD // 4
        with nc.Block() as block:

            @block.sync
            def _(sp):
                sp.dma_start(end_row[:, :], tile_end).then_inc(loaded, 16)
                sp.dma_start(rows[:, :, :, :].rearrange("t c p w -> t c (p w)"),
                             rec.rearrange("(c t p) w -> t c (p w)", c=SEG, t=128)).then_inc(loaded, 16)
                sp.wait_ge(stored, 1)
                for a, b in ((idx, idx_i), (loc, locs), (blk, blk_i), (blk_off, off)):
                    sp.dma_start(a, b[:, :]).then_inc(stored, 16)
                sp.dma_start(flat_loc.rearrange("(c t p) -> t c p", c=SEG, t=128), flat[:, :, :]).then_inc(stored, 16)
                sp.wait_ge(stored, 81)

            @block.gpsimd
            def _(pool):
                pool.iota(tcount_i[:, :], pattern=[[1, TPAD]], base=0, channel_multiplier=0).then_inc(tiled, 1)

            @block.tensor
            def _(pe):
                pe.wait_ge(loaded, 32)
                pe.matmul(col[0:NT, 0:1], end_row[:, :], c["ones"][0:1, 0:1], start=True, stop=True).then_inc(col_made, 1)
                for k in range(SEG):
                    if k >= 2:
                        pe.wait_ge(copied, 2 * (k - 1))
                    for w in range(2):
                        pe.transpose(turned[k % 2][:, w, :], rows[:, k, :, w], c["ident"][:, :]).then_inc(turn, 1)
                pe.wait_ge(blocks, 1)
                for q in range(4):
                    pe.matmul(blks[q][:, :], c["ones"][0:NT - 1, :], tcount[0:NT - 1, q * Q:(q + 1) * Q],
                              start=True, stop=True).then_inc(blocks, 1)
                for k in range(SEG):
                    mm = pe.matmul(col[:, 1 + k:2 + k], tcount[0:NT - 1, k * 128:(k + 1) * 128], c["ones"][0:NT - 1, 0:1],
                                   start=True, stop=True)
                mm.then_inc(blocks, 1)

            @block.vector
            def _(dve):
                link = Link(dve, step)
                dve.wait_ge(tiled, 1)
                link(dve.tensor_copy(tcount[:, :], tcount_i[:, :]))
                dve.wait_ge(col_made, 1)
                link(dve.tensor_copy(end_col[:, :], col[0:NT, 0:1]))
                link(dve.tensor_scalar(tcount[:, :], tcount[:, :], end_col[:, 0:1], None, ALU.is_ge))
                dve.nop().then_inc(blocks, 1)
                for k in range(SEG):
                    dve.wait_ge(turn, 2 * k + 2)
                    dve.tensor_copy(oth[:, k * 128:(k + 1) * 128], turned[k % 2][:, 0, :]).then_inc(copied, 1)
                    dve.tensor_copy(key[:, k * 128:(k + 1) * 128], turned[k % 2][:, 1, :]).then_inc(copied, 1)
                dve.wait_ge(copied, 2 * SEG)
                dve.wait_ge(blocks, 6)
                link.put(dve.tensor_copy(idx_i[:, :], oth[:, :]))
                for q in range(4):
                    s = slice(q * Q, (q + 1) * Q)
                    link.put(dve.scalar_tensor_tensor(locs[:, s], blks[q][:, :], -float(P), key[:, s], ALU.mult, ALU.add))
                    link.put(dve.tensor_scalar(off[0:1, s], blks[q][0:1, :], float(width), None, ALU.mult))
                    link.put(dve.tensor_copy(blk_i[0:1, s], blks[q][0:1, :]))
                link(dve.tensor_scalar(minus_first[:, :], col[:, 1:1 + SEG], -float(P), None, ALU.mult))
                link(dve.tensor_tensor(flat[:, :, :], rows[:, :, :, 1], bc(minus_first[:, :], 2, TILE), ALU.add))
                dve.nop().then_inc(stored, 1)


def spread_parts(nc, c, tag, flat_loc, blk, part, out, other=None):
    W = part.shape[1]
    idx, table, other_out = other if other is not None else (None, None, None)
    HALVES = TILES // BATCH
    COLS = BATCH * TILE
    with Room(nc, tag) as room:
        parts = room.sb("parts", [P, NT, W])
        blk_i = room.sb("blk_i", [1, TPAD], I32)
        row = room.sb("row", [1, 2, COLS])
        hotT = room.sb("hotT", [P, 2, COLS])
        slots = room.sb("slots", [128, W, TPAD])
        if other is not None:
            idx_i = room.sb("idx_i", [128, TPAD], I32)
            ids = room.sb("ids", [128, 2, BATCH], I32)
            got = room.sb("got", [128, 2, BATCH, W])
            got_slots = room.sb("got_slots", [128, W, TPAD])
            came = room.own_sems("came")
        idx_in, staged, taken = (room.sem(s) for s in ("idx_in", "staged", "taken"))
        own_i = room.sb("own_i", [P, 1], I32)
        own = room.sb("own", [P, 1])
        psB = [[room.ps(f"psB{u}{q}", [128, 512]) for q in range(2)] for u in range(2)]
        psP = [room.ps(f"psP{u}", [128, BATCH, W]) for u in range(2)]
        loaded, counted, own_ready, widened, hot_ready, parted, copied, cleared, stored = (room.sem(s) for s in (
            "loaded", "counted", "own_ready", "widened", "hot_ready", "parted", "copied", "cleared", "stored"))
        row_in = [room.sem(f"row_in{u}") for u in range(2)]
        flat_row = flat_loc.rearrange("(a s) -> a s", a=1)
        with nc.Block() as block:

            @block.sync
            def _(sp):
                with nc.allow_non_contiguous_dma(reason="rows of a few numbers"):
                    sp.dma_start(parts[:, :, :], part.rearrange("(t p) w -> p t w", p=P)).then_inc(loaded, 16)
                sp.dma_start(blk_i[:, :], blk).then_inc(loaded, 16)
                if other is not None:
                    sp.dma_start(idx_i[:, :], idx).then_inc(idx_in, 16)
                for i, first in turns(sp, HALVES // 2):
                    for u in range(2):
                        n = i * 2 + u
                        if not first:
                            sp.wait_ge(widened, n - 1)
                        sp.dma_start(row[:, u, :], flat_row[:, slice(n * COLS, (n + 1) * COLS) if first else bass.ds(n * COLS, COLS)])\
                          .then_inc(row_in[u], 16)
                sp.wait_ge(copied, HALVES + 2)
                sp.wait_ge(cleared, 1)
                sp.dma_start(out, slots[:, :, :]).then_inc(stored, 16)
                sp.wait_ge(stored, 16)
                if other is not None:
                    sp.wait_ge(taken, HALVES + 2)
                    sp.wait_ge(cleared, 2)
                    sp.dma_start(other_out, got_slots[:, :, :]).then_inc(stored, 16)
                    sp.wait_ge(stored, 32)

            @block.gpsimd
            def _(pool):
                pool.memset(slots[:, :, TILES:TPAD], 0.0).then_inc(cleared, 1)
                pool.iota(own_i[:, :], pattern=[[0, 1]], base=0, channel_multiplier=1).then_inc(counted, 1)
                if other is None:
                    return
                pool.memset(got_slots[:, :, TILES:TPAD], 0.0).then_inc(cleared, 1)
                pool.wait_ge(idx_in, 16)
                with pool.Fori(0, HALVES // 2) as i:
                    for u in range(2):
                        n = i * 2 + u
                        pool.wait_ge(taken, n + 1)
                        pool.nop(nofuse=True)
                        pool.tensor_copy(ids[:, u, :], idx_i[:, bass.ds(n * BATCH, BATCH)]).then_inc(staged, 1)
                        pool.wait_ge(staged, n + 1)
                        pool.nop(nofuse=True)
                        for k in range(BATCH):
                            pool.indirect_dma_start(
                                out=got[:, u, k, :], out_offset=None, in_=table[:, :],
                                in_offset=bass.IndirectOffsetOnAxis(ap=ids[:, u, k:k + 1], axis=0),
                            ).then_inc(came[u], 16)

            @block.tensor
            def _(pe):
                pe.wait_ge(loaded, 32)

                def widen(i, first, u):
                    n = i * 2 + u
                    pe.wait_ge(row_in[u], i * 16 + 16)
                    if not first:
                        pe.wait_ge(hot_ready, n - 1)
                    for q in range(2):
                        mm = pe.matmul(psB[u][q][0:P, :], c["ones"][0:1, 0:P], row[:, u, q * 512:(q + 1) * 512], start=True, stop=True)
                    mm.then_inc(widened, 1)

                def pick(n, u):
                    pe.wait_ge(hot_ready, n + 1)
                    pe.wait_ge(copied, n + 1)
                    at = slice(n * BATCH, (n + 1) * BATCH) if isinstance(n, int) else bass.ds(n * BATCH, BATCH)
                    of = numbers(nc, mybir.EngineType.PE, blk_i[0:1, at], NT - 1)
                    for k in range(BATCH):
                        mm = pe.matmul(psP[u][:, k, :], hotT[:, u, k * TILE:(k + 1) * TILE],
                                       parts[:, bass.ds(of[k], 1), :].rearrange("p a w -> p (a w)"), start=True, stop=True)
                    mm.then_inc(parted, 1)

                for i, first in turns(pe, HALVES // 2):
                    widen(i, first, 0)
                    if not first:
                        pick(i * 2 - 1, 1)
                    widen(i, first, 1)
                    pick(i * 2, 0)
                pick(HALVES - 1, 1)

            @block.vector
            def _(dve):
                dve.wait_ge(counted, 1)
                dve.tensor_copy(own[:, :], own_i[:, :]).then_inc(own_ready, 1)
                if other is not None:
                    dve.nop().then_inc(taken, 2)
                dve.wait_ge(own_ready, 1)
                for i, first in turns(dve, HALVES // 2):
                    for u in range(2):
                        n = i * 2 + u
                        dve.wait_ge(widened, n + 1)
                        if not first:
                            dve.wait_ge(parted, n - 1)
                        for q in range(2):
                            ins = dve.tensor_scalar(hotT[:, u, q * 512:(q + 1) * 512], psB[u][q][0:P, :], own[:, 0:1], None, ALU.is_equal)
                        ins.then_inc(hot_ready, 1)
                        if other is not None:
                            cols = slice(n * BATCH, (n + 1) * BATCH) if first else bass.ds(n * BATCH, BATCH)
                            dve.wait_ge(came[u], i * (16 * BATCH) + 16 * BATCH)
                            dve.tensor_copy(got_slots[:, :, cols], got[:, u, :, :].rearrange("p k w -> p w k")).then_inc(taken, 1)

            @block.scalar
            def _(act):
                act.nop().then_inc(copied, 2)
                for i, first in turns(act, HALVES // 2):
                    for u in range(2):
                        n = i * 2 + u
                        cols = slice(n * BATCH, (n + 1) * BATCH) if first else bass.ds(n * BATCH, BATCH)
                        act.wait_ge(parted, n + 1)
                        act.nop(nofuse=True)
                        act.activation(slots[:, :, cols], psP[u][:, :, :].rearrange("p k w -> p w k"), ACT.Copy).then_inc(copied, 1)


def project_rows(nc, c, tag, x, xnT, xn_rows, weights, att, outs, beside=None):
    W0 = sum(w.shape[1] for w, _ in weights)
    WA = 1 + max((col for _, _, col in att), default=-1)
    W = W0 + WA
    with Room(nc, tag) as room:
        xin = room.sb("xin", [P, 2, D])
        xn = room.sb("xn", [P, 2, D])
        stats = room.sb("stats", [P, 2, 6])
        mv = room.sb("mv", [P, 2, 2])
        sd = room.sb("sd", [P, 2, 1])
        xT = room.sb("xT", [128, 2, KC, P])
        wext = room.sb("wext", [128, KC, max(W, 1)])
        wT = room.sb("wT", [128, KC, D])
        attm = room.sb("attm", [128, KC, max(WA, 1)])
        res = room.sb("res", [P, 2, max(W, 1)])
        psT = [room.ps(f"psT{u}", [128, KC, P]) for u in range(2)]
        psW = [room.ps(f"psW{u}", [128, 512]) for u in range(2)]
        names = ("weights_in", "att_zero", "att_in", "w_turned", "wT_copied", "att_product", "wext_ready",
                 "step", "var_ready", "sd_ready", "normed", "turned", "xT_ready", "projected", "res_ready")
        s = {n: room.sem(n) for n in names}
        loaded, xT_out, res_out = ([room.sem(f"{n}{u}") for u in range(2)] for n in ("loaded", "xT_out", "res_out"))
        xn_out = room.own_sems("xn_out") if xn_rows is not None else None
        with nc.Block() as block:

            @block.sync
            def _(sp):
                for w, col in weights:
                    with nc.allow_non_contiguous_dma(reason="the router's few rows come as columns"):
                        for k in range(KC):
                            sp.dma_start(wext[:, k, col:col + w.shape[1]], w[k * 128:(k + 1) * 128, :]).then_inc(s["weights_in"], 16)
                if att:
                    sp.wait_ge(s["att_zero"], 1)
                    for src, row, col in att:
                        n = src.shape[0]
                        sp.dma_start(attm[row % 128:row % 128 + n, row // 128, col:col + 1],
                                     src.rearrange("(n a) -> n a", a=1)).then_inc(s["att_in"], 16)
                for i, first in turns(sp, NT // 2):
                    for u in range(2):
                        t = i * 2 + u
                        if not first:
                            sp.wait_ge(s["normed"], t - 1)
                        rows = slice(t * P, (t + 1) * P) if first else bass.ds(t * P, P)
                        sp.dma_start(xin[:, u, :], x[rows, :]).then_inc(loaded[u], 16)

            @block.gpsimd
            def _(pool):
                if att:
                    pool.memset(attm[:, :, :], 0.0).then_inc(s["att_zero"], 1)
                if xn_rows is not None:
                    with pool.Fori(0, NT // 2) as i:
                        for u in range(2):
                            t = i * 2 + u
                            pool.wait_ge(s["normed"], t + 1)
                            pool.nop(nofuse=True)
                            pool.dma_start(xn_rows[bass.ds(t * P, P), :], xn[:, u, :]).then_inc(xn_out[u], 16)
                    for u in range(2):
                        pool.wait_ge(xn_out[u], 16 * (NT // 2))
                if beside is not None:
                    beside(pool)

            @block.vector
            def _(dve):
                link = Link(dve, s["step"])
                if att:
                    dve.wait_ge(s["w_turned"], 2 * KC)
                    for k in range(KC):
                        dve.tensor_copy(wT[:, k, :], psW[k][:, 0:D]).then_inc(s["wT_copied"], 1)
                    dve.wait_ge(s["att_product"], KC)
                    for k in range(KC):
                        dve.tensor_copy(wext[:, k, W0:W], psT[k][:, 0, 0:WA]).then_inc(s["wext_ready"], 1)
                link.begin(6)
                for i, first in turns(dve, NT // 2):
                    link.turn(i)
                    for u in range(2):
                        t = i * 2 + u
                        dve.wait_ge(loaded[u], i * 16 + 16)
                        link(dve.bn_stats(stats[:, u, :], xin[:, u, :]), hold=True)
                        link(dve.bn_aggr(mv[:, u, :], stats[:, u, :]))
                        dve.tensor_scalar(mv[:, u, 1:2], mv[:, u, 1:2], 1e-5, None, ALU.add).then_inc(s["var_ready"], 1)
                        dve.wait_ge(s["sd_ready"], t + 1)
                        link(dve.reciprocal(sd[:, u, :], sd[:, u, :]))
                        if not first:
                            dve.wait_ge(s["turned"], t - 1)
                            if xn_rows is not None:
                                dve.wait_ge(xn_out[u], i * 16)
                        dve.tensor_scalar(xn[:, u, :], xin[:, u, :], mv[:, u, 0:1], sd[:, u, 0:1],
                                          ALU.subtract, ALU.mult).then_inc(s["normed"], 1)
                link.close(NT // 2)

            @block.scalar
            def _(act):
                for i, first in turns(act, NT // 2):
                    for u in range(2):
                        t = i * 2 + u
                        rows = slice(t * P, (t + 1) * P) if first else bass.ds(t * P, P)
                        act.wait_ge(s["var_ready"], t + 1)
                        act.activation(sd[:, u, :], mv[:, u, 1:2], ACT.Sqrt).then_inc(s["sd_ready"], 1)
                        act.wait_ge(s["turned"], t + 1)
                        if not first:
                            act.wait_ge(xT_out[u], i * 16)
                            if W:
                                act.wait_ge(s["projected"], t - 1)
                        act.activation(xT[:, u, :, :], psT[u][:, :, :], ACT.Copy).then_inc(s["xT_ready"], 1)
                        act.wait_ge(s["xT_ready"], t + 1)
                        act.dma_start(xnT[:, :, rows], xT[:, u, :, :]).then_inc(xT_out[u], 16)
                        if W:
                            act.wait_ge(s["projected"], t + 1)
                            if not first:
                                act.wait_ge(res_out[u], i * (16 * len(outs)))
                            act.activation(res[:, u, :], psW[u][0:P, 0:W], ACT.Copy).then_inc(s["res_ready"], 1)
                            act.wait_ge(s["res_ready"], t + 1)
                            for o, col, w in outs:
                                act.dma_start(o[rows, :], res[:, u, col:col + w]).then_inc(res_out[u], 16)
                for u in range(2):
                    act.wait_ge(xT_out[u], 16 * (NT // 2))
                    if W:
                        act.wait_ge(res_out[u], 16 * (NT // 2) * len(outs))

            @block.tensor
            def _(pe):
                if weights:
                    pe.wait_ge(s["weights_in"], 16 * KC * len(weights))
                if att:
                    for k in range(KC):
                        for m in range(KC):
                            pe.transpose(psW[k][:, m * 128:(m + 1) * 128], wext[:, m, k * 128:(k + 1) * 128],
                                         c["ident"][:, :]).then_inc(s["w_turned"], 1)
                    pe.wait_ge(s["wT_copied"], KC)
                    pe.wait_ge(s["att_in"], 16 * len(att))
                    for m in range(KC):
                        for k in range(KC):
                            mm = pe.matmul(psT[m][:, 0, 0:WA], wT[:, k, m * 128:(m + 1) * 128], attm[:, k, :],
                                           start=(k == 0), stop=(k == KC - 1))
                        mm.then_inc(s["att_product"], 1)
                    pe.wait_ge(s["wext_ready"], KC)
                for i, first in turns(pe, NT // 2):
                    for u in range(2):
                        t = i * 2 + u
                        pe.wait_ge(s["normed"], t + 1)
                        if not first:
                            pe.wait_ge(s["xT_ready"], t - 1)
                        for k in range(KC):
                            mm = pe.transpose(psT[u][:, k, :], xn[:, u, k * 128:(k + 1) * 128], c["ident"][0:P, 0:P])
                        mm.then_inc(s["turned"], 1)
                        if W:
                            pe.wait_ge(s["xT_ready"], t + 1)
                            if not first:
                                pe.wait_ge(s["res_ready"], t - 1)
                            for k in range(KC):
                                mm = pe.matmul(psW[u][0:P, 0:W], xT[:, u, k, :], wext[:, k, :],
                                               start=(k == 0), stop=(k == KC - 1))
                            mm.then_inc(s["projected"], 1)


def softmax_weights(nc, c, tag, rec, src_slots, dst_slots, out):
    H = src_slots.shape[1]
    RUN = SEG * TILE
    with Room(nc, tag) as room:
        src = room.sb("src", [128, H, TPAD])
        best = room.sb("best", [128, H, RUN])
        recs = room.sb("recs", [128, RUN, 2])
        fresh = room.sb("fresh", [128, RUN + 1])
        pen_last = room.sb("pen_last", [128, RUN])
        one = room.sb("one", [128, RUN])
        two = room.sb("two", [128, RUN])
        dst = room.sb("dst", [128, RUN])
        edge = room.sb("edge", [128, 4, H])
        edgeT = room.sb("edgeT", [H, 4, 128])
        join = room.sb("join", [H, 129])
        whole = room.sb("whole", [H, 128])
        reset = room.sb("reset", [H, 128])
        carry = room.sb("carry", [H, 2, 128])
        carryT = room.sb("carryT", [128, 2, H])
        ps = [room.ps(f"ps{i}", [128, 512]) for i in range(4)]
        small = room.ps("small", [128, 512])
        names = ("loaded", "rec_in", "step", "picked", "turned", "scanned", "edges_ready", "edges_turned", "carried",
                 "carry_turned", "carry_ready", "merged", "back", "spread", "dst_in", "diff", "exps", "stored")
        s = {n: room.sem(n) for n in names}
        key = recs[:, :, 1]
        rr = src[:, :, :].rearrange("p h (q r) -> p h r q", r=SEG)
        with nc.Block() as block:

            @block.sync
            def _(sp):
                sp.dma_start(recs[:, :, :].rearrange("q s w -> q (s w)"),
                             rec.rearrange("(q s) w -> q (s w)", q=128)).then_inc(s["rec_in"], 16)
                sp.dma_start(src[:, :, :], src_slots).then_inc(s["loaded"], 16)
                for h, first in turns(sp, H):
                    if not first:
                        sp.wait_ge(s["diff"], h)
                    sp.dma_start(dst[:, :], dst_slots[:, bass.ds(h, 1) if not first else slice(0, 1), :]
                                 .rearrange("p a t -> p (a t)")).then_inc(s["dst_in"], 16)
                sp.wait_ge(s["exps"], H)
                sp.dma_start(out, src[:, :, :]).then_inc(s["stored"], 16)
                sp.wait_ge(s["stored"], 16)

            @block.scalar
            def _(act):
                act.wait_ge(s["loaded"], 16)
                for h, first in turns(act, H):
                    hs = bass.ds(h, 1) if not first else slice(0, 1)
                    if not first:
                        act.wait_ge(s["scanned"], h)
                        act.nop(nofuse=True)
                    act.activation(one[:, :], src[:, hs, :].rearrange("p a t -> p (a t)"), ACT.Copy).then_inc(s["picked"], 1)
                for h, first in turns(act, H):
                    hs = bass.ds(h, 1) if not first else slice(0, 1)
                    act.wait_ge(s["diff"], h + 1)
                    act.nop(nofuse=True)
                    act.activation(src[:, hs, :].rearrange("p a t -> p (a t)"), one[:, :], ACT.Exp).then_inc(s["exps"], 1)

            @block.tensor
            def _(pe):
                for h, first in turns(pe, H):
                    pe.wait_ge(s["picked"], h + 1)
                    view = one[:, :].rearrange("p (q r) -> p r q", r=SEG)
                    for r in range(SEG):
                        mm = pe.transpose(ps[r // 4][:, r % 4 * 128:(r % 4 + 1) * 128], view[:, r, :], c["ident"][:, :])
                    mm.then_inc(s["turned"], 1)
                pe.wait_ge(s["edges_ready"], 1)
                for n in range(4):
                    mm = pe.transpose(small[0:H, n * 128:(n + 1) * 128], edge[:, n, :], c["ident"][:, :])
                mm.then_inc(s["edges_turned"], 1)
                pe.wait_ge(s["carried"], 1)
                for n in range(2):
                    mm = pe.transpose(small[:, n * H:(n + 1) * H], carry[:, n, :], c["ident"][0:H, 0:H])
                mm.then_inc(s["carry_turned"], 1)
                for h, first in turns(pe, H):
                    pe.wait_ge(s["merged"], h + 1)
                    for r in range(SEG):
                        mm = pe.transpose(ps[r // 4][:, r % 4 * 128:(r % 4 + 1) * 128],
                                          two[:, r * 128:(r + 1) * 128], c["ident"][:, :])
                    mm.then_inc(s["back"], 1)

            @block.vector
            def _(dve):
                link = Link(dve, s["step"])
                dve.wait_ge(s["rec_in"], 16)
                link.put(dve.memset(fresh[:, 0:1], -BIG))
                link.put(dve.memset(fresh[:, RUN:RUN + 1], -BIG))
                link(dve.tensor_tensor(fresh[:, 1:RUN], key[:, 1:RUN], key[:, 0:RUN - 1], ALU.is_equal))
                link(dve.tensor_scalar(fresh[:, 1:RUN], fresh[:, 1:RUN], -1.0, BIG, ALU.add, ALU.mult))
                link.begin(7)
                for h, first in turns(dve, H):
                    link.turn(h)
                    hs = bass.ds(h, 1) if not first else slice(0, 1)
                    bh = best[:, hs, :].rearrange("p a t -> p (a t)")
                    dve.wait_ge(s["turned"], h + 1)
                    for b in range(4):
                        w = min(512, RUN - b * 512)
                        link.put(dve.tensor_copy(two[:, b * 512:b * 512 + w], ps[b][:, 0:w]))
                    link.eng.wait_ge(link.sem, link.base + link.k)
                    link.put(dve.tensor_tensor_scan(bh, fresh[:, 0:RUN], two[:, :], -BIG, ALU.add, ALU.max))
                    link(dve.tensor_tensor_scan(one[:, ::-1], fresh[:, :0:-1], two[:, ::-1], -BIG, ALU.add, ALU.max))
                    link(dve.tensor_tensor(bh, bh, one[:, :], ALU.max))
                    dve.nop().then_inc(s["scanned"], 1)
                link.close(H)
                link.put(dve.tensor_copy(edge[:, 0, :], best[:, :, RUN - 1]))
                link.put(dve.tensor_copy(edge[:, 1, :], best[:, :, 0]))
                link.put(dve.tensor_copy(edge[:, 2, :], key[:, 0:1].broadcast_to([128, H])))
                link(dve.tensor_copy(edge[:, 3, :], key[:, RUN - 1:RUN].broadcast_to([128, H])))
                dve.nop().then_inc(s["edges_ready"], 1)
                dve.wait_ge(s["edges_turned"], 1)
                link.put(dve.memset(join[:, 0:1], 0.0))
                link.put(dve.memset(join[:, 128:129], 0.0))
                link(dve.tensor_copy(edgeT[:, :, :], small[0:H, :].rearrange("h (n q) -> h n q", n=4)))
                kf, kl = edgeT[:, 2, :], edgeT[:, 3, :]
                link.put(dve.tensor_tensor(join[:, 1:128], kf[:, 1:128], kl[:, 0:127], ALU.is_equal))
                link(dve.tensor_tensor(whole[:, :], kf, kl, ALU.is_equal))
                link.put(dve.tensor_scalar(join[:, :], join[:, :], -1.0, BIG, ALU.add, ALU.mult))
                link(dve.tensor_scalar(whole[:, :], whole[:, :], -1.0, BIG, ALU.add, ALU.mult))
                for n, (lo, step) in enumerate(((0, 1), (1, -1))):
                    link(dve.tensor_tensor(reset[:, :], join[:, lo:lo + 128], whole[:, :], ALU.min))
                    link(dve.tensor_tensor_scan(carry[:, n, ::step], reset[:, ::step], edgeT[:, n, ::step], -BIG, ALU.add, ALU.max))
                link.put(dve.tensor_tensor(reset[:, 1:128], carry[:, 0, 0:127], join[:, 1:128], ALU.add))
                link(dve.tensor_tensor(whole[:, 0:127], carry[:, 1, 1:128], join[:, 1:128], ALU.add))
                link.put(dve.tensor_copy(carry[:, 0, 1:128], reset[:, 1:128]))
                link.put(dve.tensor_copy(carry[:, 1, 0:127], whole[:, 0:127]))
                link.put(dve.memset(carry[:, 0, 0:1], -BIG))
                link(dve.memset(carry[:, 1, 127:128], -BIG))
                dve.nop().then_inc(s["carried"], 1)
                dve.wait_ge(s["carry_turned"], 1)
                link(dve.tensor_copy(carryT[:, :, :], small[:, 0:2 * H].rearrange("q (n h) -> q n h", n=2)))
                link.put(dve.tensor_scalar(fresh[:, 0:RUN], key, key[:, 0:1], -1.0, ALU.is_equal, ALU.add))
                link(dve.tensor_scalar(pen_last[:, :], key, key[:, RUN - 1:RUN], -1.0, ALU.is_equal, ALU.add))
                link.put(dve.tensor_scalar(fresh[:, 0:RUN], fresh[:, 0:RUN], BIG, None, ALU.mult))
                link(dve.tensor_scalar(pen_last[:, :], pen_last[:, :], BIG, None, ALU.mult))
                link.begin(12)
                for h, first in turns(dve, H):
                    link.turn(h)
                    hs = bass.ds(h, 1) if not first else slice(0, 1)
                    bh = best[:, hs, :].rearrange("p a t -> p (a t)")
                    sh = src[:, hs, :].rearrange("p a t -> p (a t)")
                    link(dve.scalar_tensor_tensor(two[:, :], fresh[:, 0:RUN], carryT[:, 0, hs], bh, ALU.add, ALU.max))
                    link(dve.scalar_tensor_tensor(two[:, :], pen_last[:, :], carryT[:, 1, hs], two[:, :], ALU.add, ALU.max))
                    dve.nop().then_inc(s["merged"], 1)
                    dve.wait_ge(s["back"], h + 1)
                    back = two[:, :].rearrange("p (q r) -> p r q", r=SEG)
                    for b in range(4):
                        w = min(4, SEG - b * 4)
                        link.put(dve.tensor_copy(back[:, b * 4:b * 4 + w, :],
                                                 ps[b][:, 0:w * 128].rearrange("p (r q) -> p r q", r=w)))
                    dve.wait_ge(s["dst_in"], h * 16 + 16)
                    if not first:
                        dve.wait_ge(s["exps"], h)
                    link(dve.tensor_tensor(one[:, :], sh, dst[:, :], ALU.add))
                    link.put(dve.tensor_tensor(two[:, :], two[:, :], dst[:, :], ALU.add))
                    link(dve.scalar_tensor_tensor(one[:, :], one[:, :], 0.2, one[:, :], ALU.mult, ALU.max))
                    link(dve.scalar_tensor_tensor(two[:, :], two[:, :], 0.2, two[:, :], ALU.mult, ALU.max))
                    link(dve.tensor_tensor(one[:, :], one[:, :], two[:, :], ALU.subtract))
                    link(dve.tensor_scalar(one[:, :], one[:, :], 0.0, None, ALU.min))
                    dve.nop().then_inc(s["diff"], 1)
                link.close(H)


def sum_edges(nc, c, tag, idx, loc, blk_off, table, H, weights_in, key_part, finish):
    C = D // H
    W = table.shape[1]
    WT = D + H
    kind, resid, bias, out = finish
    ITER = TILES // 16
    GRP = 5
    with Room(nc, tag) as room:
        acc = room.sb("acc", [P, NT, WT])
        idx_i = room.sb("idx_i", [128, TPAD], I32)
        locs = room.sb("locs", [128, TPAD])
        off = room.sb("off", [1, TPAD], I32)
        wslot = room.sb("wslot", [128, H, TPAD])
        ids = room.sb("ids", [128, 2, BATCH], I32)
        rows = room.sb("rows", [128, 2, BATCH, WT])
        hot = room.sb("hot", [128, 2, BATCH, P])
        z = room.sb("z", [128, BATCH, H])
        valid = room.sb("valid", [128, BATCH])
        res = room.sb("res", [P, GRP, D])
        neg = room.sb("neg", [P, GRP, D]) if kind == "elu" else None
        den = room.sb("den", [P, NT, H])
        biasr = room.sb("biasr", [P, D])
        ps = [room.ps(f"ps{k}", [128, 512]) for k in range(BATCH)]
        names = ("loaded", "idx_in", "step", "staged", "weights_ready", "weighted", "summed", "added", "resid_in",
                 "finished", "stored", "lrelu", "expd")
        s = {n: room.sem(n) for n in names}
        came = room.own_sems("came")
        accf = acc[:, :, :].rearrange("p t w -> p (t w)")
        countb = bc(c["count"][:, 0:P], 1, BATCH)
        with nc.Block() as block:

            @block.sync
            def _(sp):
                sp.dma_start(idx_i[:, :], idx).then_inc(s["idx_in"], 16)
                sp.dma_start(locs[:, :], loc).then_inc(s["loaded"], 16)
                sp.dma_start(off[:, :], blk_off).then_inc(s["loaded"], 16)
                sp.dma_start(wslot[:, :, :], weights_in if weights_in is not None else key_part).then_inc(s["loaded"], 16)
                if bias is not None:
                    sp.dma_start(biasr[:, :], bias.partition_broadcast(P)).then_inc(s["loaded"], 16)
                for g in range(NT // GRP):
                    if g:
                        sp.wait_ge(s["stored"], 16 * g)
                    sp.dma_start(res[:, :, :], resid[g * GRP * P:(g + 1) * GRP * P, :].rearrange("(t p) d -> p t d", p=P)).then_inc(s["resid_in"], 16)
                    sp.wait_ge(s["finished"], g + 1)
                    sp.dma_start(out[g * GRP * P:(g + 1) * GRP * P, :].rearrange("(t p) d -> p t d", p=P), res[:, :, :]).then_inc(s["stored"], 16)
                sp.wait_ge(s["stored"], 16 * (NT // GRP))

            @block.gpsimd
            def _(pool):
                pool.wait_ge(s["idx_in"], 16)
                for i, first in turns(pool, ITER):
                    for u in range(2):
                        n = i * 2 + u
                        ii = slice(n * BATCH, (n + 1) * BATCH) if first else bass.ds(n * BATCH, BATCH)
                        if not first:
                            pool.wait_ge(s["summed"], i * 16 + (u * BATCH - BATCH))
                            pool.nop(nofuse=True)
                        pool.tensor_copy(ids[:, u, :], idx_i[:, ii]).then_inc(s["staged"], 1)
                        pool.wait_ge(s["staged"], n + 1)
                        pool.nop(nofuse=True)
                        for k in range(BATCH):
                            pool.indirect_dma_start(
                                out=rows[:, u, k, 0:W], out_offset=None, in_=table[:, :],
                                in_offset=bass.IndirectOffsetOnAxis(ap=ids[:, u, k:k + 1], axis=0)).then_inc(came[u], 16)

            @block.scalar
            def _(act):
                act.wait_ge(s["loaded"], 48 + (16 if bias is not None else 0))
                for i, first in turns(act, ITER):
                    for u in range(2):
                        n = i * 2 + u
                        if weights_in is not None:
                            if not first:
                                act.wait_ge(s["summed"], i * 16 + (u * BATCH - BATCH))
                                act.nop(nofuse=True)
                            cols = slice(n * BATCH, (n + 1) * BATCH) if first else bass.ds(n * BATCH, BATCH)
                            act.activation(rows[:, u, :, D:WT], wslot[:, :, cols].rearrange("p h k -> p k h"),
                                           ACT.Copy).then_inc(s["weights_ready"], 1)
                        else:
                            act.wait_ge(s["lrelu"], n + 1)
                            act.activation(rows[:, u, :, D:WT], z[:, :, :], ACT.Exp, scale=-1.0).then_inc(s["weights_ready"], 1)
                if kind == "elu":
                    for g in range(NT // GRP):
                        act.wait_ge(s["lrelu"], 2 * ITER + g + 1)
                        act.activation(neg[:, :, :], neg[:, :, :], ACT.Exp).then_inc(s["expd"], 1)

            @block.tensor
            def _(pe):
                for i, first in turns(pe, ITER):
                    for u in range(2):
                        n = i * 2 + u
                        pe.wait_ge(s["weighted"], n + 1)
                        for k in range(BATCH):
                            if not (first and u == 0):
                                pe.wait_ge(s["added"], n * BATCH + (k + 1 - BATCH))
                            pe.matmul(ps[k][0:P, 0:WT], hot[:, u, k, :], rows[:, u, k, :], start=True, stop=True)\
                              .then_inc(s["summed"], 1)

            @block.vector
            def _(dve):
                link = Link(dve, s["step"])
                link(dve.memset(acc[:, :, :], 0.0))
                dve.wait_ge(s["loaded"], 48 + (16 if bias is not None else 0))

                def weigh(i, first, u):
                    n = i * 2 + u
                    cols = slice(n * BATCH, (n + 1) * BATCH) if isinstance(i, int) else bass.ds(n * BATCH, BATCH)
                    if not first:
                        dve.wait_ge(s["summed"], i * 16 + (u * BATCH - BATCH))
                    link.put(dve.tensor_tensor(hot[:, u, :, :], countb, bc(locs[:, cols], 2, P), ALU.is_equal))
                    dve.wait_ge(came[u], i * (16 * BATCH) + 16 * BATCH)
                    if weights_in is None:
                        link.put(dve.tensor_scalar(valid[:, :], locs[:, cols], 0.0, None, ALU.is_ge))
                        link(dve.tensor_tensor(z[:, :, :], rows[:, u, :, D:WT], wslot[:, :, cols].rearrange("p h k -> p k h"), ALU.add))
                        link(dve.scalar_tensor_tensor(z[:, :, :], z[:, :, :], 0.2, z[:, :, :], ALU.mult, ALU.max))
                        dve.tensor_tensor(z[:, :, :], z[:, :, :], bc(valid[:, :], 2, H), ALU.mult).then_inc(s["lrelu"], 1)
                    dve.wait_ge(s["weights_ready"], n + 1)
                    for k in range(0, BATCH, 4):
                        r = rows[:, u, k:k + 4, 0:D].rearrange("p k (h c) -> p k h c", h=H)
                        for kk in range(4):
                            ins = dve.tensor_tensor(rows[:, u, k + kk, 0:D].rearrange("p (h c) -> p h c", h=H),
                                                    rows[:, u, k + kk, 0:D].rearrange("p (h c) -> p h c", h=H),
                                                    bc(rows[:, u, k + kk, D:WT], 2, C), ALU.mult)
                            if k + kk < BATCH - 1:
                                link.put(ins)
                    link.eng.wait_ge(link.sem, link.base + link.k)
                    ins.then_inc(s["weighted"], 1)

                def add(i, u):
                    n = i * 2 + u
                    if not isinstance(i, int):
                        dve.nop(nofuse=True)
                    at = slice(n * BATCH, (n + 1) * BATCH) if isinstance(i, int) else bass.ds(n * BATCH, BATCH)
                    starts = numbers(nc, mybir.EngineType.DVE, off[0:1, at], (NT - 1) * WT)
                    for k in range(BATCH):
                        a = accf[:, bass.ds(starts[k], WT)]
                        dve.wait_ge(s["summed"], n * BATCH + (k + 1))
                        dve.wait_ge(s["added"], n * BATCH + k) if not (isinstance(i, int) and n * BATCH + k == 0) else None
                        dve.tensor_tensor(a, a, ps[k][0:P, 0:WT], ALU.add).then_inc(s["added"], 1)

                per = 2 * (BATCH + (3 if weights_in is None else 0))
                link.begin(per)
                for i, first in turns(dve, ITER):
                    link.turn(i)
                    weigh(i, first, 0)
                    if not first:
                        add(i - 1, 1)
                    weigh(i, first, 1)
                    add(i, 0)
                link.close(ITER)
                add(ITER - 1, 1)
                dve.wait_ge(s["added"], TILES)
                if kind == "relu":
                    link(dve.tensor_scalar(den[:, :, :], acc[:, :, D:WT], 1e-16, None, ALU.add))
                    link(dve.reciprocal(den[:, :, :], den[:, :, :]))
                else:
                    link(dve.reciprocal(den[:, :, :], acc[:, :, D:WT]))
                for g in range(NT // GRP):
                    for t in range(g * GRP, (g + 1) * GRP):
                        v = acc[:, t, 0:D].rearrange("p (h c) -> p h c", h=H)
                        link.put(dve.tensor_tensor(v, v, bc(den[:, t, :], 2, C), ALU.mult))
                    link.eng.wait_ge(link.sem, link.base + link.k)
                    v = acc[:, g * GRP:(g + 1) * GRP, 0:D]
                    if kind == "relu":
                        link(dve.tensor_tensor(v, v, bc(biasr[:, :], 1, GRP), ALU.add))
                        dve.wait_ge(s["resid_in"], 16 * (g + 1))
                        dve.scalar_tensor_tensor(res[:, :, :], v, 0.0, res[:, :, :], ALU.max, ALU.add).then_inc(s["finished"], 1)
                    else:
                        if g:
                            dve.wait_ge(s["finished"], g)
                        dve.tensor_scalar(neg[:, :, :], v, 0.0, None, ALU.min).then_inc(s["lrelu"], 1)
                        dve.wait_ge(s["resid_in"], 16 * (g + 1))
                        link(dve.scalar_tensor_tensor(res[:, :, :], v, 0.0, res[:, :, :], ALU.max, ALU.add))
                        dve.wait_ge(s["expd"], g + 1)
                        dve.scalar_tensor_tensor(res[:, :, :], neg[:, :, :], -1.0, res[:, :, :], ALU.add, ALU.add).then_inc(s["finished"], 1)


def dyn(i, first, step, width):
    return slice(i * step, i * step + width) if first or isinstance(i, int) else bass.ds(i * step, width)


RING = 5


def mix_keys(nc, c, tag, x, xnT, W_qk, b_qk, W_v, b_v, gamma, beta, out, beside):
    with Room(nc, tag) as room:
        XT = room.sb("XT", [128, KC, N])
        wq = room.sb("wq", [128, KC, D])
        wk = room.sb("wk", [128, KC, D])
        wv = room.sb("wv", [128, KC, D])
        bcol = room.sb("bcol", [128, 4, KC])
        bv = room.sb("bv", [1, D])
        kmaxs = room.sb("kmaxs", [128, KC, NCH])
        shift = room.sb("shift", [128, KC])
        kmax = room.sb("kmax", [128, KC])
        shift_row = room.sb("shift_row", [1, KC, 128])
        xs = room.sb("xs", [128, 2, KC, P])
        ek = room.sb("ek", [P, 2, D])
        val = room.sb("val", [P, 2, D + 1])
        lam = room.sb("lam", [128, KC, D])
        den = room.sb("den", [128, KC])
        stats = room.sb("stats", [128, KC, 6])
        mv = room.sb("mv", [128, KC, 2])
        sd = room.sb("sd", [128, KC])
        qT = room.sb("qT", [128, KC, CH])
        res = room.sb("res", [P, RING, 2, D])
        psK = [room.ps(f"psK{m}", [128, 512]) for m in range(KC)]
        psKV = [room.ps(f"psKV{u}", [128, 512]) for u in range(2)]
        psV = [room.ps(f"psV{u}", [128, 512]) for u in range(2)]
        psL = [room.ps(f"psL{m}", [128, 512]) for m in range(KC)]
        names = ("loaded", "step", "keyed", "maxed", "shift_ready", "shift_turned", "shift_copied", "xs_ready", "kv_ready",
                 "exp_ready", "val_ready", "lam_ready", "summed", "sd_ready", "var_ready", "bn_ready", "q_ready", "qT_ready",
                 "o_ready", "done")
        s = {n: room.sem(n) for n in names}
        res_in, res_out = ([room.sem(f"{n}{u}") for u in range(RING)] for n in ("res_in", "res_out"))
        with nc.Block() as block:

            @block.sync
            def _(sp):
                sp.dma_start(XT[:, :, :], xnT).then_inc(s["loaded"], 16)
                for w, src in ((wq, W_qk[0]), (wk, W_qk[1]), (wv, W_v)):
                    sp.dma_start(w[:, :, :], src.rearrange("(k p) w -> p k w", p=128)).then_inc(s["loaded"], 16)
                for n, src in enumerate((b_qk[0], b_qk[1], gamma, beta)):
                    with nc.allow_non_contiguous_dma(reason="a short vector, one number per partition"):
                        sp.dma_start(bcol[:, n, :], src.rearrange("(k p) -> p k", p=128)).then_inc(s["loaded"], 16)
                sp.dma_start(bv[:, :], b_v.rearrange("(a n) -> a n", a=1)).then_inc(s["loaded"], 16)
                for i, first in turns(sp, NCH // RING):
                    for u in range(RING):
                        rows = dyn(i * RING + u, first, CH, CH)
                        if not first:
                            sp.wait_ge(res_out[u], i * 16)
                        sp.dma_start(res[:, u, :, :], x[rows, :].rearrange("(t p) d -> p t d", p=P)).then_inc(res_in[u], 16)

            @block.scalar
            def _(act):
                act.wait_ge(s["loaded"], 16 * 9)
                for i, first in turns(act, NT // 2):
                    for u in range(2):
                        t = i * 2 + u
                        if not first:
                            act.wait_ge(s["kv_ready"], t - 1)
                            act.nop(nofuse=True)
                        act.activation(xs[:, u, :, :], XT[:, :, dyn(t, first, P, P)], ACT.Copy).then_inc(s["xs_ready"], 1)
                        act.wait_ge(s["kv_ready"], t + 1)
                        if not first:
                            act.wait_ge(s["lam_ready"], t - 1)
                        act.activation(ek[:, u, :], psKV[u][0:P, 0:D], ACT.Exp).then_inc(s["exp_ready"], 1)
                act.wait_ge(s["var_ready"], 1)
                act.activation(sd[:, :], mv[:, :, 1], ACT.Sqrt).then_inc(s["sd_ready"], 1)
                for i, first in turns(act, NCH // RING):
                    for u in range(RING):
                        n = i * RING + u
                        rows = dyn(n, first, CH, CH)
                        act.wait_ge(s["q_ready"], n + 1)
                        if not (first and u == 0):
                            act.wait_ge(s["o_ready"], n)
                        for m in range(KC):
                            act.activation(qT[:, m, :], psK[m][:, 0:CH], ACT.Identity, bias=bcol[:, 0, m:m + 1])\
                               .then_inc(s["qT_ready"], 1)
                        if not (first and u == 0):
                            act.wait_ge(s["done"], n)
                            prev = n - 1
                            act.dma_start(out[dyn(prev, first, CH, CH), :].rearrange("(t p) d -> p t d", p=P),
                                          res[:, (u - 1) % RING, :, :]).then_inc(res_out[(u - 1) % RING], 16)
                act.wait_ge(s["done"], NCH)
                act.dma_start(out[N - CH:N, :].rearrange("(t p) d -> p t d", p=P), res[:, RING - 1, :, :]).then_inc(res_out[RING - 1], 16)
                for u in range(RING):
                    act.wait_ge(res_out[u], 16 * (NCH // RING))

            @block.tensor
            def _(pe):
                pe.wait_ge(s["loaded"], 16 * 9)
                for i, first in turns(pe, NCH):
                    if not first:
                        pe.wait_ge(s["maxed"], i * KC)
                    for m in range(KC):
                        for k in range(KC):
                            mm = pe.matmul(psK[m][:, 0:CH], wk[:, k, m * 128:(m + 1) * 128], XT[:, k, dyn(i, first, CH, CH)],
                                           start=(k == 0), stop=(k == KC - 1))
                        mm.then_inc(s["keyed"], 1)
                pe.wait_ge(s["shift_ready"], 1)
                for m in range(KC):
                    pe.transpose(psKV[0][0:1, m * 128:(m + 1) * 128], shift[:, m:m + 1], c["ident"][:, :])\
                      .then_inc(s["shift_turned"], 1)
                pe.wait_ge(s["shift_copied"], 1)
                for i, first in turns(pe, NT // 2):
                    for u in range(2):
                        t = i * 2 + u
                        pe.wait_ge(s["xs_ready"], t + 1)
                        if not first:
                            pe.wait_ge(s["exp_ready"], t - 1)
                            pe.wait_ge(s["val_ready"], t - 1)
                        for w, o, b in ((wk, psKV[u], shift_row[:, :, :].rearrange("a k n -> a (k n)")), (wv, psV[u], bv[:, :])):
                            pe.matmul(o[0:P, 0:D], c["ones"][0:1, 0:P], b, start=True, stop=False)
                            for k in range(KC):
                                mm = pe.matmul(o[0:P, 0:D], xs[:, u, k, :], w[:, k, :], start=False, stop=(k == KC - 1))
                        mm.then_inc(s["kv_ready"], 1)
                        pe.wait_ge(s["exp_ready"], t + 1)
                        pe.wait_ge(s["val_ready"], t + 1)
                        for m in range(KC):
                            mm = pe.matmul(psL[m][:, 0:D + 1], ek[:, u, m * 128:(m + 1) * 128], val[:, u, :],
                                           start=(first and u == 0), stop=False, skip_group_check=True)
                        mm.then_inc(s["lam_ready"], 1)
                for m in range(KC):
                    mm = pe.matmul(psL[m][:, 0:D + 1], c["zero"][0:1, :], val[0:1, 0, :], start=False, stop=True, skip_group_check=True)
                mm.then_inc(s["summed"], 1)
                pe.wait_ge(s["bn_ready"], 1)
                for i, first in turns(pe, NCH // RING):
                    for u in range(RING):
                        n = i * RING + u
                        if not (first and u == 0):
                            pe.wait_ge(s["qT_ready"], n * KC)
                        for m in range(KC):
                            for k in range(KC):
                                mm = pe.matmul(psK[m][:, 0:CH], wq[:, k, m * 128:(m + 1) * 128], XT[:, k, dyn(n, first, CH, CH)],
                                               start=(k == 0), stop=(k == KC - 1))
                        mm.then_inc(s["q_ready"], 1)
                        pe.wait_ge(s["qT_ready"], n * KC + KC)
                        if not (first and u == 0):
                            pe.wait_ge(s["done"], n)
                        for j in range(2):
                            for m in range(KC):
                                mm = pe.matmul(psKV[0][0:P, j * D:(j + 1) * D], qT[:, m, j * P:(j + 1) * P], lam[:, m, :],
                                               start=(m == 0), stop=(m == KC - 1))
                        mm.then_inc(s["o_ready"], 1)

            @block.gpsimd
            def _(pool):
                beside(pool)

            @block.vector
            def _(dve):
                link = Link(dve, s["step"])
                link(dve.memset(val[:, :, D:D + 1], 1.0))
                for i, first in turns(dve, NCH):
                    for m in range(KC):
                        dve.wait_ge(s["keyed"], i * KC + (m + 1))
                        dve.nop(nofuse=True)
                        dve.tensor_reduce(kmaxs[:, m, dyn(i, first, 1, 1)], psK[m][:, 0:CH], AX, ALU.max).then_inc(s["maxed"], 1)
                dve.wait_ge(s["maxed"], NCH * KC)
                link(dve.tensor_reduce(kmax[:, :], kmaxs[:, :, :], AX, ALU.max))
                dve.wait_ge(s["loaded"], 16 * 9)
                link(dve.tensor_tensor(kmax[:, :], kmax[:, :], bcol[:, 1, :], ALU.add))
                link(dve.tensor_tensor(shift[:, :], bcol[:, 1, :], kmax[:, :], ALU.subtract))
                dve.nop().then_inc(s["shift_ready"], 1)
                dve.wait_ge(s["shift_turned"], KC)
                dve.tensor_copy(shift_row[:, :, :].rearrange("a k n -> a (k n)"), psKV[0][0:1, 0:KC * 128]).then_inc(s["shift_copied"], 1)
                for i, first in turns(dve, NT // 2):
                    for u in range(2):
                        t = i * 2 + u
                        dve.wait_ge(s["kv_ready"], t + 1)
                        if not first:
                            dve.wait_ge(s["lam_ready"], t - 1)
                        dve.tensor_copy(val[:, u, 0:D], psV[u][0:P, 0:D]).then_inc(s["val_ready"], 1)
                dve.wait_ge(s["summed"], 1)
                for m in range(KC):
                    link(dve.reciprocal(den[:, m:m + 1], psL[m][:, D:D + 1]))
                    link(dve.tensor_scalar(lam[:, m, :], psL[m][:, 0:D], den[:, m:m + 1], None, ALU.mult))
                    link(dve.bn_stats(stats[:, m, :], lam[:, m, :]))
                    link(dve.bn_aggr(mv[:, m, :], stats[:, m, :]))
                link(dve.tensor_scalar(mv[:, :, 1], mv[:, :, 1], 1e-5, None, ALU.add))
                dve.nop().then_inc(s["var_ready"], 1)
                dve.wait_ge(s["sd_ready"], 1)
                link(dve.reciprocal(sd[:, :], sd[:, :]))
                for m in range(KC):
                    link(dve.tensor_scalar(lam[:, m, :], lam[:, m, :], mv[:, m, 0:1], sd[:, m:m + 1], ALU.subtract, ALU.mult))
                    link(dve.tensor_scalar(lam[:, m, :], lam[:, m, :], bcol[:, 2, m:m + 1], bcol[:, 3, m:m + 1], ALU.mult, ALU.add))
                dve.nop().then_inc(s["bn_ready"], 1)
                for i, first in turns(dve, NCH // RING):
                    for u in range(RING):
                        n = i * RING + u
                        dve.wait_ge(res_in[u], i * 16 + 16)
                        dve.wait_ge(s["o_ready"], n + 1)
                        r = res[:, u, :, :].rearrange("p t d -> p (t d)")
                        dve.tensor_tensor(r, r, psKV[0][0:P, :], ALU.add).then_inc(s["done"], 1)


def experts(nc, c, tag, x, xnT, logits, w1, w2, w3, out, beside):
    X, HID = w1.shape[0], w1.shape[1]
    HC = -(-HID // 128)
    PAIRS = HC // 2
    GRP = NT // 5
    part = [min(128, HID - j * 128) for j in range(HC)]
    with Room(nc, tag) as room:
        XT = room.sb("XT", [128, KC, N])
        Y = room.sb("Y", [P, NT, D])
        raw1 = room.sb("raw1", [128, HC, D])
        raw3 = room.sb("raw3", [128, HC, D])
        raw2 = room.sb("raw2", [128, KC, HID])
        w1T = room.sb("w1T", [128, KC, HC * 128])
        w3T = room.sb("w3T", [128, KC, HC * 128])
        w2T = room.sb("w2T", [128, HC, D])
        sil = room.sb("sil", [128, PAIRS, 2, CH])
        hT = room.sb("hT", [128, PAIRS, 2, CH])
        gate = room.sb("gate", [P, X, NT])
        g1 = room.sb("g1", [P, NT])
        g2 = room.sb("g2", [P, NT])
        mask = room.sb("mask", [P, X, NT])
        cand = room.sb("cand", [P, X, NT])
        both = room.sb("both", [P, X, NT])
        gcol = room.sb("gcol", [P, NT])
        lraw = room.sb("lraw", [P, NT, X])
        res = room.sb("res", [P, GRP, D])
        psH = [[room.ps(f"psH{n}{q}", [128, 512]) for q in range(PAIRS)] for n in range(2)]
        psY = room.ps("psY", [128, 512])
        psT = room.ps("psT", [128, 512])
        names = ("loaded", "raw_in", "step", "shifted", "exped", "turned", "copied", "gate_set", "hid", "silued", "mulled",
                 "y_ready", "added", "res_in", "done", "stored")
        s = {n: room.sem(n) for n in names}
        turnjobs = []
        for raw, wT in ((raw1, w1T), (raw3, w3T)):
            for k in range(KC):
                for j in range(HC):
                    turnjobs.append((raw[0:part[j], j, k * 128:(k + 1) * 128], part[j], wT[:, k, j * 128:j * 128 + part[j]], 128))
        for j in range(HC):
            for k in range(KC):
                turnjobs.append((raw2[:, k, j * 128:j * 128 + part[j]], 128, w2T[0:part[j], j, k * 128:(k + 1) * 128], part[j]))
        NTJ = len(turnjobs)
        with nc.Block() as block:

            @block.sync
            def _(sp):
                sp.dma_start(XT[:, :, :], xnT).then_inc(s["loaded"], 16)
                sp.dma_start(lraw[:, :, :], logits.rearrange("(t p) e -> p t e", p=P)).then_inc(s["loaded"], 16)
                full = HID // 128
                for e, first in turns(sp, X):
                    if not first:
                        sp.wait_ge(s["turned"], e * NTJ)
                    es = dyn(e, first, 1, 1)
                    for raw, w in ((raw1, w1), (raw3, w3)):
                        we = w[es, :, :].rearrange("e h c -> (e h) c")
                        sp.dma_start(raw[:, 0:full, :], we[0:full * 128, :].rearrange("(j p) c -> p j c", p=128)).then_inc(s["raw_in"], 16)
                        sp.dma_start(raw[0:part[-1], full, :], we[full * 128:HID, :]).then_inc(s["raw_in"], 16)
                    sp.dma_start(raw2[:, :, :], w2[es, :, :].rearrange("e (k p) h -> p (e k) h", p=128)).then_inc(s["raw_in"], 16)
                tiles_of = lambda ap, g: ap[g * GRP * P:(g + 1) * GRP * P, :].rearrange("(t p) d -> p t d", p=P)
                for g in range(NT // GRP):
                    if g:
                        sp.wait_ge(s["done"], g)
                    sp.dma_start(res[:, :, :], tiles_of(x, g)).then_inc(s["res_in"], 16)
                    if g:
                        sp.dma_start(tiles_of(out, g - 1), Y[:, (g - 1) * GRP:g * GRP, :]).then_inc(s["stored"], 16)
                sp.wait_ge(s["done"], NT // GRP)
                sp.dma_start(tiles_of(out, NT // GRP - 1), Y[:, NT - GRP:NT, :]).then_inc(s["stored"], 16)
                sp.wait_ge(s["stored"], 16 * (NT // GRP))

            @block.scalar
            def _(act):
                act.wait_ge(s["shifted"], 1)
                act.activation(gate[:, :, :], gate[:, :, :], ACT.Exp).then_inc(s["exped"], 1)
                with act.Fori(0, X) as e:
                    for i, first in turns(act, NCH):
                        n = e * NCH + i
                        for q in range(PAIRS):
                            act.wait_ge(s["hid"], n * PAIRS + (q + 1))
                            if part[2 * q + 1] == 128:
                                act.activation(sil[:, q, :, :].rearrange("p j n -> p (j n)"), psH[0][q][:, 0:2 * CH], ACT.Silu)\
                                   .then_inc(s["silued"], 1)
                            else:
                                w = part[2 * q + 1]
                                act.activation(sil[0:w, q, 1, :], psH[0][q][0:w, CH:2 * CH], ACT.Silu)
                                act.activation(sil[:, q, 0, :], psH[0][q][:, 0:CH], ACT.Silu).then_inc(s["silued"], 1)

            @block.tensor
            def _(pe):
                pe.wait_ge(s["loaded"], 32)
                with pe.Fori(0, X) as e:
                    pe.wait_ge(s["raw_in"], e * 80 + 80)
                    for n, (src, rows, dst, w) in enumerate(turnjobs):
                        if n % 4 == 0:
                            pe.wait_ge(s["copied"], e * NTJ + (n + 1))
                        pe.transpose(psT[0:w, n % 4 * 128:n % 4 * 128 + rows], src, c["ident"][0:rows, 0:rows]).then_inc(s["turned"], 1)
                    pe.wait_ge(s["copied"], e * NTJ + (NTJ + 1))
                    for i, first in turns(pe, NCH):
                        n = e * NCH + i
                        cols = dyn(i, first, CH, CH)

                        def hidden(q):
                            pe.wait_ge(s["mulled"], n * PAIRS + (q + 1))
                            for a, wT in enumerate((w1T, w3T)):
                                for j in (2 * q, 2 * q + 1):
                                    for k in range(KC):
                                        mm = pe.matmul(psH[a][q][0:part[j], (j % 2) * CH:(j % 2 + 1) * CH],
                                                       wT[:, k, j * 128:j * 128 + part[j]], XT[:, k, cols],
                                                       start=(k == 0), stop=(k == KC - 1))
                            mm.then_inc(s["hid"], 1)

                        def down(q):
                            pe.wait_ge(s["mulled"], n * PAIRS + (PAIRS + q + 1))
                            if q == 0:
                                pe.wait_ge(s["added"], n * 2 + 2)
                            for t in range(2):
                                for j in (2 * q, 2 * q + 1):
                                    mm = pe.matmul(psY[0:P, t * D:(t + 1) * D], hT[0:part[j], q, j % 2, t * P:(t + 1) * P],
                                                   w2T[0:part[j], j, :], start=(j == 0 and t == 0), stop=(j == HC - 1), skip_group_check=True)
                            if q == PAIRS - 1:
                                mm.then_inc(s["y_ready"], 1)

                        hidden(0)
                        for q in range(1, PAIRS):
                            hidden(q)
                            down(q - 1)
                        down(PAIRS - 1)

            @block.gpsimd
            def _(pool):
                beside(pool)

            @block.vector
            def _(dve):
                link = Link(dve, s["step"])
                link(dve.memset(Y[:, :, :], 0.0))
                dve.wait_ge(s["loaded"], 32)
                link(dve.tensor_copy(gate[:, :, :], lraw[:, :, :].rearrange("p t e -> p e t")))
                by_tile = lambda ap: ap[:, :, :].rearrange("p e t -> p t e")
                row = lambda ap: bc(ap[:, :], 1, X)
                link(dve.tensor_reduce(g1[:, :], by_tile(gate), AX, ALU.max))
                link(dve.tensor_tensor(gate[:, :, :], gate[:, :, :], row(g1), ALU.subtract))
                dve.nop().then_inc(s["shifted"], 1)
                dve.wait_ge(s["exped"], 1)
                link(dve.tensor_reduce(g1[:, :], by_tile(gate), AX, ALU.add))
                link(dve.reciprocal(g1[:, :], g1[:, :]))
                link(dve.tensor_tensor(gate[:, :, :], gate[:, :, :], row(g1), ALU.mult))
                link(dve.memset(both[:, :, :], 0.0))
                for _ in range(2):
                    link(dve.scalar_tensor_tensor(cand[:, :, :], both[:, :, :], -2.0, gate[:, :, :], ALU.mult, ALU.add))
                    link(dve.tensor_reduce(g2[:, :], by_tile(cand), AX, ALU.max))
                    link(dve.tensor_tensor(mask[:, :, :], cand[:, :, :], row(g2), ALU.is_equal))
                    number = c["count"][0:P, 0:X].unsqueeze(2).broadcast_to([P, X, NT])
                    link(dve.scalar_tensor_tensor(cand[:, :, :], mask[:, :, :], -float(X), number, ALU.mult, ALU.add))
                    link(dve.tensor_reduce(g2[:, :], by_tile(cand), AX, ALU.min))
                    link(dve.tensor_tensor(mask[:, :, :], cand[:, :, :], row(g2), ALU.is_equal))
                    link(dve.tensor_tensor(both[:, :, :], both[:, :, :], mask[:, :, :], ALU.add))
                link(dve.tensor_tensor(gate[:, :, :], gate[:, :, :], both[:, :, :], ALU.mult))
                link(dve.tensor_reduce(g1[:, :], by_tile(gate), AX, ALU.add))
                link(dve.tensor_scalar(g1[:, :], g1[:, :], 1e-9, None, ALU.add))
                link(dve.reciprocal(g1[:, :], g1[:, :]))
                link(dve.tensor_tensor(gate[:, :, :], gate[:, :, :], row(g1), ALU.mult))
                dve.nop().then_inc(s["copied"], 1)
                dve.nop().then_inc(s["mulled"], PAIRS)
                dve.nop().then_inc(s["added"], 2)
                with dve.Fori(0, X) as e:
                    if True:
                        dve.wait_ge(s["added"], e * (2 * NCH) + 2)
                        dve.nop(nofuse=True)
                        dve.tensor_copy(gcol[:, :], gate[:, bass.ds(e, 1), :].rearrange("p a t -> p (a t)")).then_inc(s["gate_set"], 1)
                    for n, (src, rows, dst, w) in enumerate(turnjobs):
                        if n % 4 == 0:
                            dve.wait_ge(s["turned"], e * NTJ + min(n + 4, NTJ))
                        dve.tensor_copy(dst, psT[0:w, n % 4 * 128:n % 4 * 128 + rows]).then_inc(s["copied"], 1)
                    dve.wait_ge(s["gate_set"], e + 1)
                    for i, first in turns(dve, NCH):
                        n = e * NCH + i
                        for q in range(PAIRS):
                            dve.wait_ge(s["silued"], n * PAIRS + (q + 1))
                            if part[2 * q + 1] == 128:
                                dve.tensor_tensor(hT[:, q, :, :].rearrange("p j n -> p (j n)"),
                                                  sil[:, q, :, :].rearrange("p j n -> p (j n)"), psH[1][q][:, 0:2 * CH],
                                                  ALU.mult).then_inc(s["mulled"], 1)
                            else:
                                w = part[2 * q + 1]
                                dve.tensor_tensor(hT[0:w, q, 1, :], sil[0:w, q, 1, :], psH[1][q][0:w, CH:2 * CH], ALU.mult)
                                dve.tensor_tensor(hT[:, q, 0, :], sil[:, q, 0, :], psH[1][q][:, 0:CH], ALU.mult).then_inc(s["mulled"], 1)
                        dve.wait_ge(s["y_ready"], n + 1)
                        dve.nop(nofuse=True)
                        for t in range(2):
                            tt = dyn(i * 2 + t, first, 1, 1)
                            y = Y[:, tt, :].rearrange("p a d -> p (a d)")
                            dve.scalar_tensor_tensor(y, psY[0:P, t * D:(t + 1) * D], gcol[:, tt], y, ALU.mult, ALU.add).then_inc(s["added"], 1)
                dve.wait_ge(s["added"], X * NCH * 2 + 2)
                for g in range(NT // GRP):
                    y = Y[:, g * GRP:(g + 1) * GRP, :]
                    dve.wait_ge(s["res_in"], g * 16 + 16)
                    dve.tensor_tensor(y, y, res[:, :, :], ALU.add).then_inc(s["done"], 1)


def mix_heads(nc, c, tag, x, xn_rows, xnT, w_qkv, b_qkv, k_g, k_b, v_g, v_b, w1, b1, w2, b2, out):
    HCOLS = k_g.shape[0]
    H = D // HCOLS
    HB = H // KC
    with Room(nc, tag) as room:
        XT = room.sb("XT", [128, KC, N])
        wkv = room.sb("wkv", [128, KC, 2, H, HCOLS])
        wq = room.sb("wq", [128, KC, H, HCOLS])
        w1s = room.sb("w1s", [128, KC, D])
        w2s = room.sb("w2s", [128, KC, D])
        bkv = room.sb("bkv", [1, 2, H, HCOLS])
        bq = room.sb("bq", [128, KC])
        b1c = room.sb("b1c", [128, KC])
        b2r = room.sb("b2r", [1, D])
        gain = room.sb("gain", [P, 2, 2, HCOLS])
        xs = room.sb("xs", [128, 2, KC, P])
        cen = room.sb("cen", [P, 2, 2 * H, HCOLS])
        sq = room.sb("sq", [P, 2 * H, HCOLS])
        mean = room.sb("mean", [P, 2 * H])
        var = room.sb("var", [P, 2 * H])
        kv = room.sb("kv", [128, KC, 128])
        qT = room.sb("qT", [128, KC, CH])
        retT = room.sb("retT", [128, KC, CH])
        hT = room.sb("hT", [128, KC, CH])
        res = room.sb("res", [P, RING, 2, D])
        xnr = room.sb("xnr", [P, RING, 2, D])
        ps = [room.ps(f"ps{n}", [128, 512]) for n in range(8)]
        psR, psKV = ps[0:2], ps[2:4]
        psQ, psH, psY = ps[4:6], ps[6:8], ps[0]
        names = ("loaded", "step", "xs_ready", "kv_ready", "centred", "var_ready", "sd_ready", "normed", "kv_added", "kv_done",
                 "kv_set", "q_ready", "qT_ready", "ret_ready", "retT_ready", "h_ready", "hT_ready", "y_ready", "done")
        s = {n: room.sem(n) for n in names}
        res_in, res_out = ([room.sem(f"{n}{u}") for u in range(RING)] for n in ("res_in", "res_out"))
        LOADS = 1 + KC * 3 + 3 + 2 + 2 + 4 + 1
        with nc.Block() as block:

            @block.sync
            def _(sp):
                def load(dst, src):
                    with nc.allow_non_contiguous_dma(reason="short vectors as columns"):
                        sp.dma_start(dst, src).then_inc(s["loaded"], 16)
                load(XT[:, :, :], xnT)
                parts = w_qkv.rearrange("(k p) (h s c) -> k s p h c", p=128, h=H, s=3)
                bparts = b_qkv.rearrange("(h s c) -> s h c", h=H, s=3)
                for k in range(KC):
                    load(wq[:, k, :, :], parts[k, 0])
                    for n in range(2):
                        load(wkv[:, k, n, :, :], parts[k, 1 + n])
                load(w1s[:, :, :], w1.rearrange("(k p) w -> p k w", p=128))
                load(w2s[:, :, :], w2.rearrange("(k p) w -> p k w", p=128))
                load(b1c[:, :], b1.rearrange("(k p) -> p k", p=128))
                for n in range(2):
                    load(bkv[:, n, :, :], bparts[1 + n].unsqueeze(0))
                    for h in range(HB):
                        sp.dma_start(bq[h * HCOLS:(h + 1) * HCOLS, n:n + 1],
                                     bparts[0, n * HB + h].rearrange("(c a) -> c a", a=1)).then_inc(s["loaded"], 16)
                for n, v in enumerate((k_g, v_g, k_b, v_b)):
                    load(gain[:, n // 2, n % 2, :], v.partition_broadcast(P))
                load(b2r[:, :], b2.rearrange("(a n) -> a n", a=1))
                for i, first in turns(sp, NCH // RING):
                    for u in range(RING):
                        rows = dyn(i * RING + u, first, CH, CH)
                        if not first:
                            sp.wait_ge(res_out[u], i * 16)
                        for dst, src in ((res, x), (xnr, xn_rows)):
                            sp.dma_start(dst[:, u, :, :], src[rows, :].rearrange("(t p) d -> p t d", p=P)).then_inc(res_in[u], 16)

            ALL = 16 * (1 + 3 * KC + 2 + 1 + 2 + 2 * HB + 4 + 1)

            @block.scalar
            def _(act):
                act.wait_ge(s["loaded"], ALL)
                for i, first in turns(act, NT // 2):
                    for u in range(2):
                        t = i * 2 + u
                        if not first:
                            act.wait_ge(s["kv_ready"], t - 1)
                            act.nop(nofuse=True)
                        act.activation(xs[:, u, :, :], XT[:, :, dyn(t, first, P, P)], ACT.Copy).then_inc(s["xs_ready"], 1)
                        act.wait_ge(s["var_ready"], t + 1)
                        act.activation(var[:, :], var[:, :], ACT.Sqrt).then_inc(s["sd_ready"], 1)
                for i, first in turns(act, NCH // RING):
                    for u in range(RING):
                        n = i * RING + u
                        begun = not (first and u == 0)
                        act.wait_ge(s["q_ready"], n + 1)
                        if begun:
                            act.wait_ge(s["ret_ready"], n)
                        for m in range(KC):
                            act.activation(qT[:, m, :], psQ[m][:, 0:CH], ACT.Identity, bias=bq[:, m:m + 1]).then_inc(s["qT_ready"], 1)
                        act.wait_ge(s["h_ready"], n + 1)
                        if begun:
                            act.wait_ge(s["y_ready"], n)
                        for m in range(KC):
                            act.activation(hT[:, m, :], psH[m][:, 0:CH], ACT.Gelu, bias=b1c[:, m:m + 1]).then_inc(s["hT_ready"], 1)
                        act.wait_ge(s["done"], n + 1)
                        act.dma_start(out[dyn(n, first, CH, CH), :].rearrange("(t p) d -> p t d", p=P), res[:, u, :, :]).then_inc(res_out[u], 16)
                for u in range(RING):
                    act.wait_ge(res_out[u], 16 * (NCH // RING))

            @block.tensor
            def _(pe):
                pe.wait_ge(s["loaded"], ALL)
                for i, first in turns(pe, NT // 2):
                    for u in range(2):
                        t = i * 2 + u
                        pe.wait_ge(s["xs_ready"], t + 1)
                        if not first:
                            pe.wait_ge(s["centred"], t - 1)
                        pe.matmul(psR[u][0:P, :], c["ones"][0:1, 0:P], bkv[:, :, :, :].rearrange("a n h c -> a (n h c)"), start=True, stop=False)
                        for k in range(KC):
                            mm = pe.matmul(psR[u][0:P, :], xs[:, u, k, :], wkv[:, k, :, :, :].rearrange("p n h c -> p (n h c)"),
                                           start=False, stop=(k == KC - 1))
                        mm.then_inc(s["kv_ready"], 1)
                        pe.wait_ge(s["normed"], t + 1)
                        flat = cen[:, u, :, :].rearrange("p g c -> p (g c)")
                        for m in range(KC):
                            mm = pe.matmul(psKV[m][:, 0:128], flat[:, m * 128:(m + 1) * 128], flat[:, D + m * 128:D + (m + 1) * 128],
                                           start=(first and u == 0), stop=False, skip_group_check=True)
                        mm.then_inc(s["kv_added"], 1)
                for m in range(KC):
                    mm = pe.matmul(psKV[m][:, 0:128], c["zero"][0:1, :], c["zero"][0:1, :], start=False, stop=True, skip_group_check=True)
                mm.then_inc(s["kv_done"], 1)
                pe.wait_ge(s["kv_set"], 1)
                for i, first in turns(pe, NCH // RING):
                    for u in range(RING):
                        n = i * RING + u
                        begun = not (first and u == 0)
                        for m in range(KC):
                            for k in range(KC):
                                mm = pe.matmul(psQ[m][:, 0:CH], wq[:, k, m * HB:(m + 1) * HB, :].rearrange("p h c -> p (h c)"),
                                               XT[:, k, dyn(n, first, CH, CH)], start=(k == 0), stop=(k == KC - 1))
                        mm.then_inc(s["q_ready"], 1)
                        pe.wait_ge(s["qT_ready"], n * KC + KC)
                        for m in range(KC):
                            mm = pe.matmul(psKV[m][:, 0:CH], kv[:, m, :], qT[:, m, :], start=True, stop=True)
                        mm.then_inc(s["ret_ready"], 1)
                        pe.wait_ge(s["retT_ready"], n * KC + KC)
                        for m in range(KC):
                            for k in range(KC):
                                mm = pe.matmul(psH[m][:, 0:CH], w1s[:, k, m * 128:(m + 1) * 128], retT[:, k, :], start=(k == 0), stop=(k == KC - 1))
                        mm.then_inc(s["h_ready"], 1)
                        pe.wait_ge(s["hT_ready"], n * KC + KC)
                        if begun:
                            pe.wait_ge(s["done"], n)
                        for j in range(2):
                            pe.matmul(psY[0:P, j * D:(j + 1) * D], c["ones"][0:1, 0:P], b2r[:, :], start=True, stop=False)
                            for k in range(KC):
                                mm = pe.matmul(psY[0:P, j * D:(j + 1) * D], hT[:, k, j * P:(j + 1) * P], w2s[:, k, :], start=False, stop=(k == KC - 1))
                        mm.then_inc(s["y_ready"], 1)

            @block.vector
            def _(dve):
                link = Link(dve, s["step"])
                dve.wait_ge(s["loaded"], ALL)
                link.begin(2 * 9)
                for i, first in turns(dve, NT // 2):
                    link.turn(i)
                    for u in range(2):
                        t = i * 2 + u
                        raw = psR[u][0:P, :].rearrange("p (g c) -> p g c", c=HCOLS)
                        cu = cen[:, u, :, :]
                        dve.wait_ge(s["kv_ready"], t + 1)
                        link(dve.tensor_reduce(mean[:, :], raw, AX, ALU.add))
                        link(dve.tensor_scalar(mean[:, :], mean[:, :], 1.0 / HCOLS, None, ALU.mult))
                        if not first:
                            dve.wait_ge(s["kv_added"], t - 1)
                        dve.tensor_tensor(cu, raw, bc(mean[:, :], 2, HCOLS), ALU.subtract).then_inc(s["centred"], 1)
                        dve.wait_ge(s["centred"], t + 1)
                        link(dve.tensor_tensor(sq[:, :, :], cu, cu, ALU.mult))
                        link(dve.tensor_reduce(mean[:, :], sq[:, :, :], AX, ALU.add))
                        link(dve.tensor_scalar(var[:, :], mean[:, :], 1.0 / HCOLS, 1e-5, ALU.mult, ALU.add))
                        dve.nop().then_inc(s["var_ready"], 1)
                        dve.wait_ge(s["sd_ready"], t + 1)
                        link(dve.reciprocal(mean[:, :], var[:, :]))
                        link(dve.tensor_tensor(cu, cu, bc(mean[:, :], 2, HCOLS), ALU.mult))
                        by_kv = cu.rearrange("p (n h) c -> p n h c", n=2)
                        link.put(dve.tensor_tensor(by_kv[:, 0], by_kv[:, 0], bc(gain[:, 0, 0, :], 1, H), ALU.mult))
                        link(dve.tensor_tensor(by_kv[:, 1], by_kv[:, 1], bc(gain[:, 0, 1, :], 1, H), ALU.mult))
                        dve.tensor_tensor(by_kv[:, 0], by_kv[:, 0], bc(gain[:, 1, 0, :], 1, H), ALU.add)
                        dve.tensor_tensor(by_kv[:, 1], by_kv[:, 1], bc(gain[:, 1, 1, :], 1, H), ALU.add).then_inc(s["normed"], 1)
                link.close(NT // 2)
                link(dve.memset(kv[:, :, :], 0.0))
                dve.wait_ge(s["kv_done"], 1)
                for m in range(KC):
                    for h in range(HB):
                        b = slice(h * HCOLS, (h + 1) * HCOLS)
                        ins = dve.tensor_scalar(kv[b, m, b], psKV[m][b, b], 1.0 / N, None, ALU.mult)
                        link(ins)
                dve.nop().then_inc(s["kv_set"], 1)
                for i, first in turns(dve, NCH // RING):
                    for u in range(RING):
                        n = i * RING + u
                        dve.wait_ge(s["ret_ready"], n + 1)
                        for m in range(KC):
                            dve.tensor_tensor(retT[:, m, :], psKV[m][:, 0:CH], XT[:, m, dyn(n, first, CH, CH)], ALU.add).then_inc(s["retT_ready"], 1)
                        dve.wait_ge(res_in[u], i * 32 + 32)
                        dve.tensor_tensor(res[:, u, :, :], res[:, u, :, :], xnr[:, u, :, :], ALU.add).then_inc(s["step"], 1)
                        dve.wait_ge(s["y_ready"], n + 1)
                        dve.wait_ge(s["step"], n + (link.base + link.k + 1))
                        r = res[:, u, :, :].rearrange("p t d -> p (t d)")
                        dve.tensor_tensor(r, r, psY[0:P, :], ALU.add).then_inc(s["done"], 1)


def slice_attention(nc, c, tag, x, xnT, W_fx, b_fx, W_x, b_x, W_slice, b_slice, W_q, W_k, W_v, W_out, b_out, temperature,
                    wT_dram, out):
    G = W_slice.shape[1]
    HD = W_slice.shape[0]
    INNER = W_fx.shape[1]
    H = INNER // HD
    M = INNER // 128
    with Room(nc, tag) as room:
        XT = room.sb("XT", [128, KC, N])
        wfx = room.sb("wfx", [128, KC, INNER])
        wx = room.sb("wx", [128, KC, INNER])
        wsl = room.sb("wsl", [128, 128])
        small_w = room.sb("small_w", [HD, 3, HD])
        wout = room.sb("wout", [HD, H, D])
        bfx = room.sb("bfx", [1, INNER])
        bout = room.sb("bout", [1, D])
        bsl = room.sb("bsl", [1, H, G])
        bslr = room.sb("bslr", [1, G])
        bxc = room.sb("bxc", [128, M])
        temp = room.sb("temp", [P, H])
        xs = room.sb("xs", [128, 2, KC, P])
        xm = room.sb("xm", [128, 2, M, P])
        fx = room.sb("fx", [P, 2, INNER])
        w = room.sb("w", [P, 2, H, G])
        mx = room.sb("mx", [P, H])
        wT = room.sb("wT", [128, 2, M, P])
        norm = room.sb("norm", [128, M])
        tok = room.sb("tok", [128, M, HD])
        tokT = room.sb("tokT", [HD, M * 128])
        qk = room.sb("qk", [HD, 2, M * 128])
        at = room.sb("at", [G, H, G])
        am = room.sb("am", [G, H])
        atT = room.sb("atT", [G, H * G])
        val = room.sb("val", [G, H, HD])
        osT = room.sb("osT", [HD, H, G])
        mixm = room.sb("mixm", [128, M, D])
        low = room.sb("low", [G, M, D])
        res = room.sb("res", [P, RING, D])
        wTin = room.sb("wTin", [128, RING, M, P])
        ps = [room.ps(f"ps{n}", [128, 512]) for n in range(8)]
        psX, psL, psF, psT, psTok, psNorm = ps[0:6]
        names = ("loaded", "step", "wsl_zero", "xs_ready", "x_ready", "xm_ready", "l_ready", "shifted", "exped", "w_ready", "f_ready",
                 "fx_ready", "tok_added", "turned", "wT_ready", "tok_done", "stage", "stage_done", "o_ready", "done", "sl_in",
                 "att_shifted", "att_exped")
        s = {n: room.sem(n) for n in names}
        wT_out = [room.sem(f"wT_out{u}") for u in range(2)]
        res_in, res_out = ([room.sem(f"{n}{u}") for u in range(RING)] for n in ("res_in", "res_out"))
        ALL = 16 * 13
        with nc.Block() as block:

            @block.sync
            def _(sp):
                def load(dst, src):
                    with nc.allow_non_contiguous_dma(reason="short vectors as columns"):
                        sp.dma_start(dst, src).then_inc(s["loaded"], 16)
                load(XT[:, :, :], xnT)
                load(wfx[:, :, :], W_fx.rearrange("(k p) w -> p k w", p=128))
                load(wx[:, :, :], W_x.rearrange("(k p) w -> p k w", p=128))
                for n, v in enumerate((W_q, W_k, W_v)):
                    load(small_w[:, n, :], v)
                load(wout[:, :, :], W_out.rearrange("(h c) d -> c h d", c=HD))
                load(bfx[:, :], b_fx.rearrange("(a n) -> a n", a=1))
                load(bout[:, :], b_out.rearrange("(a n) -> a n", a=1))
                load(bslr[:, :], b_slice.rearrange("(a n) -> a n", a=1))
                load(bxc[:, :], b_x.rearrange("(m p) -> p m", p=128))
                load(temp[:, :], temperature.rearrange("a h b d -> (a h b d)").partition_broadcast(P))
                sp.wait_ge(s["wsl_zero"], 1)
                sp.dma_start(wsl[0:HD, 0:G], W_slice).then_inc(s["sl_in"], 16)
                sp.dma_start(wsl[HD:128, G:128], W_slice).then_inc(s["sl_in"], 16)
                for u in range(2):
                    sp.wait_ge(wT_out[u], 16 * (NT // 2))
                for i, first in turns(sp, NT // RING):
                    for u in range(RING):
                        t = i * RING + u
                        if not first:
                            sp.wait_ge(res_out[u], i * 16)
                        sp.dma_start(res[:, u, :], x[dyn(t, first, P, P), :]).then_inc(res_in[u], 16)
                        sp.dma_start(wTin[:, u, :, :].rearrange("p m n -> p (m n)"),
                                     wT_dram[dyn(t, first, 1, 1), :, :].rearrange("t p n -> p (t n)")).then_inc(res_in[u], 16)

            LOADED = 16 * 12

            @block.gpsimd
            def _(pool):
                pool.memset(wsl[:, :], 0.0).then_inc(s["wsl_zero"], 1)

            @block.scalar
            def _(act):
                act.wait_ge(s["loaded"], LOADED)
                for i, first in turns(act, NT // 2):
                    for u in range(2):
                        t = i * 2 + u
                        if not first:
                            act.wait_ge(s["f_ready"], t - 1)
                            act.nop(nofuse=True)
                        act.activation(xs[:, u, :, :], XT[:, :, dyn(t, first, P, P)], ACT.Copy).then_inc(s["xs_ready"], 1)
                        act.wait_ge(s["x_ready"], t + 1)
                        if not first:
                            act.wait_ge(s["l_ready"], t - 1)
                        for m in range(M):
                            act.activation(xm[:, u, m, :], psX[:, m * P:(m + 1) * P], ACT.Identity, bias=bxc[:, m:m + 1])\
                               .then_inc(s["xm_ready"], 1)
                        act.wait_ge(s["f_ready"], t + 1)
                        if not first:
                            act.wait_ge(s["tok_added"], t - 1)
                        act.activation(fx[:, u, :], psF[0:P, :], ACT.Copy).then_inc(s["fx_ready"], 1)
                        act.wait_ge(s["shifted"], t + 1)
                        act.activation(w[:, u, :, :], w[:, u, :, :], ACT.Exp).then_inc(s["exped"], 1)
                        act.wait_ge(s["turned"], t + 1)
                        if not first:
                            act.wait_ge(wT_out[u], i * 16)
                        act.activation(wT[:, u, :, :].rearrange("p m n -> p (m n)"), psT[:, 0:M * P], ACT.Copy).then_inc(s["wT_ready"], 1)
                        act.wait_ge(s["wT_ready"], t + 1)
                        act.dma_start(wT_dram[dyn(t, first, 1, 1), :, :].rearrange("t p n -> p (t n)"),
                                      wT[:, u, :, :].rearrange("p m n -> p (m n)")).then_inc(wT_out[u], 16)
                act.wait_ge(s["att_shifted"], 1)
                act.activation(at[:, :, :], at[:, :, :], ACT.Exp, scale=float(HD) ** -0.5).then_inc(s["att_exped"], 1)
                for i, first in turns(act, NT // RING):
                    for u in range(RING):
                        t = i * RING + u
                        act.wait_ge(s["done"], t + 1)
                        act.dma_start(out[dyn(t, first, P, P), :], res[:, u, :]).then_inc(res_out[u], 16)
                for u in range(RING):
                    act.wait_ge(res_out[u], 16 * (NT // RING))

            @block.tensor
            def _(pe):
                pe.wait_ge(s["loaded"], LOADED)
                pe.wait_ge(s["sl_in"], 32)
                pe.wait_ge(s["stage_done"], 1)
                for i, first in turns(pe, NT // 2):
                    for u in range(2):
                        t = i * 2 + u
                        begun = not (first and u == 0)
                        if begun:
                            pe.wait_ge(s["xm_ready"], t * M)
                        for m in range(M):
                            for k in range(KC):
                                mm = pe.matmul(psX[:, m * P:(m + 1) * P], wx[:, k, m * 128:(m + 1) * 128], XT[:, k, dyn(t, first, P, P)],
                                               start=(k == 0), stop=(k == KC - 1))
                        mm.then_inc(s["x_ready"], 1)
                        pe.wait_ge(s["xs_ready"], t + 1)
                        if begun:
                            pe.wait_ge(s["fx_ready"], t)
                        pe.matmul(psF[0:P, :], c["ones"][0:1, 0:P], bfx[:, :], start=True, stop=False)
                        for k in range(KC):
                            mm = pe.matmul(psF[0:P, :], xs[:, u, k, :], wfx[:, k, :], start=False, stop=(k == KC - 1))
                        mm.then_inc(s["f_ready"], 1)
                        pe.wait_ge(s["xm_ready"], t * M + M)
                        if begun:
                            pe.wait_ge(s["shifted"], t)
                        for m in range(M):
                            cols = slice(m * 128, (m + 1) * 128)
                            pe.matmul(psL[0:P, cols], c["ones"][0:1, 0:P], bsl[:, :, :].rearrange("a h g -> a (h g)")[:, cols], start=True, stop=False)
                            mm = pe.matmul(psL[0:P, cols], xm[:, u, m, :], wsl[:, :], start=False, stop=True)
                        mm.then_inc(s["l_ready"], 1)
                        pe.wait_ge(s["w_ready"], t + 1)
                        pe.wait_ge(s["fx_ready"], t + 1)
                        flat = w[:, u, :, :].rearrange("p h g -> p (h g)")
                        for m in range(M):
                            cols = slice(m * 128, (m + 1) * 128)
                            opens = not begun and m == 0
                            pe.matmul(psTok[:, cols], flat[:, cols], fx[:, u, cols], start=opens, stop=False, skip_group_check=True)
                            mm = pe.matmul(psNorm[:, m:m + 1], flat[:, cols], c["ones"][0:P, 0:1], start=opens, stop=False, skip_group_check=True)
                        mm.then_inc(s["tok_added"], 1)
                        if begun:
                            pe.wait_ge(s["wT_ready"], t)
                        for m in range(M):
                            mm = pe.transpose(psT[:, m * P:(m + 1) * P], flat[:, m * 128:(m + 1) * 128], c["ident"][0:P, 0:P])
                        mm.then_inc(s["turned"], 1)
                pe.matmul(psTok[:, :], c["zero"][0:1, :], bc(c["zero"][0:1, :], 1, 4), start=False, stop=True, skip_group_check=True)
                pe.matmul(psNorm[:, 0:M], c["zero"][0:1, :], c["zero"][0:1, 0:M], start=False, stop=True, skip_group_check=True).then_inc(s["tok_done"], 1)
                pe.wait_ge(s["wT_ready"], NT)
                pe.wait_ge(s["stage_done"], 2)
                for m in range(M):
                    mm = pe.transpose(psX[0:HD, m * 128:(m + 1) * 128], tok[:, m, :], c["ident"][:, :])
                mm.then_inc(s["stage"], 1)
                pe.wait_ge(s["stage_done"], 3)
                for n in range(2):
                    mm = pe.matmul(ps[1 + n][0:HD, :], small_w[:, n, :], tokT[:, :], start=True, stop=True)
                for h in range(H):
                    mm = pe.matmul(psT[0:G, h * HD:(h + 1) * HD], tokT[:, h * G:(h + 1) * G], small_w[:, 2, :], start=True, stop=True)
                mm.then_inc(s["stage"], 1)
                pe.wait_ge(s["stage_done"], 4)
                for h in range(H):
                    mm = pe.matmul(psX[0:G, h * G:(h + 1) * G], qk[:, 0, h * G:(h + 1) * G], qk[:, 1, h * G:(h + 1) * G], start=True, stop=True)
                mm.then_inc(s["stage"], 1)
                pe.wait_ge(s["stage_done"], 5)
                for h in range(H):
                    mm = pe.transpose(psL[0:G, h * G:(h + 1) * G], at[:, h, :], c["ident"][0:G, 0:G])
                mm.then_inc(s["stage"], 1)
                pe.wait_ge(s["stage_done"], 6)
                for h in range(H):
                    mm = pe.matmul(psF[0:HD, h * G:(h + 1) * G], val[:, h, :], atT[:, h * G:(h + 1) * G], start=True, stop=True)
                mm.then_inc(s["stage"], 1)
                pe.wait_ge(s["stage_done"], 7)
                for h in range(H):
                    mm = pe.matmul(ps[4 + h % 2 * 2 + h // 4][0:G, h // 2 % 2 * D:(h // 2 % 2 + 1) * D], osT[:, h, :], wout[:, h, :], start=True, stop=True)
                mm.then_inc(s["stage"], 1)
                pe.wait_ge(s["stage_done"], 8)
                for i, first in turns(pe, NT // RING):
                    for u in range(RING):
                        t = i * RING + u
                        pe.wait_ge(res_in[u], i * 32 + 32)
                        if not first:
                            pe.wait_ge(s["done"], t - (RING - 1))
                        o = ps[u]
                        pe.matmul(o[0:P, 0:D], c["ones"][0:1, 0:P], bout[:, :], start=True, stop=False)
                        for m in range(M):
                            mm = pe.matmul(o[0:P, 0:D], wTin[:, u, m, :], mixm[:, m, :], start=False, stop=(m == M - 1))
                        mm.then_inc(s["o_ready"], 1)

            @block.vector
            def _(dve):
                link = Link(dve, s["step"])
                dve.wait_ge(s["loaded"], LOADED)
                link.put(dve.tensor_copy(bsl[:, :, :], bc(bslr[:, :], 1, H)))
                link(dve.tensor_scalar(temp[:, :], temp[:, :], 0.1, 5.0, ALU.max, ALU.min))
                link(dve.reciprocal(temp[:, :], temp[:, :]))
                dve.nop().then_inc(s["stage_done"], 1)
                link.begin(2 * 4)
                for i, first in turns(dve, NT // 2):
                    link.turn(i)
                    for u in range(2):
                        t = i * 2 + u
                        wu = w[:, u, :, :]
                        dve.wait_ge(s["l_ready"], t + 1)
                        if not first:
                            dve.wait_ge(s["turned"], t - 1)
                        link(dve.tensor_tensor(wu, psL[0:P, :].rearrange("p (h g) -> p h g", g=G), bc(temp[:, :], 2, G), ALU.mult))
                        link(dve.tensor_reduce(mx[:, :], wu, AX, ALU.max))
                        dve.tensor_tensor(wu, wu, bc(mx[:, :], 2, G), ALU.subtract).then_inc(s["shifted"], 1)
                        dve.wait_ge(s["exped"], t + 1)
                        link(dve.tensor_reduce(mx[:, :], wu, AX, ALU.add))
                        link(dve.reciprocal(mx[:, :], mx[:, :]))
                        dve.tensor_tensor(wu, wu, bc(mx[:, :], 2, G), ALU.mult).then_inc(s["w_ready"], 1)
                link.close(NT // 2)
                dve.wait_ge(s["tok_done"], 1)
                link(dve.tensor_scalar(norm[:, :], psNorm[:, 0:M], 1e-5, None, ALU.add))
                link(dve.reciprocal(norm[:, :], norm[:, :]))
                for m in range(M):
                    for a in range(2):
                        r = slice(a * G, (a + 1) * G)
                        link(dve.tensor_scalar(tok[r, m, :], psTok[r, m * 128 + a * HD:m * 128 + (a + 1) * HD], norm[r, m:m + 1], None, ALU.mult))
                dve.nop().then_inc(s["stage_done"], 1)
                dve.wait_ge(s["stage"], 1)
                link(dve.tensor_copy(tokT[:, :], psX[0:HD, :]))
                dve.nop().then_inc(s["stage_done"], 1)
                dve.wait_ge(s["stage"], 2)
                for n in range(2):
                    link(dve.tensor_copy(qk[:, n, :], ps[1 + n][0:HD, :]))
                link(dve.tensor_copy(val[:, :, :], psT[0:G, :].rearrange("k (h c) -> k h c", h=H)))
                dve.nop().then_inc(s["stage_done"], 1)
                dve.wait_ge(s["stage"], 3)
                lg = psX[0:G, :].rearrange("g (h k) -> g h k", h=H)
                link(dve.tensor_reduce(am[:, :], lg, AX, ALU.max))
                link(dve.tensor_tensor(at[:, :, :], lg, bc(am[:, :], 2, G), ALU.subtract))
                dve.nop().then_inc(s["att_shifted"], 1)
                dve.wait_ge(s["att_exped"], 1)
                link(dve.tensor_reduce(am[:, :], at[:, :, :], AX, ALU.add))
                link(dve.reciprocal(am[:, :], am[:, :]))
                link(dve.tensor_tensor(at[:, :, :], at[:, :, :], bc(am[:, :], 2, G), ALU.mult))
                dve.nop().then_inc(s["stage_done"], 1)
                dve.wait_ge(s["stage"], 4)
                link(dve.tensor_copy(atT[:, :], psL[0:G, :]))
                dve.nop().then_inc(s["stage_done"], 1)
                dve.wait_ge(s["stage"], 5)
                link(dve.tensor_copy(osT[:, :, :], psF[0:HD, :].rearrange("c (h g) -> c h g", h=H)))
                dve.nop().then_inc(s["stage_done"], 1)
                dve.wait_ge(s["stage"], 6)
                for a in range(2):
                    for b in range(2):
                        v = ps[4 + a * 2 + b][0:G, :].rearrange("g (m d) -> g m d", m=2)
                        link(dve.tensor_copy(mixm[a * G:(a + 1) * G, 2 * b:2 * b + 2, :], v))
                dve.nop().then_inc(s["stage_done"], 1)
                for i, first in turns(dve, NT // RING):
                    for u in range(RING):
                        t = i * RING + u
                        dve.wait_ge(s["o_ready"], t + 1)
                        dve.wait_ge(res_in[u], i * 32 + 32)
                        dve.tensor_tensor(res[:, u, :], res[:, u, :], ps[u][0:P, 0:D], ALU.add).then_inc(s["done"], 1)


SHARES = (TURNS * 2 // 10, TURNS * 5 // 10)


def program(nc, a, out):
    def dram(name, shape, dt=F32):
        return nc.dram_tensor(name, shape, dt, kind="Internal").ap()

    with Room(nc, "const") as fixed:
        c = constants(nc, fixed)
        H, HC = a["L0_gnn_att_src"].shape
        X = a["L0_ffn_router_w"].shape[0]
        HW = a["L1_gnn_W1"].shape[1]
        xnT = [dram(f"xnT{k}", (128, KC, N)) for k in range(4)]
        xn_rows, mixed0, x1, x2, mixed1, x3, table0 = (
            dram(n, (N, D)) for n in ("xn_rows", "mixed0", "x1", "x2", "mixed1", "x3", "table0"))
        src_part0, dst_part0, logits = dram("src_part0", (N, H)), dram("dst_part0", (N, H)), dram("logits", (N, X))
        src_slots, dst_slots, weights0 = (dram(n, (128, H, TPAD)) for n in ("src_slots", "dst_slots", "weights0"))
        table1, key_part1, key_slots = dram("table1", (N, D + 2)), dram("key_part1", (N, 2)), dram("key_slots", (128, 2, TPAD))
        rec = [dram(f"rec{g}", (TPAD * TILE, 2)) for g in range(2)]
        tile_end = [dram(f"tile_end{g}", (1, NT)) for g in range(2)]
        idx = [dram(f"idx{g}", (128, TPAD), I32) for g in range(2)]
        flat_loc = [dram(f"flat_loc{g}", (TPAD * TILE,)) for g in range(2)]
        blk = [dram(f"blk{g}", (1, TPAD), I32) for g in range(2)]
        loc = [dram(f"loc{g}", (128, TPAD)) for g in range(2)]
        blk_off = [dram(f"blk_off{g}", (1, TPAD), I32) for g in range(2)]

        att = [(a[f"L0_gnn_att_{end}"][h, :], h * HC, n * H + h) for n, end in enumerate(("src", "dst")) for h in range(H)]
        with Room(nc, "by_source") as room1:
            with Room(nc, "by_target") as room0:
                send1, send0 = Sender(nc, room1, rec[1]), Sender(nc, room0, rec[0])
                place_edges(nc, c, "sort0", a["dst"], a["src"], send0, tile_end[0])
                project_rows(nc, c, "ln0", a["x"], xnT[0], None, [(a["L0_gnn_W"], 0)], att,
                             [(table0, 0, D), (src_part0, D, H), (dst_part0, D + H, H)],
                             lambda pool: send0.send(pool, 0, SHARES[0]))
                mix_keys(nc, c, "mix0", a["x"], xnT[0], *(a[f"L0_mix_{n}"] for n in (
                    "W_qk", "b_qk", "W_v", "b_v", "gamma", "beta")), mixed0, lambda pool: send0.send(pool, SHARES[0], SHARES[1]))
                place_edges(nc, c, "sort1", a["src"], a["dst"], send1, tile_end[1],
                            lambda pool: send0.send(pool, SHARES[1], TURNS))
            lay_slots(nc, c, "slots0", rec[0], tile_end[0], idx[0], loc[0], flat_loc[0], blk[0], blk_off[0], D + H)
            spread_parts(nc, c, "spread0", flat_loc[0], blk[0], dst_part0, dst_slots, (idx[0], src_part0, src_slots))
            softmax_weights(nc, c, "soft", rec[0], src_slots, dst_slots, weights0)
            sum_edges(nc, c, "edges0", idx[0], loc[0], blk_off[0], table0, H, weights0, None,
                      ("relu", mixed0, a["L0_gnn_bias"], x1))
            project_rows(nc, c, "ln1", x1, xnT[1], None, [(a["L0_ffn_router_w"].rearrange("e c -> c e"), 0)], [], [(logits, 0, X)])
            experts(nc, c, "moe", x1, xnT[1], logits, a["L0_ffn_w1"], a["L0_ffn_w2"], a["L0_ffn_w3"], x2,
                    lambda pool: send1.send(pool, 0, TURNS))
        lay_slots(nc, c, "slots1", rec[1], tile_end[1], idx[1], loc[1], flat_loc[1], blk[1], blk_off[1], D + 2)

        halves = [(a[f"L1_gnn_a{n + 1}"][0, end * HW:(end + 1) * HW], n * HW, col) for n in range(2) for end, col in ((1, n), (0, 2 + n))]
        project_rows(nc, c, "ln2", x2, xnT[2], xn_rows, [(a["L1_gnn_W1"], 0), (a["L1_gnn_W2"], HW)], halves,
                     [(table1, 0, D + 2), (key_part1, D + 2, 2)])
        mix_heads(nc, c, "mix1", x2, xn_rows, xnT[2], *(a[f"L1_mix_{n}"] for n in (
            "w_qkv", "b_qkv", "kln_g", "kln_b", "vln_g", "vln_b", "w1", "b1", "w2", "b2")), mixed1)
        spread_parts(nc, c, "spread1", flat_loc[1], blk[1], key_part1, key_slots)
        sum_edges(nc, c, "edges1", idx[1], loc[1], blk_off[1], table1, 2, None, key_slots, ("elu", mixed1, None, x3))
        project_rows(nc, c, "ln3", x3, xnT[3], None, [], [], [])
        slice_attention(nc, c, "slice", x3, xnT[3], *(a[f"L1_ffn_{n}"] for n in (
            "W_fx", "b_fx", "W_x", "b_x", "W_slice", "b_slice", "W_q", "W_k", "W_v", "W_out", "b_out", "temperature")),
            dram("slices", (NT, 128, KC * 2 * P)), out)


def kernel(**inputs):
    import numpy as _np
    import concourse.bacc as _bacc
    from concourse import mybir as _mybir
    from concourse.bass_utils import run_bass_kernel_spmd as _run

    nc = _bacc.Bacc("TRN2", target_bir_lowering=False, num_devices=1)
    arrays, args = {}, {}
    for name in inputs:
        v = _np.ascontiguousarray(inputs[name])
        arrays[f"in_{name}"] = v
        args[name] = nc.dram_tensor(f"in_{name}", v.shape, _mybir.dt.from_np(v.dtype), kind="ExternalInput").ap()
    out = nc.dram_tensor("out_dram", (N, D), F32, kind="ExternalOutput").ap()
    program(nc, args, out)
    r = _run(nc, [arrays], core_ids=[0])
    return r.results[0]["out_dram"]
```

```python
from contextlib import ExitStack

import concourse.bass as bass
from concourse import mybir

F32 = mybir.dt.float32
I32 = mybir.dt.int32
ALU = mybir.AluOpType
ACT = mybir.ActivationFunctionType
AX = mybir.AxisListType.X

N = 6250
D = 256
E = 200000
P = 125
NT = N // P
KC = D // 128
EJ = E // P
TILE = 128
TILES = -(-(E // TILE + NT) // 32) * 32
SEG = -(-TILES // 128)
TPAD = SEG * 128
BATCH = 8
CH = 2 * P
NCH = N // CH
BIG = 1e30
SEND = 32
TURNS = EJ // SEND


class Link:

    def __init__(self, eng, sem, start=0):
        self.eng, self.sem, self.base, self.k = eng, sem, start, 0

    def begin(self, per):
        self.start, self.per, self.k = self.base + self.k, per, 0

    def turn(self, i):
        assert self.k in (0, self.per), (self.k, self.per)
        self.base, self.k = i * self.per + self.start, 0

    def close(self, turns):
        assert self.k == self.per, (self.k, self.per)
        self.base, self.k = self.start + turns * self.per, 0

    def put(self, ins):
        self.k += 1
        return ins.then_inc(self.sem, 1)

    def sync(self, hold=False):
        self.eng.wait_ge(self.sem, self.base + self.k)
        if hold:
            self.eng.nop(nofuse=True)

    def __call__(self, ins, hold=False):
        self.put(ins)
        self.sync(hold)


def turns(eng, n):
    yield 0, True
    with eng.Fori(1, n) as i:
        yield i, False


def bc(ap, axis, n):
    a = ap.unsqueeze(axis)
    shape = list(a.shape)
    shape[axis] = n
    return a.broadcast_to(shape)


def numbers(nc, engine, ap, top):
    _, values = nc.values_load_multi_w_load_instructions(
        ap, engines=[engine], min_val=0, max_val=top,
        skip_runtime_bounds_check_because="they are counts of blocks, below NT by their making")
    return values


class Room:

    def __init__(self, nc, tag):
        self.nc, self.tag, self.stack, self.sems = nc, tag, ExitStack(), []

    def __enter__(self):
        self.stack.__enter__()
        return self

    def __exit__(self, *a):
        if a[0] is None:
            with self.nc.Block() as block:

                @block.sync
                def _(sp):
                    for sem in self.sems:
                        sp.sem_clear(sem)
        return self.stack.__exit__(*a)

    def sb(self, name, shape, dt=F32):
        return self.stack.enter_context(self.nc.sbuf_tensor(f"{self.tag}_{name}", shape, dt))

    def ps(self, name, shape, dt=F32):
        return self.stack.enter_context(self.nc.psum_tensor(f"{self.tag}_{name}", shape, dt))

    def own_sems(self, name, n=2):
        return [self.nc.alloc_semaphore(name=f"{self.tag}_{name}{u}") for u in range(n)]

    def sem(self, name):
        self.sems.append(self.stack.enter_context(self.nc.semaphore(f"{self.tag}_{name}")))
        return self.sems[-1]


def constants(nc, room):
    c = {
        "ident": room.sb("ident", [128, 128]),
        "ones": room.sb("ones", [128, 128]),
        "before": room.sb("before", [P, P]),
        "count": room.sb("count", [128, 128]),
        "zero": room.sb("zero", [128, 128]),
        "own": room.sb("own", [128, 1]),
    }
    count_i = room.sb("count_i", [128, 128], I32)
    own_i = room.sb("own_i", [128, 1], I32)
    filled, made = room.sem("filled"), room.sem("made")
    with nc.Block() as block:

        @block.gpsimd
        def _(pool):
            pool.memset(c["ident"][:, :], 0.0).then_inc(filled, 1)
            pool.memset(c["ones"][:, :], 1.0).then_inc(filled, 1)
            pool.memset(c["before"][:, :], 1.0).then_inc(filled, 1)
            pool.memset(c["zero"][:, :], 0.0).then_inc(filled, 1)
            pool.iota(count_i[:, :], pattern=[[1, 128]], base=0, channel_multiplier=0).then_inc(filled, 1)
            pool.iota(own_i[:, :], pattern=[[0, 1]], base=0, channel_multiplier=1).then_inc(filled, 1)
            pool.wait_ge(filled, 6)
            pool.affine_select(out=c["ident"][:, :], in_=c["ident"][:, :], compare_op=ALU.not_equal, fill=1.0,
                               base=0, pattern=[[-1, 128]], channel_multiplier=1).then_inc(made, 1)
            pool.affine_select(out=c["before"][:, :], in_=c["before"][:, :], compare_op=ALU.is_gt, fill=0.0,
                               base=0, pattern=[[1, P]], channel_multiplier=-1).then_inc(made, 1)

        @block.vector
        def _(dve):
            dve.wait_ge(filled, 6)
            dve.tensor_copy(c["count"][:, :], count_i[:, :]).then_inc(made, 1)
            dve.tensor_copy(c["own"][:, :], own_i[:, :]).then_inc(made, 1)
    return c


class Sender:

    def __init__(self, nc, room, rec):
        self.nc, self.rec = nc, rec
        self.rec3 = room.sb("rec3", [P, EJ, 3], I32)
        self.stage = room.sb("stage", [P, SEND, 3], I32)
        self.staged, self.sent = room.own_sems("staged", 1)[0], room.own_sems("sent")

    def send(self, pool, lo, hi):
        with pool.Fori(lo, hi) as i:
            pool.tensor_copy(self.stage[:, :, :], self.rec3[:, bass.ds(i * SEND, SEND), :]).then_inc(self.staged, 1)
            pool.wait_ge(self.staged, i + 1)
            pool.nop(nofuse=True)
            for k in range(SEND):
                pool.indirect_dma_start(
                    out=self.rec[:, :], out_offset=bass.IndirectOffsetOnAxis(ap=self.stage[:, k, 0:1], axis=0),
                    in_=self.stage[:, k, 1:3], in_offset=None).then_inc(self.sent[k // (SEND // 2)], 16)
            for h in range(2):
                pool.wait_ge(self.sent[h], i * (8 * SEND) + 8 * SEND)
            pool.nop(nofuse=True)


def block_of(dve, link, key, blk, blk_i, hit):
    link(dve.tensor_scalar(blk[:, :], key[:, :], 0.5, 1.0 / P, ALU.add, ALU.mult))
    link(dve.tensor_copy(blk_i[:, :], blk[:, :]))
    link(dve.tensor_copy(blk[:, :], blk_i[:, :]))
    link(dve.scalar_tensor_tensor(hit[:, :], blk[:, :], float(P), key[:, :], ALU.mult, ALU.is_gt))
    link(dve.tensor_tensor(blk[:, :], blk[:, :], hit[:, :], ALU.subtract))


def order_edges(nc, c, tag, src, dst, pairs):
    with Room(nc, tag) as room:
        sender = Sender(nc, room, pairs)
        rec3 = sender.rec3
        ends_i = room.sb("ends_i", [P, 2, EJ], I32)
        both = room.sb("both", [P, EJ, 2], I32)
        next_i = room.sb("next_i", [P, 1], I32)
        nextf = room.sb("nextf", [P, 1])
        keyf = room.sb("keyf", [P, EJ])
        blk = room.sb("blk", [P, EJ])
        blk_i = room.sb("blk_i", [P, EJ], I32)
        hit = room.sb("hit", [P, EJ])
        upto = room.sb("upto", [P, EJ])
        pos = room.sb("pos", [P, EJ])
        zeros = room.sb("zeros", [P, EJ])
        falls = room.sb("falls", [P, 2])
        flag = room.sb("flag", [1, 2], I32)
        cnt = room.sb("cnt", [P, P])
        upper = room.sb("upper", [P, P])
        base = room.sb("base", [P, P])
        fallen = room.ps("fallen", [128, 2])
        tot = room.ps("tot", [128, P])
        pre = room.ps("pre", [128, P])
        loaded, step, counted, summed, paired, stored, flagged, placed, tabled = (room.sem(s) for s in (
            "loaded", "step", "counted", "summed", "paired", "stored", "flagged", "placed", "tabled"))
        flat = dst.rearrange("(p j) -> p j", p=P)
        with nc.Block() as block:

            @block.sync
            def _(sp):
                sp.dma_start(ends_i[:, 0, :], src.rearrange("(p j) -> p j", p=P)).then_inc(loaded, 16)
                sp.dma_start(ends_i[:, 1, :], flat).then_inc(loaded, 16)
                with nc.allow_non_contiguous_dma(reason="the first key of each partition"):
                    sp.dma_start(next_i[0:P - 1, :], flat[1:P, 0:1]).then_inc(loaded, 16)
                sp.wait_ge(paired, 1)
                sp.dma_start(pairs.rearrange("(p j) w -> p j w", p=P), both[:, :, :]).then_inc(stored, 16)
                sp.wait_ge(stored, 16)

            @block.vector
            def _(dve):
                link = Link(dve, step)
                link.put(dve.memset(falls[:, :], 0.0))
                dve.wait_ge(loaded, 48)
                link.put(dve.tensor_copy(both[:, :, 0], ends_i[:, 0, :]))
                link.put(dve.tensor_copy(both[:, :, 1], ends_i[:, 1, :]))
                link.put(dve.tensor_copy(nextf[0:P - 1, :], next_i[0:P - 1, :]))
                link(dve.tensor_copy(keyf[:, :], ends_i[:, 1, :]))
                dve.nop().then_inc(paired, 1)
                link(dve.tensor_tensor(hit[:, 0:EJ - 1], keyf[:, 0:EJ - 1], keyf[:, 1:EJ], ALU.is_gt))
                link(dve.tensor_reduce(falls[:, 0:1], hit[:, 0:EJ - 1], AX, ALU.max))
                link(dve.tensor_tensor(falls[0:P - 1, 1:2], keyf[0:P - 1, EJ - 1:EJ], nextf[0:P - 1, :], ALU.is_gt))
                dve.nop().then_inc(counted, 1)
                dve.wait_ge(summed, 1)
                link(dve.tensor_scalar(falls[0:1, :], fallen[0:1, :], 1.0, None, ALU.min))
                link(dve.tensor_tensor(falls[0:1, 0:1], falls[0:1, 0:1], falls[0:1, 1:2], ALU.max))
                link(dve.tensor_copy(flag[0:1, :], falls[0:1, 0:1].broadcast_to([1, 2])))

            @block.tensor
            def _(pe):
                pe.wait_ge(counted, 1)
                pe.matmul(fallen[:, :], c["ones"][0:P, :], falls[:, :], start=True, stop=True).then_inc(summed, 1)

        with nc.Block() as block:

            @block.vector
            def _(dve):
                unsorted = dve.value_load(flag[0:1, 0:1], min_val=0, max_val=1)
                with dve.If(unsorted > 0):
                    link = Link(dve, placed)
                    link.put(dve.memset(zeros[:, :], 0.0))
                    link.put(dve.memset(pos[:, :], 0.0))
                    link.put(dve.tensor_copy(rec3[:, :, 1], both[:, :, 0]))
                    link.put(dve.tensor_copy(rec3[:, :, 2], both[:, :, 1]))
                    block_of(dve, link, keyf, blk, blk_i, hit)
                    link(dve.scalar_tensor_tensor(blk[:, :], blk[:, :], -float(P), keyf[:, :], ALU.mult, ALU.add))
                    link.begin(1)
                    with dve.Fori(0, P) as b:
                        link.turn(b)
                        link(dve.tensor_scalar(hit[:, :], blk[:, :], c["count"][0:P, bass.ds(b, 1)], 0.0,
                                               ALU.is_equal, ALU.add, accum_out=cnt[:, bass.ds(b, 1)]))
                    link.close(P)
                    dve.nop().then_inc(counted, 1)
                    dve.wait_ge(summed, 3)
                    link(dve.tensor_tensor_scan(upper[:, :], tot[0:P, :], c["zero"][0:P, 0:P], -1.0, ALU.add, ALU.add))
                    link(dve.tensor_tensor(base[:, :], upper[:, :], tot[0:P, :], ALU.subtract))
                    link(dve.tensor_tensor(base[:, :], base[:, :], pre[0:P, :], ALU.add))
                    link.begin(4)
                    with dve.Fori(0, P) as b:
                        link.turn(b)
                        link(dve.tensor_scalar(hit[:, :], blk[:, :], c["count"][0:P, bass.ds(b, 1)], None, ALU.is_equal))
                        link(dve.tensor_tensor_scan(upto[:, :], hit[:, :], zeros[:, :], base[:, bass.ds(b, 1)],
                                                    ALU.add, ALU.add))
                        link(dve.scalar_tensor_tensor(upto[:, :], blk[:, :], c["count"][0:P, bass.ds(b, 1)], upto[:, :],
                                                      ALU.is_equal, ALU.mult))
                        link(dve.tensor_tensor(pos[:, :], pos[:, :], upto[:, :], ALU.add))
                    link.close(P)
                    link(dve.tensor_copy(rec3[:, :, 0], pos[:, :]))
                    dve.nop().then_inc(tabled, 1)
                dve.nop()

            @block.tensor
            def _(pe):
                unsorted = pe.value_load(flag[0:1, 0:1], min_val=0, max_val=1)
                with pe.If(unsorted > 0):
                    pe.wait_ge(counted, 2)
                    pe.matmul(tot[:, :], c["ones"][0:P, :], cnt[:, :], start=True, stop=True).then_inc(summed, 1)
                    pe.matmul(pre[0:P, :], c["before"][:, :], cnt[:, :], start=True, stop=True).then_inc(summed, 1)
                pe.nop()

            @block.gpsimd
            def _(pool):
                unsorted = pool.value_load(flag[0:1, 0:1], min_val=0, max_val=1)
                with pool.If(unsorted > 0):
                    pool.wait_ge(tabled, 1)
                    sender.send(pool, 0, TURNS)
                pool.nop()


def place_edges(nc, c, tag, pairs, end, sender, tile_end, beside=None):
    rec, rec3 = sender.rec, sender.rec3
    with Room(nc, tag) as room:
        both = room.sb("both", [P, EJ, 2], I32)
        keyf = room.sb("keyf", [P, EJ])
        blk = room.sb("blk", [P, EJ])
        blk_i = room.sb("blk_i", [P, EJ], I32)
        hit = room.sb("hit", [P, EJ])
        upto = room.sb("upto", [P, EJ])
        pos = room.sb("pos", [P, EJ])
        zeros = room.sb("zeros", [P, EJ])
        cnt = room.sb("cnt", [P, NT])
        tot_i = room.sb("tot_i", [128, NT], I32)
        tiles = room.sb("tiles", [128, NT])
        ends = room.sb("ends", [128, NT])
        base = room.sb("base", [128, NT])
        blank = room.sb("blank", [128, SEG * TILE, 2], I32)
        tot = room.ps("tot", [128, NT])
        pre = room.ps("pre", [128, NT])
        loaded, step, counted, summed = (room.sem(s) for s in ("loaded", "step", "counted", "summed"))
        placed, blanked, blank_set = (room.sem(s) for s in ("placed", "blanked", "blank_set"))
        ended = room.sem("ended")
        rec_rows = rec.rearrange("(q s) w -> q (s w)", q=128)
        with nc.Block() as block:

            @block.sync
            def _(sp):
                sp.dma_start(both[:, :, :], pairs.rearrange("(p j) w -> p j w", p=P)).then_inc(loaded, 16)
                sp.wait_ge(blank_set, 2)
                sp.dma_start(rec_rows, blank[:, :, :].rearrange("p s w -> p (s w)")).then_inc(blanked, 16)
                sp.wait_ge(placed, 1)
                sp.dma_start(tile_end, ends[0:1, :]).then_inc(ended, 16)
                sp.wait_ge(ended, 16)
                sp.wait_ge(blanked, 16)

            @block.vector
            def _(dve):
                link = Link(dve, step)
                link.put(dve.memset(zeros[:, :], 0.0))
                link.put(dve.memset(pos[:, :], 0.0))
                dve.wait_ge(loaded, 16)
                link.put(dve.tensor_copy(rec3[:, :, 1], both[:, :, 1 - end]))
                link.put(dve.tensor_copy(rec3[:, :, 2], both[:, :, end]))
                link(dve.tensor_copy(keyf[:, :], both[:, :, end]))
                block_of(dve, link, keyf, blk, blk_i, hit)
                link.begin(1)
                with dve.Fori(0, NT) as b:
                    link.turn(b)
                    link(dve.tensor_scalar(hit[:, :], blk[:, :], c["count"][0:P, bass.ds(b, 1)], 0.0,
                                           ALU.is_equal, ALU.add, accum_out=cnt[:, bass.ds(b, 1)]))
                link.close(NT)
                dve.nop().then_inc(counted, 1)
                dve.wait_ge(summed, 2)
                link(dve.tensor_scalar(tiles[:, :], tot[:, :], float(TILE - 1), None, ALU.add))
                link(dve.tensor_copy(tot_i[:, :], tiles[:, :]))
                link(dve.tensor_scalar(tot_i[:, :], tot_i[:, :], 7, None, ALU.logical_shift_right))
                link(dve.tensor_copy(tiles[:, :], tot_i[:, :]))
                link(dve.tensor_tensor_scan(ends[:, :], tiles[:, :], c["zero"][:, 0:NT],
                                            0.0, ALU.add, ALU.add))
                dve.nop().then_inc(placed, 1)
                link(dve.tensor_tensor(base[:, :], ends[:, :], tiles[:, :], ALU.subtract))
                link(dve.tensor_scalar(base[:, :], base[:, :], float(TILE), -1.0, ALU.mult, ALU.add))
                link(dve.tensor_tensor(base[0:P, :], base[0:P, :], pre[0:P, :], ALU.add))
                link.begin(4)
                with dve.Fori(0, NT) as b:
                    link.turn(b)
                    link(dve.tensor_scalar(hit[:, :], blk[:, :], c["count"][0:P, bass.ds(b, 1)], None, ALU.is_equal))
                    link(dve.tensor_tensor_scan(upto[:, :], hit[:, :], zeros[:, :], base[0:P, bass.ds(b, 1)],
                                                ALU.add, ALU.add))
                    link(dve.scalar_tensor_tensor(upto[:, :], blk[:, :], c["count"][0:P, bass.ds(b, 1)], upto[:, :],
                                                  ALU.is_equal, ALU.mult))
                    link(dve.tensor_tensor(pos[:, :], pos[:, :], upto[:, :], ALU.add))
                link.close(NT)
                link(dve.tensor_copy(rec3[:, :, 0], pos[:, :]))
                dve.nop().then_inc(placed, 1)

            @block.tensor
            def _(pe):
                pe.wait_ge(counted, 1)
                pe.matmul(tot[:, :], c["ones"][0:P, :], cnt[:, :], start=True, stop=True).then_inc(summed, 1)
                pe.matmul(pre[0:P, :], c["before"][:, :], cnt[:, :], start=True, stop=True).then_inc(summed, 1)

            @block.gpsimd
            def _(pool):
                pool.memset(blank[:, :, 0], 0).then_inc(blank_set, 1)
                pool.memset(blank[:, :, 1], -1).then_inc(blank_set, 1)
                if beside is not None:
                    beside(pool)


def lay_slots(nc, c, tag, rec, tile_end, idx, loc, flat_loc, blk, blk_off, width):
    with Room(nc, tag) as room:
        rows_i = room.sb("rows_i", [128, SEG, TILE, 2], I32)
        rows = room.sb("rows", [128, SEG, TILE, 2])
        oth = room.sb("oth", [128, TPAD])
        key = room.sb("key", [128, TPAD])
        idx_i = room.sb("idx_i", [128, TPAD], I32)
        locs = room.sb("locs", [128, TPAD])
        minus_first = room.sb("minus_first", [128, SEG])
        flat = room.sb("flat", [128, SEG, TILE])
        blk_i = room.sb("blk_i", [1, TPAD], I32)
        off = room.sb("off", [1, TPAD], I32)
        tcount_i = room.sb("tcount_i", [NT, TPAD], I32)
        tcount = room.sb("tcount", [NT, TPAD])
        end_row = room.sb("end_row", [1, NT])
        end_col = room.sb("end_col", [NT, 1])
        turned = [room.ps(f"turned{i}", [128, 2, 128]) for i in range(2)]
        col = room.ps("col", [128, 1 + SEG])
        blks = [room.ps(f"blk{i}", [128, TPAD // 4]) for i in range(4)]
        loaded, step, turn, copied = (room.sem(s) for s in ("loaded", "step", "turn", "copied"))
        tiled, blocks, col_made, stored = (room.sem(s) for s in ("tiled", "blocks", "col_made", "stored"))
        Q = TPAD // 4
        with nc.Block() as block:

            @block.sync
            def _(sp):
                sp.dma_start(end_row[:, :], tile_end).then_inc(loaded, 16)
                sp.dma_start(rows_i[:, :, :, :].rearrange("t c p w -> t c (p w)"),
                             rec.rearrange("(c t p) w -> t c (p w)", c=SEG, t=128)).then_inc(loaded, 16)
                sp.wait_ge(stored, 1)
                for a, b in ((idx, idx_i), (loc, locs), (blk, blk_i), (blk_off, off)):
                    sp.dma_start(a, b[:, :]).then_inc(stored, 16)
                sp.dma_start(flat_loc.rearrange("(c t p) -> t c p", c=SEG, t=128), flat[:, :, :]).then_inc(stored, 16)
                sp.wait_ge(stored, 81)

            @block.gpsimd
            def _(pool):
                pool.iota(tcount_i[:, :], pattern=[[1, TPAD]], base=0, channel_multiplier=0).then_inc(tiled, 1)

            @block.tensor
            def _(pe):
                pe.wait_ge(loaded, 32)
                pe.matmul(col[0:NT, 0:1], end_row[:, :], c["ones"][0:1, 0:1], start=True, stop=True).then_inc(col_made, 1)
                pe.wait_ge(col_made, 2)
                for k in range(SEG):
                    if k >= 2:
                        pe.wait_ge(copied, 2 * (k - 1))
                    for w in range(2):
                        pe.transpose(turned[k % 2][:, w, :], rows[:, k, :, w], c["ident"][:, :]).then_inc(turn, 1)
                pe.wait_ge(blocks, 1)
                for q in range(4):
                    pe.matmul(blks[q][:, :], c["ones"][0:NT - 1, :], tcount[0:NT - 1, q * Q:(q + 1) * Q],
                              start=True, stop=True).then_inc(blocks, 1)
                for k in range(SEG):
                    mm = pe.matmul(col[:, 1 + k:2 + k], tcount[0:NT - 1, k * 128:(k + 1) * 128], c["ones"][0:NT - 1, 0:1],
                                   start=True, stop=True)
                mm.then_inc(blocks, 1)

            @block.vector
            def _(dve):
                link = Link(dve, step)
                dve.wait_ge(loaded, 32)
                dve.tensor_copy(rows[:, :, :, :], rows_i[:, :, :, :]).then_inc(col_made, 1)
                dve.wait_ge(tiled, 1)
                link(dve.tensor_copy(tcount[:, :], tcount_i[:, :]))
                dve.wait_ge(col_made, 2)
                link(dve.tensor_copy(end_col[:, :], col[0:NT, 0:1]))
                link(dve.tensor_scalar(tcount[:, :], tcount[:, :], end_col[:, 0:1], None, ALU.is_ge))
                dve.nop().then_inc(blocks, 1)
                for k in range(SEG):
                    dve.wait_ge(turn, 2 * k + 2)
                    dve.tensor_copy(oth[:, k * 128:(k + 1) * 128], turned[k % 2][:, 0, :]).then_inc(copied, 1)
                    dve.tensor_copy(key[:, k * 128:(k + 1) * 128], turned[k % 2][:, 1, :]).then_inc(copied, 1)
                dve.wait_ge(copied, 2 * SEG)
                dve.wait_ge(blocks, 6)
                link.put(dve.tensor_copy(idx_i[:, :], oth[:, :]))
                for q in range(4):
                    s = slice(q * Q, (q + 1) * Q)
                    link.put(dve.scalar_tensor_tensor(locs[:, s], blks[q][:, :], -float(P), key[:, s], ALU.mult, ALU.add))
                    link.put(dve.tensor_scalar(off[0:1, s], blks[q][0:1, :], float(width), None, ALU.mult))
                    link.put(dve.tensor_copy(blk_i[0:1, s], blks[q][0:1, :]))
                link(dve.tensor_scalar(minus_first[:, :], col[:, 1:1 + SEG], -float(P), None, ALU.mult))
                link(dve.tensor_tensor(flat[:, :, :], rows[:, :, :, 1], bc(minus_first[:, :], 2, TILE), ALU.add))
                dve.nop().then_inc(stored, 1)


def spread_parts(nc, c, tag, flat_loc, blk, part, out, other=None):
    W = part.shape[1]
    idx, table, other_out = other if other is not None else (None, None, None)
    HALVES = TILES // BATCH
    COLS = BATCH * TILE
    with Room(nc, tag) as room:
        parts = room.sb("parts", [P, NT, W])
        blk_i = room.sb("blk_i", [1, TPAD], I32)
        row = room.sb("row", [1, 2, COLS])
        hotT = room.sb("hotT", [P, 2, COLS])
        slots = room.sb("slots", [128, W, TPAD])
        if other is not None:
            idx_i = room.sb("idx_i", [128, TPAD], I32)
            ids = room.sb("ids", [128, 2, BATCH], I32)
            got = room.sb("got", [128, 2, BATCH, W])
            got_slots = room.sb("got_slots", [128, W, TPAD])
            came = room.own_sems("came")
        idx_in, staged, taken = (room.sem(s) for s in ("idx_in", "staged", "taken"))
        psB = [[room.ps(f"psB{u}{q}", [128, 512]) for q in range(2)] for u in range(2)]
        psP = [room.ps(f"psP{u}", [128, BATCH, W]) for u in range(2)]
        loaded, widened, hot_ready, parted, copied, cleared, stored = (room.sem(s) for s in (
            "loaded", "widened", "hot_ready", "parted", "copied", "cleared", "stored"))
        row_in = [room.sem(f"row_in{u}") for u in range(2)]
        flat_row = flat_loc.rearrange("(a s) -> a s", a=1)
        with nc.Block() as block:

            @block.sync
            def _(sp):
                with nc.allow_non_contiguous_dma(reason="rows of a few numbers"):
                    sp.dma_start(parts[:, :, :], part.rearrange("(t p) w -> p t w", p=P)).then_inc(loaded, 16)
                sp.dma_start(blk_i[:, :], blk).then_inc(loaded, 16)
                if other is not None:
                    sp.dma_start(idx_i[:, :], idx).then_inc(idx_in, 16)
                for i, first in turns(sp, HALVES // 2):
                    for u in range(2):
                        n = i * 2 + u
                        if not first:
                            sp.wait_ge(widened, n - 1)
                        sp.dma_start(row[:, u, :], flat_row[:, slice(n * COLS, (n + 1) * COLS) if first else bass.ds(n * COLS, COLS)])\
                          .then_inc(row_in[u], 16)
                sp.wait_ge(copied, HALVES + 2)
                sp.wait_ge(cleared, 1)
                sp.dma_start(out, slots[:, :, :]).then_inc(stored, 16)
                sp.wait_ge(stored, 16)
                if other is not None:
                    sp.wait_ge(taken, HALVES + 2)
                    sp.wait_ge(cleared, 2)
                    sp.dma_start(other_out, got_slots[:, :, :]).then_inc(stored, 16)
                    sp.wait_ge(stored, 32)

            @block.gpsimd
            def _(pool):
                pool.memset(slots[:, :, TILES:TPAD], 0.0).then_inc(cleared, 1)
                if other is None:
                    return
                pool.memset(got_slots[:, :, TILES:TPAD], 0.0).then_inc(cleared, 1)
                pool.wait_ge(idx_in, 16)
                with pool.Fori(0, HALVES // 2) as i:
                    for u in range(2):
                        n = i * 2 + u
                        pool.wait_ge(taken, n + 1)
                        pool.nop(nofuse=True)
                        pool.tensor_copy(ids[:, u, :], idx_i[:, bass.ds(n * BATCH, BATCH)]).then_inc(staged, 1)
                        pool.wait_ge(staged, n + 1)
                        pool.nop(nofuse=True)
                        for k in range(BATCH):
                            pool.indirect_dma_start(
                                out=got[:, u, k, :], out_offset=None, in_=table[:, :],
                                in_offset=bass.IndirectOffsetOnAxis(ap=ids[:, u, k:k + 1], axis=0),
                            ).then_inc(came[u], 16)

            @block.tensor
            def _(pe):
                pe.wait_ge(loaded, 32)

                def widen(i, first, u):
                    n = i * 2 + u
                    pe.wait_ge(row_in[u], i * 16 + 16)
                    if not first:
                        pe.wait_ge(hot_ready, n - 1)
                    for q in range(2):
                        mm = pe.matmul(psB[u][q][0:P, :], c["ones"][0:1, 0:P], row[:, u, q * 512:(q + 1) * 512], start=True, stop=True)
                    mm.then_inc(widened, 1)

                def pick(n, u):
                    pe.wait_ge(hot_ready, n + 1)
                    pe.wait_ge(copied, n + 1)
                    at = slice(n * BATCH, (n + 1) * BATCH) if isinstance(n, int) else bass.ds(n * BATCH, BATCH)
                    of = numbers(nc, mybir.EngineType.PE, blk_i[0:1, at], NT - 1)
                    for k in range(BATCH):
                        mm = pe.matmul(psP[u][:, k, :], hotT[:, u, k * TILE:(k + 1) * TILE],
                                       parts[:, bass.ds(of[k], 1), :].rearrange("p a w -> p (a w)"), start=True, stop=True)
                    mm.then_inc(parted, 1)

                for i, first in turns(pe, HALVES // 2):
                    widen(i, first, 0)
                    if not first:
                        pick(i * 2 - 1, 1)
                    widen(i, first, 1)
                    pick(i * 2, 0)
                pick(HALVES - 1, 1)

            @block.vector
            def _(dve):
                if other is not None:
                    dve.nop().then_inc(taken, 2)
                for i, first in turns(dve, HALVES // 2):
                    for u in range(2):
                        n = i * 2 + u
                        dve.wait_ge(widened, n + 1)
                        if not first:
                            dve.wait_ge(parted, n - 1)
                        for q in range(2):
                            ins = dve.tensor_scalar(hotT[:, u, q * 512:(q + 1) * 512], psB[u][q][0:P, :], c["own"][0:P, 0:1], None, ALU.is_equal)
                        ins.then_inc(hot_ready, 1)
                        if other is not None:
                            cols = slice(n * BATCH, (n + 1) * BATCH) if first else bass.ds(n * BATCH, BATCH)
                            dve.wait_ge(came[u], i * (16 * BATCH) + 16 * BATCH)
                            dve.tensor_copy(got_slots[:, :, cols], got[:, u, :, :].rearrange("p k w -> p w k")).then_inc(taken, 1)

            @block.scalar
            def _(act):
                act.nop().then_inc(copied, 2)
                for i, first in turns(act, HALVES // 2):
                    for u in range(2):
                        n = i * 2 + u
                        cols = slice(n * BATCH, (n + 1) * BATCH) if first else bass.ds(n * BATCH, BATCH)
                        act.wait_ge(parted, n + 1)
                        act.nop(nofuse=True)
                        act.activation(slots[:, :, cols], psP[u][:, :, :].rearrange("p k w -> p w k"), ACT.Copy).then_inc(copied, 1)

SET = 5
LOAD = 10



def project_rows(nc, c, tag, x, xnT, xn_rows, weights, att, outs, beside=None):
    W0 = sum(w.shape[1] for w, _ in weights)
    WA = 1 + max((col for _, _, col in att), default=-1)
    W = W0 + WA
    with Room(nc, tag) as room:
        xin = room.sb("xin", [P, NT, D])
        xn = room.sb("xn", [P, 2, SET, D])
        stats = room.sb("stats", [P, SET, 6])
        moments = room.sb("moments", [P, SET, 2])
        mv = room.sb("mv", [P, NT, 2])
        sd = room.sb("sd", [P, NT])
        xT = room.sb("xT", [128, 2, KC, SET * P])
        wext = room.sb("wext", [128, KC, max(W, 1)])
        wT = room.sb("wT", [128, KC, D])
        attm = room.sb("attm", [128, KC, max(WA, 1)])
        res = room.sb("res", [P, 2, SET, max(W, 1)])
        psT = [room.ps(f"psT{u}", [128, KC, P]) for u in range(2)]
        psW = [room.ps(f"psW{u}", [128, 512]) for u in range(2)]
        names = ("weights_in", "att_zero", "att_in", "w_turned", "wT_copied", "att_product", "wext_ready",
                 "step", "var_ready", "sd_ready", "normed", "turned", "xT_ready", "projected",
                 "res_ready")
        s = {n: room.sem(n) for n in names}
        loaded = [room.sem(f"loaded{g}") for g in range(NT // LOAD)]
        xT_out, res_out, xn_out = ([room.sem(f"{n}{v}") for v in range(2)] for n in ("xT_out", "res_out", "xn_out"))

        def rows_of(ap, i, first, v):
            n = SET * P
            rows = slice(v * n, (v + 1) * n) if first else bass.ds((i * 2 + v) * n, n)
            return ap[rows, :].rearrange("(t p) w -> p t w", p=P)

        with nc.Block() as block:

            @block.sync
            def _(sp):
                for g in range(NT // LOAD):
                    sp.dma_start(xin[:, g * LOAD:(g + 1) * LOAD, :],
                                 x[g * LOAD * P:(g + 1) * LOAD * P, :].rearrange("(t p) d -> p t d", p=P)).then_inc(loaded[g], 16)
                for w, col in weights:
                    with nc.allow_non_contiguous_dma(reason="the router's few rows come as columns"):
                        for k in range(KC):
                            sp.dma_start(wext[:, k, col:col + w.shape[1]], w[k * 128:(k + 1) * 128, :]).then_inc(s["weights_in"], 16)
                if att:
                    sp.wait_ge(s["att_zero"], 1)
                    for src, row, col in att:
                        n = src.shape[0]
                        sp.dma_start(attm[row % 128:row % 128 + n, row // 128, col:col + 1],
                                     src.rearrange("(n a) -> n a", a=1)).then_inc(s["att_in"], 16)
                for i, first in turns(sp, NT // (2 * SET)):
                    for v in range(2):
                        sets = i * 2 + v + 1
                        if xn_rows is not None:
                            sp.wait_ge(s["normed"], sets * SET)
                            sp.nop(nofuse=True)
                            sp.dma_start(rows_of(xn_rows, i, first, v), xn[:, v, :, :]).then_inc(xn_out[v], 16)
                        sp.wait_ge(s["xT_ready"], sets * SET)
                        sp.nop(nofuse=True)
                        n = SET * P
                        cols = slice(v * n, (v + 1) * n) if first else bass.ds((i * 2 + v) * n, n)
                        sp.dma_start(xnT[:, :, cols], xT[:, v, :, :]).then_inc(xT_out[v], 16)
                        if W:
                            sp.wait_ge(s["res_ready"], sets * SET)
                            sp.nop(nofuse=True)
                            with nc.allow_non_contiguous_dma(reason="rows of a few numbers"):
                                for o, col, w in outs:
                                    sp.dma_start(rows_of(o, i, first, v), res[:, v, :, col:col + w]).then_inc(res_out[v], 16)
                for v in range(2):
                    sp.wait_ge(xT_out[v], 16 * (NT // (2 * SET)))
                    if W:
                        sp.wait_ge(res_out[v], 16 * (NT // (2 * SET)) * len(outs))
                    if xn_rows is not None:
                        sp.wait_ge(xn_out[v], 16 * (NT // (2 * SET)))

            @block.gpsimd
            def _(pool):
                if att:
                    pool.memset(attm[:, :, :], 0.0).then_inc(s["att_zero"], 1)
                if beside is not None:
                    beside(pool)

            @block.vector
            def _(dve):
                link = Link(dve, s["step"])
                if att:
                    dve.wait_ge(s["w_turned"], 2 * KC)
                    for k in range(KC):
                        dve.tensor_copy(wT[:, k, :], psW[k][:, 0:D]).then_inc(s["wT_copied"], 1)
                    dve.wait_ge(s["att_product"], KC)
                    for k in range(KC):
                        dve.tensor_copy(wext[:, k, W0:W], psT[k][:, 0, 0:WA]).then_inc(s["wext_ready"], 1)
                link.begin(2 * SET + 1)
                for g in range(NT // LOAD):
                    dve.wait_ge(loaded[g], 16)
                    with dve.Fori(g * LOAD // SET, (g + 1) * LOAD // SET) as n:
                        link.turn(n)
                        for j in range(SET):
                            link.put(dve.bn_stats(stats[:, j, :], xin[:, bass.ds(n * SET + j, 1), :].rearrange("p a d -> p (a d)")))
                        link.sync(hold=True)
                        for j in range(SET):
                            link.put(dve.bn_aggr(moments[:, j, :], stats[:, j, :]))
                        link.sync()
                        link(dve.tensor_copy(mv[:, bass.ds(n * SET, SET), :], moments[:, :, :]))
                link.close(NT // SET)
                dve.tensor_scalar(sd[:, :], mv[:, :, 1], 1e-5, None, ALU.add).then_inc(s["var_ready"], 1)
                dve.wait_ge(s["sd_ready"], 1)
                link(dve.reciprocal(sd[:, :], sd[:, :]))
                for i, first in turns(dve, NT // (2 * SET)):
                    for u in range(2 * SET):
                        t = i * 2 * SET + u
                        v, j = u // SET, u % SET
                        if not first:
                            dve.wait_ge(s["turned"], t - (2 * SET - 1))
                            if xn_rows is not None and j == 0:
                                dve.wait_ge(xn_out[v], i * 16)
                        tt = slice(t, t + 1) if first else bass.ds(t, 1)
                        dve.tensor_scalar(xn[:, v, j, :], xin[:, tt, :].rearrange("p a d -> p (a d)"),
                                          mv[:, tt, 0], sd[:, tt], ALU.subtract, ALU.mult).then_inc(s["normed"], 1)

            @block.scalar
            def _(act):
                act.wait_ge(s["var_ready"], 1)
                act.activation(sd[:, :], sd[:, :], ACT.Sqrt).then_inc(s["sd_ready"], 1)

                for i, first in turns(act, NT // (2 * SET)):
                    for u in range(2 * SET):
                        t = i * 2 * SET + u
                        v, j = u // SET, u % SET
                        act.wait_ge(s["turned"], t + 1)
                        if j == 0 and not first:
                            act.wait_ge(xT_out[v], i * 16)
                        act.activation(xT[:, v, :, j * P:(j + 1) * P], psT[u % 2][:, :, :], ACT.Copy).then_inc(s["xT_ready"], 1)
                        if W and not (first and u == 0):
                            before = (u - 1) % (2 * SET)
                            act.wait_ge(s["projected"], t)
                            if before % SET == 0 and not first:
                                act.wait_ge(res_out[before // SET], i * (16 * len(outs)))
                            act.activation(res[:, before // SET, before % SET, :], psW[before % 2][0:P, 0:W], ACT.Copy)\
                               .then_inc(s["res_ready"], 1)
                if W:
                    act.wait_ge(s["projected"], NT)
                    act.activation(res[:, 1, SET - 1, :], psW[1][0:P, 0:W], ACT.Copy).then_inc(s["res_ready"], 1)

            @block.tensor
            def _(pe):
                if weights:
                    pe.wait_ge(s["weights_in"], 16 * KC * len(weights))
                if att:
                    for k in range(KC):
                        for m in range(KC):
                            pe.transpose(psW[k][:, m * 128:(m + 1) * 128], wext[:, m, k * 128:(k + 1) * 128],
                                         c["ident"][:, :]).then_inc(s["w_turned"], 1)
                    pe.wait_ge(s["wT_copied"], KC)
                    pe.wait_ge(s["att_in"], 16 * len(att))
                    for m in range(KC):
                        for k in range(KC):
                            mm = pe.matmul(psT[m][:, 0, 0:WA], wT[:, k, m * 128:(m + 1) * 128], attm[:, k, :],
                                           start=(k == 0), stop=(k == KC - 1))
                        mm.then_inc(s["att_product"], 1)
                    pe.wait_ge(s["wext_ready"], KC)
                def project(t, u, begun):
                    v, j = u // SET, u % SET
                    pe.wait_ge(s["xT_ready"], t + 1)
                    if begun:
                        pe.wait_ge(s["res_ready"], t - 1)
                    for k in range(KC):
                        mm = pe.matmul(psW[u % 2][0:P, 0:W], xT[:, v, k, j * P:(j + 1) * P], wext[:, k, :],
                                       start=(k == 0), stop=(k == KC - 1))
                    mm.then_inc(s["projected"], 1)

                for i, first in turns(pe, NT // (2 * SET)):
                    for u in range(2 * SET):
                        t = i * 2 * SET + u
                        pe.wait_ge(s["normed"], t + 1)
                        if not (first and u < 2):
                            pe.wait_ge(s["xT_ready"], t - 1)
                        for k in range(KC):
                            mm = pe.transpose(psT[u % 2][:, k, :], xn[:, u // SET, u % SET, k * 128:(k + 1) * 128], c["ident"][0:P, 0:P])
                        mm.then_inc(s["turned"], 1)
                        if W and not (first and u == 0):
                            project(t - 1, (u - 1) % (2 * SET), not (first and u < 3))
                if W:
                    project(NT - 1, 2 * SET - 1, True)


def softmax_weights(nc, c, tag, rec, src_slots, dst_slots, out):
    H = src_slots.shape[1]
    RUN = SEG * TILE
    with Room(nc, tag) as room:
        src = room.sb("src", [128, H, TPAD])
        best = room.sb("best", [128, H, RUN])
        recs = room.sb("recs", [128, RUN, 2], I32)
        keys = room.sb("keys", [128, RUN])
        fresh = room.sb("fresh", [128, RUN + 1])
        pen_last = room.sb("pen_last", [128, RUN])
        one = room.sb("one", [128, RUN])
        two = room.sb("two", [128, RUN])
        dst = room.sb("dst", [128, RUN])
        edge = room.sb("edge", [128, 4, H])
        edgeT = room.sb("edgeT", [H, 4, 128])
        join = room.sb("join", [H, 129])
        whole = room.sb("whole", [H, 128])
        reset = room.sb("reset", [H, 128])
        carry = room.sb("carry", [H, 2, 128])
        carryT = room.sb("carryT", [128, 2, H])
        ps = [room.ps(f"ps{i}", [128, 512]) for i in range(4)]
        small = room.ps("small", [128, 512])
        names = ("loaded", "rec_in", "step", "picked", "turned", "scanned", "edges_ready", "edges_turned", "carried",
                 "carry_turned", "carry_ready", "merged", "back", "spread", "dst_in", "diff", "exps", "stored")
        s = {n: room.sem(n) for n in names}
        key = keys[:, :]
        rr = src[:, :, :].rearrange("p h (q r) -> p h r q", r=SEG)
        with nc.Block() as block:

            @block.sync
            def _(sp):
                sp.dma_start(recs[:, :, :].rearrange("q s w -> q (s w)"),
                             rec.rearrange("(q s) w -> q (s w)", q=128)).then_inc(s["rec_in"], 16)
                sp.dma_start(src[:, :, :], src_slots).then_inc(s["loaded"], 16)
                for h, first in turns(sp, H):
                    if not first:
                        sp.wait_ge(s["diff"], h)
                    sp.dma_start(dst[:, :], dst_slots[:, bass.ds(h, 1) if not first else slice(0, 1), :]
                                 .rearrange("p a t -> p (a t)")).then_inc(s["dst_in"], 16)
                sp.wait_ge(s["exps"], H)
                sp.dma_start(out, src[:, :, :]).then_inc(s["stored"], 16)
                sp.wait_ge(s["stored"], 16)

            @block.scalar
            def _(act):
                act.wait_ge(s["loaded"], 16)
                for h, first in turns(act, H):
                    hs = bass.ds(h, 1) if not first else slice(0, 1)
                    if not first:
                        act.wait_ge(s["scanned"], h)
                        act.nop(nofuse=True)
                    act.activation(one[:, :], src[:, hs, :].rearrange("p a t -> p (a t)"), ACT.Copy).then_inc(s["picked"], 1)
                for h, first in turns(act, H):
                    hs = bass.ds(h, 1) if not first else slice(0, 1)
                    act.wait_ge(s["diff"], h + 1)
                    act.nop(nofuse=True)
                    act.activation(src[:, hs, :].rearrange("p a t -> p (a t)"), one[:, :], ACT.Exp).then_inc(s["exps"], 1)

            @block.tensor
            def _(pe):
                for h, first in turns(pe, H):
                    pe.wait_ge(s["picked"], h + 1)
                    view = one[:, :].rearrange("p (q r) -> p r q", r=SEG)
                    for r in range(SEG):
                        mm = pe.transpose(ps[r // 4][:, r % 4 * 128:(r % 4 + 1) * 128], view[:, r, :], c["ident"][:, :])
                    mm.then_inc(s["turned"], 1)
                pe.wait_ge(s["edges_ready"], 1)
                for n in range(4):
                    mm = pe.transpose(small[0:H, n * 128:(n + 1) * 128], edge[:, n, :], c["ident"][:, :])
                mm.then_inc(s["edges_turned"], 1)
                pe.wait_ge(s["carried"], 1)
                for n in range(2):
                    mm = pe.transpose(small[:, n * H:(n + 1) * H], carry[:, n, :], c["ident"][0:H, 0:H])
                mm.then_inc(s["carry_turned"], 1)
                for h, first in turns(pe, H):
                    pe.wait_ge(s["merged"], h + 1)
                    for r in range(SEG):
                        mm = pe.transpose(ps[r // 4][:, r % 4 * 128:(r % 4 + 1) * 128],
                                          two[:, r * 128:(r + 1) * 128], c["ident"][:, :])
                    mm.then_inc(s["back"], 1)

            @block.vector
            def _(dve):
                link = Link(dve, s["step"])
                dve.wait_ge(s["rec_in"], 16)
                link(dve.tensor_copy(keys[:, :], recs[:, :, 1]))
                link.put(dve.memset(fresh[:, 0:1], -BIG))
                link.put(dve.memset(fresh[:, RUN:RUN + 1], -BIG))
                link(dve.tensor_tensor(fresh[:, 1:RUN], key[:, 1:RUN], key[:, 0:RUN - 1], ALU.is_equal))
                link(dve.tensor_scalar(fresh[:, 1:RUN], fresh[:, 1:RUN], -1.0, BIG, ALU.add, ALU.mult))
                link.begin(7)
                for h, first in turns(dve, H):
                    link.turn(h)
                    hs = bass.ds(h, 1) if not first else slice(0, 1)
                    bh = best[:, hs, :].rearrange("p a t -> p (a t)")
                    dve.wait_ge(s["turned"], h + 1)
                    for b in range(4):
                        w = min(512, RUN - b * 512)
                        link.put(dve.tensor_copy(two[:, b * 512:b * 512 + w], ps[b][:, 0:w]))
                    link.sync()
                    link.put(dve.tensor_tensor_scan(bh, fresh[:, 0:RUN], two[:, :], -BIG, ALU.add, ALU.max))
                    link(dve.tensor_tensor_scan(one[:, ::-1], fresh[:, :0:-1], two[:, ::-1], -BIG, ALU.add, ALU.max))
                    link(dve.tensor_tensor(bh, bh, one[:, :], ALU.max))
                    dve.nop().then_inc(s["scanned"], 1)
                link.close(H)
                link.put(dve.tensor_copy(edge[:, 0, :], best[:, :, RUN - 1]))
                link.put(dve.tensor_copy(edge[:, 1, :], best[:, :, 0]))
                link.put(dve.tensor_copy(edge[:, 2, :], key[:, 0:1].broadcast_to([128, H])))
                link(dve.tensor_copy(edge[:, 3, :], key[:, RUN - 1:RUN].broadcast_to([128, H])))
                dve.nop().then_inc(s["edges_ready"], 1)
                dve.wait_ge(s["edges_turned"], 1)
                link.put(dve.memset(join[:, 0:1], 0.0))
                link.put(dve.memset(join[:, 128:129], 0.0))
                link(dve.tensor_copy(edgeT[:, :, :], small[0:H, :].rearrange("h (n q) -> h n q", n=4)))
                kf, kl = edgeT[:, 2, :], edgeT[:, 3, :]
                link.put(dve.tensor_tensor(join[:, 1:128], kf[:, 1:128], kl[:, 0:127], ALU.is_equal))
                link(dve.tensor_tensor(whole[:, :], kf, kl, ALU.is_equal))
                link.put(dve.tensor_scalar(join[:, :], join[:, :], -1.0, BIG, ALU.add, ALU.mult))
                link(dve.tensor_scalar(whole[:, :], whole[:, :], -1.0, BIG, ALU.add, ALU.mult))
                for n, (lo, step) in enumerate(((0, 1), (1, -1))):
                    link(dve.tensor_tensor(reset[:, :], join[:, lo:lo + 128], whole[:, :], ALU.min))
                    link(dve.tensor_tensor_scan(carry[:, n, ::step], reset[:, ::step], edgeT[:, n, ::step], -BIG, ALU.add, ALU.max))
                link.put(dve.tensor_tensor(reset[:, 1:128], carry[:, 0, 0:127], join[:, 1:128], ALU.add))
                link(dve.tensor_tensor(whole[:, 0:127], carry[:, 1, 1:128], join[:, 1:128], ALU.add))
                link.put(dve.tensor_copy(carry[:, 0, 1:128], reset[:, 1:128]))
                link.put(dve.tensor_copy(carry[:, 1, 0:127], whole[:, 0:127]))
                link.put(dve.memset(carry[:, 0, 0:1], -BIG))
                link(dve.memset(carry[:, 1, 127:128], -BIG))
                dve.nop().then_inc(s["carried"], 1)
                dve.wait_ge(s["carry_turned"], 1)
                link(dve.tensor_copy(carryT[:, :, :], small[:, 0:2 * H].rearrange("q (n h) -> q n h", n=2)))
                link.put(dve.tensor_scalar(fresh[:, 0:RUN], key, key[:, 0:1], -1.0, ALU.is_equal, ALU.add))
                link(dve.tensor_scalar(pen_last[:, :], key, key[:, RUN - 1:RUN], -1.0, ALU.is_equal, ALU.add))
                link.put(dve.tensor_scalar(fresh[:, 0:RUN], fresh[:, 0:RUN], BIG, None, ALU.mult))
                link(dve.tensor_scalar(pen_last[:, :], pen_last[:, :], BIG, None, ALU.mult))
                link.begin(12)
                for h, first in turns(dve, H):
                    link.turn(h)
                    hs = bass.ds(h, 1) if not first else slice(0, 1)
                    bh = best[:, hs, :].rearrange("p a t -> p (a t)")
                    sh = src[:, hs, :].rearrange("p a t -> p (a t)")
                    link(dve.scalar_tensor_tensor(two[:, :], fresh[:, 0:RUN], carryT[:, 0, hs], bh, ALU.add, ALU.max))
                    link(dve.scalar_tensor_tensor(two[:, :], pen_last[:, :], carryT[:, 1, hs], two[:, :], ALU.add, ALU.max))
                    dve.nop().then_inc(s["merged"], 1)
                    dve.wait_ge(s["back"], h + 1)
                    back = two[:, :].rearrange("p (q r) -> p r q", r=SEG)
                    for b in range(4):
                        w = min(4, SEG - b * 4)
                        link.put(dve.tensor_copy(back[:, b * 4:b * 4 + w, :],
                                                 ps[b][:, 0:w * 128].rearrange("p (r q) -> p r q", r=w)))
                    dve.wait_ge(s["dst_in"], h * 16 + 16)
                    if not first:
                        dve.wait_ge(s["exps"], h)
                    link(dve.tensor_tensor(one[:, :], sh, dst[:, :], ALU.add))
                    link.put(dve.tensor_tensor(two[:, :], two[:, :], dst[:, :], ALU.add))
                    link(dve.scalar_tensor_tensor(one[:, :], one[:, :], 0.2, one[:, :], ALU.mult, ALU.max))
                    link(dve.scalar_tensor_tensor(two[:, :], two[:, :], 0.2, two[:, :], ALU.mult, ALU.max))
                    link(dve.tensor_tensor(one[:, :], one[:, :], two[:, :], ALU.subtract))
                    link(dve.tensor_scalar(one[:, :], one[:, :], 0.0, None, ALU.min))
                    dve.nop().then_inc(s["diff"], 1)
                link.close(H)


def sum_edges(nc, c, tag, idx, loc, blk_off, table, H, weights_in, key_side, finish):
    C = D // H
    W = table.shape[1]
    WT = D + H
    kind, resid, bias, out = finish
    own_weights = weights_in is None
    SETS = TILES // BATCH
    RINGR = 4
    BANKS = 4 if own_weights else 8
    COLS = BATCH * TILE
    GRP = 5
    with Room(nc, tag) as room:
        acc = room.sb("acc", [P, NT, WT])
        idx_i = room.sb("idx_i", [128, TPAD], I32)
        locs = room.sb("locs", [128, TPAD])
        off = room.sb("off", [1, TPAD], I32)
        ids = room.sb("ids", [128, RINGR, BATCH], I32)
        rows = room.sb("rows", [128, RINGR, BATCH, WT])
        hot = room.sb("hot", [128, 2, BATCH, P])
        if own_weights:
            flat_loc, blk, part = key_side
            flat_row = flat_loc.rearrange("(a s) -> a s", a=1)
            parts = room.sb("parts", [P, NT, H])
            blk_i = room.sb("blk_i", [1, TPAD], I32)
            row = room.sb("row", [1, 2, COLS])
            hotT = room.sb("hotT", [P, 2, COLS])
            z = room.sb("z", [128, BATCH, H])
            valid = room.sb("valid", [128, BATCH])
            neg = room.sb("neg", [P, GRP, D])
            psB = [room.ps(f"psB{q}", [128, 512]) for q in range(2)]
            psP = [room.ps(f"psP{u}", [128, 512]) for u in range(2)]
        else:
            wslot = room.sb("wslot", [128, H, TPAD])
        res = room.sb("res", [P, GRP, D])
        den = room.sb("den", [P, NT, H])
        biasr = room.sb("biasr", [P, D])
        ps = [room.ps(f"ps{k}", [128, 512]) for k in range(BANKS)]
        names = ("loaded", "idx_in", "step", "staged", "weights_ready", "weighted", "summed", "added", "resid_in",
                 "finished", "stored", "lrelu", "expd", "widened", "hotT_ready", "picked", "key_used")
        s = {n: room.sem(n) for n in names}
        row_in = [room.sem(f"row_in{u}") for u in range(2)]
        came = room.own_sems("came", RINGR)
        LOADS = 4 if own_weights else 3 + (bias is not None)
        accf = acc[:, :, :].rearrange("p t w -> p (t w)")
        countb = bc(c["count"][:, 0:P], 1, BATCH)

        def cols(n):
            return slice(n * BATCH, (n + 1) * BATCH) if isinstance(n, int) else bass.ds(n * BATCH, BATCH)

        def steps(eng):
            for i, first in turns(eng, SETS // RINGR):
                for r in range(RINGR):
                    yield i, r, i * RINGR + r

        late = lambda n, k: not isinstance(n, int) or n >= k
        with nc.Block() as block:

            @block.sync
            def _(sp):
                sp.dma_start(idx_i[:, :], idx).then_inc(s["idx_in"], 16)
                sp.dma_start(locs[:, :], loc).then_inc(s["loaded"], 16)
                sp.dma_start(off[:, :], blk_off).then_inc(s["loaded"], 16)
                if own_weights:
                    with nc.allow_non_contiguous_dma(reason="rows of a few numbers"):
                        sp.dma_start(parts[:, :, :], part.rearrange("(t p) w -> p t w", p=P)).then_inc(s["loaded"], 16)
                    sp.dma_start(blk_i[:, :], blk).then_inc(s["loaded"], 16)
                    sp.dma_start(row[:, 0, :], flat_row[:, 0:COLS]).then_inc(row_in[0], 16)
                    for i, r, n in steps(sp):
                        if late(n, 1):
                            sp.wait_ge(s["widened"], n)
                            sp.nop(nofuse=True)
                        at = (n + 1) * COLS
                        sp.dma_start(row[:, (r + 1) % 2, :], flat_row[:, slice(at, at + COLS) if isinstance(n, int) else bass.ds(at, COLS)])\
                          .then_inc(row_in[(r + 1) % 2], 16)
                else:
                    sp.dma_start(wslot[:, :, :], weights_in).then_inc(s["loaded"], 16)
                if bias is not None:
                    sp.dma_start(biasr[:, :], bias.partition_broadcast(P)).then_inc(s["loaded"], 16)
                for g in range(NT // GRP):
                    if g:
                        sp.wait_ge(s["stored"], 16 * g)
                    sp.dma_start(res[:, :, :], resid[g * GRP * P:(g + 1) * GRP * P, :].rearrange("(t p) d -> p t d", p=P)).then_inc(s["resid_in"], 16)
                    sp.wait_ge(s["finished"], g + 1)
                    sp.dma_start(out[g * GRP * P:(g + 1) * GRP * P, :].rearrange("(t p) d -> p t d", p=P), res[:, :, :]).then_inc(s["stored"], 16)
                sp.wait_ge(s["stored"], 16 * (NT // GRP))

            @block.gpsimd
            def _(pool):
                pool.wait_ge(s["idx_in"], 16)
                for i, r, n in steps(pool):
                    if late(n, RINGR):
                        pool.wait_ge(s["summed"], (n - (RINGR - 1)) * BATCH)
                        pool.nop(nofuse=True)
                    pool.tensor_copy(ids[:, r, :], idx_i[:, cols(n)]).then_inc(s["staged"], 1)
                    pool.wait_ge(s["staged"], n + 1)
                    pool.nop(nofuse=True)
                    for k in range(BATCH):
                        pool.indirect_dma_start(
                            out=rows[:, r, k, 0:W], out_offset=None, in_=table[:, :],
                            in_offset=bass.IndirectOffsetOnAxis(ap=ids[:, r, k:k + 1], axis=0)).then_inc(came[r], 16)

            @block.scalar
            def _(act):
                act.wait_ge(s["loaded"], 16 * LOADS)
                for i, r, n in steps(act):
                    if own_weights:
                        act.wait_ge(s["lrelu"], n + 1)
                        act.activation(rows[:, r, :, D:WT], z[:, :, :], ACT.Exp, scale=-1.0).then_inc(s["weights_ready"], 1)
                    else:
                        if late(n, RINGR):
                            act.wait_ge(s["summed"], (n - (RINGR - 1)) * BATCH)
                            act.nop(nofuse=True)
                        act.activation(rows[:, r, :, D:WT], wslot[:, :, cols(n)].rearrange("p h k -> p k h"),
                                       ACT.Copy).then_inc(s["weights_ready"], 1)
                if kind == "elu":
                    for g in range(NT // GRP):
                        act.wait_ge(s["lrelu"], SETS + g + 1)
                        act.activation(neg[:, :, :], neg[:, :, :], ACT.Exp).then_inc(s["expd"], 1)

            @block.tensor
            def _(pe):
                pe.wait_ge(s["loaded"], 16 * LOADS)

                def widen(m, par, times):
                    pe.wait_ge(row_in[par], 16 * times)
                    if late(m, 1):
                        pe.wait_ge(s["hotT_ready"], m)
                    for q in range(2):
                        mm = pe.matmul(psB[q][0:P, :], c["ones"][0:1, 0:P], row[:, par, q * 512:(q + 1) * 512], start=True, stop=True)
                    mm.then_inc(s["widened"], 1)

                def pick(n, r):
                    pe.wait_ge(s["hotT_ready"], n + 1)
                    if late(n, 2):
                        pe.wait_ge(s["key_used"], n - 1)
                    of = numbers(nc, mybir.EngineType.PE, blk_i[0:1, cols(n)], NT - 1)
                    for k in range(BATCH):
                        mm = pe.matmul(psP[r % 2][:, k * H:(k + 1) * H], hotT[:, r % 2, k * TILE:(k + 1) * TILE],
                                       parts[:, bass.ds(of[k], 1), :].rearrange("p a w -> p (a w)"), start=True, stop=True)
                    mm.then_inc(s["picked"], 1)

                def sums(n, r):
                    pe.wait_ge(s["weighted"], n + 1)
                    for k in range(BATCH):
                        if late(n * BATCH + k, BANKS):
                            pe.wait_ge(s["added"], n * BATCH + (k + 1 - BANKS))
                        pe.matmul(ps[k % BANKS][0:P, 0:WT], hot[:, r % 2, k, :], rows[:, r, k, :], start=True, stop=True)\
                          .then_inc(s["summed"], 1)

                if own_weights:
                    widen(0, 0, 1)
                for i, r, n in steps(pe):
                    if own_weights:
                        pick(n, r)
                        widen(n + 1, (r + 1) % 2, i * (RINGR // 2) + (r + 1) // 2 + 1)
                    if late(n, 1):
                        sums(n - 1, (r - 1) % RINGR)
                sums(SETS - 1, RINGR - 1)

            @block.vector
            def _(dve):
                link = Link(dve, s["step"])
                link(dve.memset(acc[:, :, :], 0.0))
                dve.wait_ge(s["loaded"], 16 * LOADS)

                def turn_hot(m, par):
                    dve.wait_ge(s["widened"], m + 1)
                    if late(m, 2):
                        dve.wait_ge(s["picked"], m - 1)
                    for q in range(2):
                        ins = dve.tensor_scalar(hotT[:, par, q * 512:(q + 1) * 512], psB[q][0:P, :], c["own"][0:P, 0:1], None, ALU.is_equal)
                    ins.then_inc(s["hotT_ready"], 1)

                def weigh(i, r, n):
                    if late(n, 2):
                        dve.wait_ge(s["summed"], (n - 1) * BATCH)
                    link.put(dve.tensor_tensor(hot[:, r % 2, :, :], countb, bc(locs[:, cols(n)], 2, P), ALU.is_equal))
                    if own_weights:
                        link.put(dve.tensor_scalar(valid[:, :], locs[:, cols(n)], 0.0, None, ALU.is_ge))
                    dve.wait_ge(came[r], i * (16 * BATCH) + 16 * BATCH)
                    if own_weights:
                        dve.wait_ge(s["picked"], n + 1)
                        link(dve.tensor_tensor(z[:, :, :], rows[:, r, :, D:WT],
                                               psP[r % 2][:, 0:BATCH * H].rearrange("p (k h) -> p k h", h=H), ALU.add))
                        dve.nop().then_inc(s["key_used"], 1)
                        link(dve.scalar_tensor_tensor(z[:, :, :], z[:, :, :], 0.2, z[:, :, :], ALU.mult, ALU.max))
                        dve.tensor_tensor(z[:, :, :], z[:, :, :], bc(valid[:, :], 2, H), ALU.mult).then_inc(s["lrelu"], 1)
                    dve.wait_ge(s["weights_ready"], n + 1)
                    for k in range(BATCH):
                        v = rows[:, r, k, 0:D].rearrange("p (h c) -> p h c", h=H)
                        link.put(dve.tensor_tensor(v, v, bc(rows[:, r, k, D:WT], 2, C), ALU.mult))
                    link.sync()
                    dve.nop().then_inc(s["weighted"], 1)

                def add(n):
                    starts = numbers(nc, mybir.EngineType.DVE, off[0:1, cols(n)], (NT - 1) * WT)
                    for k in range(BATCH):
                        a = accf[:, bass.ds(starts[k], WT)]
                        dve.wait_ge(s["summed"], n * BATCH + (k + 1))
                        if late(n * BATCH + k, 1):
                            dve.wait_ge(s["added"], n * BATCH + k)
                        dve.tensor_tensor(a, a, ps[k % BANKS][0:P, 0:WT], ALU.add).then_inc(s["added"], 1)

                if own_weights:
                    turn_hot(0, 0)
                link.begin(RINGR * (1 + BATCH + (3 if own_weights else 0)))
                for i, r, n in steps(dve):
                    if r == 0:
                        link.turn(i)
                    weigh(i, r, n)
                    if own_weights:
                        turn_hot(n + 1, (r + 1) % 2)
                    if late(n, 1):
                        add(n - 1)
                link.close(SETS // RINGR)
                add(SETS - 1)
                dve.wait_ge(s["added"], TILES)
                if kind == "relu":
                    link(dve.tensor_scalar(den[:, :, :], acc[:, :, D:WT], 1e-16, None, ALU.add))
                    link(dve.reciprocal(den[:, :, :], den[:, :, :]))
                else:
                    link(dve.reciprocal(den[:, :, :], acc[:, :, D:WT]))
                for g in range(NT // GRP):
                    for t in range(g * GRP, (g + 1) * GRP):
                        v = acc[:, t, 0:D].rearrange("p (h c) -> p h c", h=H)
                        link.put(dve.tensor_tensor(v, v, bc(den[:, t, :], 2, C), ALU.mult))
                    link.sync()
                    v = acc[:, g * GRP:(g + 1) * GRP, 0:D]
                    if kind == "relu":
                        link(dve.tensor_tensor(v, v, bc(biasr[:, :], 1, GRP), ALU.add))
                        dve.wait_ge(s["resid_in"], 16 * (g + 1))
                        dve.scalar_tensor_tensor(res[:, :, :], v, 0.0, res[:, :, :], ALU.max, ALU.add).then_inc(s["finished"], 1)
                    else:
                        if g:
                            dve.wait_ge(s["finished"], g)
                        dve.tensor_scalar(neg[:, :, :], v, 0.0, None, ALU.min).then_inc(s["lrelu"], 1)
                        dve.wait_ge(s["resid_in"], 16 * (g + 1))
                        link(dve.scalar_tensor_tensor(res[:, :, :], v, 0.0, res[:, :, :], ALU.max, ALU.add))
                        dve.wait_ge(s["expd"], g + 1)
                        dve.scalar_tensor_tensor(res[:, :, :], neg[:, :, :], -1.0, res[:, :, :], ALU.add, ALU.add).then_inc(s["finished"], 1)


def dyn(i, first, step, width):
    return slice(i * step, i * step + width) if first or isinstance(i, int) else bass.ds(i * step, width)


RING = 5


def mix_keys(nc, c, tag, x, xnT, W_qk, b_qk, W_v, b_v, gamma, beta, out, beside):
    with Room(nc, tag) as room:
        XT = room.sb("XT", [128, KC, N])
        wq = room.sb("wq", [128, KC, D])
        wk = room.sb("wk", [128, KC, D])
        wv = room.sb("wv", [128, KC, D])
        bcol = room.sb("bcol", [128, 4, KC])
        bv = room.sb("bv", [1, D])
        kmaxs = room.sb("kmaxs", [128, KC, NCH])
        shift = room.sb("shift", [128, KC])
        kmax = room.sb("kmax", [128, KC])
        shift_row = room.sb("shift_row", [1, KC, 128])
        xs = room.sb("xs", [128, 2, KC, P])
        ek = room.sb("ek", [P, 2, D])
        val = room.sb("val", [P, 2, D + 1])
        lam = room.sb("lam", [128, KC, D])
        den = room.sb("den", [128, KC])
        stats = room.sb("stats", [128, KC, 6])
        mv = room.sb("mv", [128, KC, 2])
        sd = room.sb("sd", [128, KC])
        qT = room.sb("qT", [128, KC, CH])
        res = room.sb("res", [P, RING, 2, D])
        psK = [room.ps(f"psK{m}", [128, 512]) for m in range(KC)]
        psKV = [room.ps(f"psKV{u}", [128, 512]) for u in range(2)]
        psV = [room.ps(f"psV{u}", [128, 512]) for u in range(2)]
        psL = [room.ps(f"psL{m}", [128, 512]) for m in range(KC)]
        names = ("loaded", "step", "keyed", "maxed", "shift_ready", "shift_turned", "shift_copied", "xs_ready", "kv_ready",
                 "exp_ready", "val_ready", "lam_ready", "summed", "sd_ready", "var_ready", "bn_ready", "q_ready", "qT_ready",
                 "o_ready", "done")
        s = {n: room.sem(n) for n in names}
        res_in, res_out = ([room.sem(f"{n}{u}") for u in range(RING)] for n in ("res_in", "res_out"))
        with nc.Block() as block:

            @block.sync
            def _(sp):
                sp.dma_start(XT[:, :, :], xnT).then_inc(s["loaded"], 16)
                for w, src in ((wq, W_qk[0]), (wk, W_qk[1]), (wv, W_v)):
                    sp.dma_start(w[:, :, :], src.rearrange("(k p) w -> p k w", p=128)).then_inc(s["loaded"], 16)
                for n, src in enumerate((b_qk[0], b_qk[1], gamma, beta)):
                    with nc.allow_non_contiguous_dma(reason="a short vector, one number per partition"):
                        sp.dma_start(bcol[:, n, :], src.rearrange("(k p) -> p k", p=128)).then_inc(s["loaded"], 16)
                sp.dma_start(bv[:, :], b_v.rearrange("(a n) -> a n", a=1)).then_inc(s["loaded"], 16)
                for i, first in turns(sp, NCH // RING):
                    for u in range(RING):
                        rows = dyn(i * RING + u, first, CH, CH)
                        if not first:
                            sp.wait_ge(res_out[u], i * 16)
                        sp.dma_start(res[:, u, :, :], x[rows, :].rearrange("(t p) d -> p t d", p=P)).then_inc(res_in[u], 16)

            @block.scalar
            def _(act):
                act.wait_ge(s["loaded"], 16 * 9)
                for i, first in turns(act, NT // 2):
                    for u in range(2):
                        t = i * 2 + u
                        if not first:
                            act.wait_ge(s["kv_ready"], t - 1)
                            act.nop(nofuse=True)
                        act.activation(xs[:, u, :, :], XT[:, :, dyn(t, first, P, P)], ACT.Copy).then_inc(s["xs_ready"], 1)
                        act.wait_ge(s["kv_ready"], t + 1)
                        if not first:
                            act.wait_ge(s["lam_ready"], t - 1)
                        act.activation(ek[:, u, :], psKV[u][0:P, 0:D], ACT.Exp).then_inc(s["exp_ready"], 1)
                act.wait_ge(s["var_ready"], 1)
                act.activation(sd[:, :], mv[:, :, 1], ACT.Sqrt).then_inc(s["sd_ready"], 1)
                for i, first in turns(act, NCH // RING):
                    for u in range(RING):
                        n = i * RING + u
                        rows = dyn(n, first, CH, CH)
                        act.wait_ge(s["q_ready"], n + 1)
                        if not (first and u == 0):
                            act.wait_ge(s["o_ready"], n)
                        for m in range(KC):
                            act.activation(qT[:, m, :], psK[m][:, 0:CH], ACT.Identity, bias=bcol[:, 0, m:m + 1])\
                               .then_inc(s["qT_ready"], 1)
                        if not (first and u == 0):
                            act.wait_ge(s["done"], n)
                            prev = n - 1
                            act.dma_start(out[dyn(prev, first, CH, CH), :].rearrange("(t p) d -> p t d", p=P),
                                          res[:, (u - 1) % RING, :, :]).then_inc(res_out[(u - 1) % RING], 16)
                act.wait_ge(s["done"], NCH)
                act.dma_start(out[N - CH:N, :].rearrange("(t p) d -> p t d", p=P), res[:, RING - 1, :, :]).then_inc(res_out[RING - 1], 16)
                for u in range(RING):
                    act.wait_ge(res_out[u], 16 * (NCH // RING))

            @block.tensor
            def _(pe):
                pe.wait_ge(s["loaded"], 16 * 9)
                for i, first in turns(pe, NCH):
                    if not first:
                        pe.wait_ge(s["maxed"], i * KC)
                    for m in range(KC):
                        for k in range(KC):
                            mm = pe.matmul(psK[m][:, 0:CH], wk[:, k, m * 128:(m + 1) * 128], XT[:, k, dyn(i, first, CH, CH)],
                                           start=(k == 0), stop=(k == KC - 1))
                        mm.then_inc(s["keyed"], 1)
                pe.wait_ge(s["shift_ready"], 1)
                for m in range(KC):
                    pe.transpose(psKV[0][0:1, m * 128:(m + 1) * 128], shift[:, m:m + 1], c["ident"][:, :])\
                      .then_inc(s["shift_turned"], 1)
                pe.wait_ge(s["shift_copied"], 1)
                for i, first in turns(pe, NT // 2):
                    for u in range(2):
                        t = i * 2 + u
                        pe.wait_ge(s["xs_ready"], t + 1)
                        if not first:
                            pe.wait_ge(s["exp_ready"], t - 1)
                            pe.wait_ge(s["val_ready"], t - 1)
                        for w, o, b in ((wk, psKV[u], shift_row[:, :, :].rearrange("a k n -> a (k n)")), (wv, psV[u], bv[:, :])):
                            pe.matmul(o[0:P, 0:D], c["ones"][0:1, 0:P], b, start=True, stop=False)
                            for k in range(KC):
                                mm = pe.matmul(o[0:P, 0:D], xs[:, u, k, :], w[:, k, :], start=False, stop=(k == KC - 1))
                        mm.then_inc(s["kv_ready"], 1)
                        pe.wait_ge(s["exp_ready"], t + 1)
                        pe.wait_ge(s["val_ready"], t + 1)
                        for m in range(KC):
                            mm = pe.matmul(psL[m][:, 0:D + 1], ek[:, u, m * 128:(m + 1) * 128], val[:, u, :],
                                           start=(first and u == 0), stop=False, skip_group_check=True)
                        mm.then_inc(s["lam_ready"], 1)
                for m in range(KC):
                    mm = pe.matmul(psL[m][:, 0:D + 1], c["zero"][0:1, :], val[0:1, 0, :], start=False, stop=True, skip_group_check=True)
                mm.then_inc(s["summed"], 1)
                pe.wait_ge(s["bn_ready"], 1)
                for i, first in turns(pe, NCH // RING):
                    for u in range(RING):
                        n = i * RING + u
                        if not (first and u == 0):
                            pe.wait_ge(s["qT_ready"], n * KC)
                        for m in range(KC):
                            for k in range(KC):
                                mm = pe.matmul(psK[m][:, 0:CH], wq[:, k, m * 128:(m + 1) * 128], XT[:, k, dyn(n, first, CH, CH)],
                                               start=(k == 0), stop=(k == KC - 1))
                        mm.then_inc(s["q_ready"], 1)
                        pe.wait_ge(s["qT_ready"], n * KC + KC)
                        if not (first and u == 0):
                            pe.wait_ge(s["done"], n)
                        for j in range(2):
                            for m in range(KC):
                                mm = pe.matmul(psKV[0][0:P, j * D:(j + 1) * D], qT[:, m, j * P:(j + 1) * P], lam[:, m, :],
                                               start=(m == 0), stop=(m == KC - 1))
                        mm.then_inc(s["o_ready"], 1)

            @block.gpsimd
            def _(pool):
                beside(pool)

            @block.vector
            def _(dve):
                link = Link(dve, s["step"])
                link(dve.memset(val[:, :, D:D + 1], 1.0))
                for i, first in turns(dve, NCH):
                    for m in range(KC):
                        dve.wait_ge(s["keyed"], i * KC + (m + 1))
                        dve.nop(nofuse=True)
                        dve.tensor_reduce(kmaxs[:, m, dyn(i, first, 1, 1)], psK[m][:, 0:CH], AX, ALU.max).then_inc(s["maxed"], 1)
                dve.wait_ge(s["maxed"], NCH * KC)
                link(dve.tensor_reduce(kmax[:, :], kmaxs[:, :, :], AX, ALU.max))
                dve.wait_ge(s["loaded"], 16 * 9)
                link(dve.tensor_tensor(kmax[:, :], kmax[:, :], bcol[:, 1, :], ALU.add))
                link(dve.tensor_tensor(shift[:, :], bcol[:, 1, :], kmax[:, :], ALU.subtract))
                dve.nop().then_inc(s["shift_ready"], 1)
                dve.wait_ge(s["shift_turned"], KC)
                dve.tensor_copy(shift_row[:, :, :].rearrange("a k n -> a (k n)"), psKV[0][0:1, 0:KC * 128]).then_inc(s["shift_copied"], 1)
                for i, first in turns(dve, NT // 2):
                    for u in range(2):
                        t = i * 2 + u
                        dve.wait_ge(s["kv_ready"], t + 1)
                        if not first:
                            dve.wait_ge(s["lam_ready"], t - 1)
                        dve.tensor_copy(val[:, u, 0:D], psV[u][0:P, 0:D]).then_inc(s["val_ready"], 1)
                dve.wait_ge(s["summed"], 1)
                for m in range(KC):
                    link(dve.reciprocal(den[:, m:m + 1], psL[m][:, D:D + 1]))
                    link(dve.tensor_scalar(lam[:, m, :], psL[m][:, 0:D], den[:, m:m + 1], None, ALU.mult))
                    link(dve.bn_stats(stats[:, m, :], lam[:, m, :]))
                    link(dve.bn_aggr(mv[:, m, :], stats[:, m, :]))
                link(dve.tensor_scalar(mv[:, :, 1], mv[:, :, 1], 1e-5, None, ALU.add))
                dve.nop().then_inc(s["var_ready"], 1)
                dve.wait_ge(s["sd_ready"], 1)
                link(dve.reciprocal(sd[:, :], sd[:, :]))
                for m in range(KC):
                    link(dve.tensor_scalar(lam[:, m, :], lam[:, m, :], mv[:, m, 0:1], sd[:, m:m + 1], ALU.subtract, ALU.mult))
                    link(dve.tensor_scalar(lam[:, m, :], lam[:, m, :], bcol[:, 2, m:m + 1], bcol[:, 3, m:m + 1], ALU.mult, ALU.add))
                dve.nop().then_inc(s["bn_ready"], 1)
                for i, first in turns(dve, NCH // RING):
                    for u in range(RING):
                        n = i * RING + u
                        dve.wait_ge(res_in[u], i * 16 + 16)
                        dve.wait_ge(s["o_ready"], n + 1)
                        r = res[:, u, :, :].rearrange("p t d -> p (t d)")
                        dve.tensor_tensor(r, r, psKV[0][0:P, :], ALU.add).then_inc(s["done"], 1)


def experts(nc, c, tag, x, xnT, logits, w1, w2, w3, out, beside):
    X, HID = w1.shape[0], w1.shape[1]
    HC = -(-HID // 128)
    PAIRS = HC // 2
    GRP = NT // 5
    part = [min(128, HID - j * 128) for j in range(HC)]
    with Room(nc, tag) as room:
        XT = room.sb("XT", [128, KC, N])
        Y = room.sb("Y", [P, NT, D])
        raw1 = room.sb("raw1", [128, HC, D])
        raw3 = room.sb("raw3", [128, HC, D])
        raw2 = room.sb("raw2", [128, KC, HID])
        w1T = room.sb("w1T", [128, KC, HC * 128])
        w3T = room.sb("w3T", [128, KC, HC * 128])
        w2T = room.sb("w2T", [128, HC, D])
        sil = room.sb("sil", [128, PAIRS, 2, CH])
        hT = room.sb("hT", [128, PAIRS, 2, CH])
        gate = room.sb("gate", [P, X, NT])
        g1 = room.sb("g1", [P, NT])
        g2 = room.sb("g2", [P, NT])
        mask = room.sb("mask", [P, X, NT])
        cand = room.sb("cand", [P, X, NT])
        both = room.sb("both", [P, X, NT])
        gcol = room.sb("gcol", [P, NT])
        lraw = room.sb("lraw", [P, NT, X])
        res = room.sb("res", [P, GRP, D])
        psH = [[room.ps(f"psH{n}{q}", [128, 512]) for q in range(PAIRS)] for n in range(2)]
        psY = room.ps("psY", [128, 512])
        psT = room.ps("psT", [128, 512])
        names = ("loaded", "raw_in", "step", "shifted", "exped", "turned", "copied", "gate_set", "hid", "silued", "mulled",
                 "y_ready", "added", "res_in", "done", "stored")
        s = {n: room.sem(n) for n in names}
        turnjobs = []
        for raw, wT in ((raw1, w1T), (raw3, w3T)):
            for k in range(KC):
                for j in range(HC):
                    turnjobs.append((raw[0:part[j], j, k * 128:(k + 1) * 128], part[j], wT[:, k, j * 128:j * 128 + part[j]], 128))
        for j in range(HC):
            for k in range(KC):
                turnjobs.append((raw2[:, k, j * 128:j * 128 + part[j]], 128, w2T[0:part[j], j, k * 128:(k + 1) * 128], part[j]))
        NTJ = len(turnjobs)
        with nc.Block() as block:

            @block.sync
            def _(sp):
                sp.dma_start(XT[:, :, :], xnT).then_inc(s["loaded"], 16)
                sp.dma_start(lraw[:, :, :], logits.rearrange("(t p) e -> p t e", p=P)).then_inc(s["loaded"], 16)
                full = HID // 128
                for e, first in turns(sp, X):
                    if not first:
                        sp.wait_ge(s["turned"], e * NTJ)
                    es = dyn(e, first, 1, 1)
                    for raw, w in ((raw1, w1), (raw3, w3)):
                        we = w[es, :, :].rearrange("e h c -> (e h) c")
                        sp.dma_start(raw[:, 0:full, :], we[0:full * 128, :].rearrange("(j p) c -> p j c", p=128)).then_inc(s["raw_in"], 16)
                        sp.dma_start(raw[0:part[-1], full, :], we[full * 128:HID, :]).then_inc(s["raw_in"], 16)
                    sp.dma_start(raw2[:, :, :], w2[es, :, :].rearrange("e (k p) h -> p (e k) h", p=128)).then_inc(s["raw_in"], 16)
                tiles_of = lambda ap, g: ap[g * GRP * P:(g + 1) * GRP * P, :].rearrange("(t p) d -> p t d", p=P)
                for g in range(NT // GRP):
                    if g:
                        sp.wait_ge(s["done"], g)
                    sp.dma_start(res[:, :, :], tiles_of(x, g)).then_inc(s["res_in"], 16)
                    if g:
                        sp.dma_start(tiles_of(out, g - 1), Y[:, (g - 1) * GRP:g * GRP, :]).then_inc(s["stored"], 16)
                sp.wait_ge(s["done"], NT // GRP)
                sp.dma_start(tiles_of(out, NT // GRP - 1), Y[:, NT - GRP:NT, :]).then_inc(s["stored"], 16)
                sp.wait_ge(s["stored"], 16 * (NT // GRP))

            @block.scalar
            def _(act):
                act.wait_ge(s["shifted"], 1)
                act.activation(gate[:, :, :], gate[:, :, :], ACT.Exp).then_inc(s["exped"], 1)
                with act.Fori(0, X) as e:
                    for i, first in turns(act, NCH):
                        n = e * NCH + i
                        for q in range(PAIRS):
                            act.wait_ge(s["hid"], n * PAIRS + (q + 1))
                            if part[2 * q + 1] == 128:
                                act.activation(sil[:, q, :, :].rearrange("p j n -> p (j n)"), psH[0][q][:, 0:2 * CH], ACT.Silu)\
                                   .then_inc(s["silued"], 1)
                            else:
                                w = part[2 * q + 1]
                                act.activation(sil[0:w, q, 1, :], psH[0][q][0:w, CH:2 * CH], ACT.Silu)
                                act.activation(sil[:, q, 0, :], psH[0][q][:, 0:CH], ACT.Silu).then_inc(s["silued"], 1)

            @block.tensor
            def _(pe):
                pe.wait_ge(s["loaded"], 32)
                with pe.Fori(0, X) as e:
                    pe.wait_ge(s["raw_in"], e * 80 + 80)
                    for n, (src, rows, dst, w) in enumerate(turnjobs):
                        if n % 4 == 0:
                            pe.wait_ge(s["copied"], e * NTJ + (n + 1))
                        pe.transpose(psT[0:w, n % 4 * 128:n % 4 * 128 + rows], src, c["ident"][0:rows, 0:rows]).then_inc(s["turned"], 1)
                    pe.wait_ge(s["copied"], e * NTJ + (NTJ + 1))
                    for i, first in turns(pe, NCH):
                        n = e * NCH + i
                        cols = dyn(i, first, CH, CH)

                        def hidden(q):
                            pe.wait_ge(s["mulled"], n * PAIRS + (q + 1))
                            for a, wT in enumerate((w1T, w3T)):
                                for j in (2 * q, 2 * q + 1):
                                    for k in range(KC):
                                        mm = pe.matmul(psH[a][q][0:part[j], (j % 2) * CH:(j % 2 + 1) * CH],
                                                       wT[:, k, j * 128:j * 128 + part[j]], XT[:, k, cols],
                                                       start=(k == 0), stop=(k == KC - 1))
                            mm.then_inc(s["hid"], 1)

                        def down(q):
                            pe.wait_ge(s["mulled"], n * PAIRS + (PAIRS + q + 1))
                            if q == 0:
                                pe.wait_ge(s["added"], n * 2 + 2)
                            for t in range(2):
                                for j in (2 * q, 2 * q + 1):
                                    mm = pe.matmul(psY[0:P, t * D:(t + 1) * D], hT[0:part[j], q, j % 2, t * P:(t + 1) * P],
                                                   w2T[0:part[j], j, :], start=(j == 0 and t == 0), stop=(j == HC - 1), skip_group_check=True)
                            if q == PAIRS - 1:
                                mm.then_inc(s["y_ready"], 1)

                        hidden(0)
                        for q in range(1, PAIRS):
                            hidden(q)
                            down(q - 1)
                        down(PAIRS - 1)

            @block.gpsimd
            def _(pool):
                beside(pool)

            @block.vector
            def _(dve):
                link = Link(dve, s["step"])
                link(dve.memset(Y[:, :, :], 0.0))
                dve.wait_ge(s["loaded"], 32)
                link(dve.tensor_copy(gate[:, :, :], lraw[:, :, :].rearrange("p t e -> p e t")))
                by_tile = lambda ap: ap[:, :, :].rearrange("p e t -> p t e")
                row = lambda ap: bc(ap[:, :], 1, X)
                link(dve.tensor_reduce(g1[:, :], by_tile(gate), AX, ALU.max))
                link(dve.tensor_tensor(gate[:, :, :], gate[:, :, :], row(g1), ALU.subtract))
                dve.nop().then_inc(s["shifted"], 1)
                dve.wait_ge(s["exped"], 1)
                link(dve.tensor_reduce(g1[:, :], by_tile(gate), AX, ALU.add))
                link(dve.reciprocal(g1[:, :], g1[:, :]))
                link(dve.tensor_tensor(gate[:, :, :], gate[:, :, :], row(g1), ALU.mult))
                link(dve.memset(both[:, :, :], 0.0))
                for _ in range(2):
                    link(dve.scalar_tensor_tensor(cand[:, :, :], both[:, :, :], -2.0, gate[:, :, :], ALU.mult, ALU.add))
                    link(dve.tensor_reduce(g2[:, :], by_tile(cand), AX, ALU.max))
                    link(dve.tensor_tensor(mask[:, :, :], cand[:, :, :], row(g2), ALU.is_equal))
                    number = c["count"][0:P, 0:X].unsqueeze(2).broadcast_to([P, X, NT])
                    link(dve.scalar_tensor_tensor(cand[:, :, :], mask[:, :, :], -float(X), number, ALU.mult, ALU.add))
                    link(dve.tensor_reduce(g2[:, :], by_tile(cand), AX, ALU.min))
                    link(dve.tensor_tensor(mask[:, :, :], cand[:, :, :], row(g2), ALU.is_equal))
                    link(dve.tensor_tensor(both[:, :, :], both[:, :, :], mask[:, :, :], ALU.add))
                link(dve.tensor_tensor(gate[:, :, :], gate[:, :, :], both[:, :, :], ALU.mult))
                link(dve.tensor_reduce(g1[:, :], by_tile(gate), AX, ALU.add))
                link(dve.tensor_scalar(g1[:, :], g1[:, :], 1e-9, None, ALU.add))
                link(dve.reciprocal(g1[:, :], g1[:, :]))
                link(dve.tensor_tensor(gate[:, :, :], gate[:, :, :], row(g1), ALU.mult))
                dve.nop().then_inc(s["copied"], 1)
                dve.nop().then_inc(s["mulled"], PAIRS)
                dve.nop().then_inc(s["added"], 2)
                with dve.Fori(0, X) as e:
                    dve.wait_ge(s["added"], e * (2 * NCH) + 2)
                    dve.nop(nofuse=True)
                    dve.tensor_copy(gcol[:, :], gate[:, bass.ds(e, 1), :].rearrange("p a t -> p (a t)")).then_inc(s["gate_set"], 1)
                    for n, (src, rows, dst, w) in enumerate(turnjobs):
                        if n % 4 == 0:
                            dve.wait_ge(s["turned"], e * NTJ + min(n + 4, NTJ))
                        dve.tensor_copy(dst, psT[0:w, n % 4 * 128:n % 4 * 128 + rows]).then_inc(s["copied"], 1)
                    dve.wait_ge(s["gate_set"], e + 1)
                    for i, first in turns(dve, NCH):
                        n = e * NCH + i
                        for q in range(PAIRS):
                            dve.wait_ge(s["silued"], n * PAIRS + (q + 1))
                            if part[2 * q + 1] == 128:
                                dve.tensor_tensor(hT[:, q, :, :].rearrange("p j n -> p (j n)"),
                                                  sil[:, q, :, :].rearrange("p j n -> p (j n)"), psH[1][q][:, 0:2 * CH],
                                                  ALU.mult).then_inc(s["mulled"], 1)
                            else:
                                w = part[2 * q + 1]
                                dve.tensor_tensor(hT[0:w, q, 1, :], sil[0:w, q, 1, :], psH[1][q][0:w, CH:2 * CH], ALU.mult)
                                dve.tensor_tensor(hT[:, q, 0, :], sil[:, q, 0, :], psH[1][q][:, 0:CH], ALU.mult).then_inc(s["mulled"], 1)
                        dve.wait_ge(s["y_ready"], n + 1)
                        dve.nop(nofuse=True)
                        for t in range(2):
                            tt = dyn(i * 2 + t, first, 1, 1)
                            y = Y[:, tt, :].rearrange("p a d -> p (a d)")
                            dve.scalar_tensor_tensor(y, psY[0:P, t * D:(t + 1) * D], gcol[:, tt], y, ALU.mult, ALU.add).then_inc(s["added"], 1)
                dve.wait_ge(s["added"], X * NCH * 2 + 2)
                for g in range(NT // GRP):
                    y = Y[:, g * GRP:(g + 1) * GRP, :]
                    dve.wait_ge(s["res_in"], g * 16 + 16)
                    dve.tensor_tensor(y, y, res[:, :, :], ALU.add).then_inc(s["done"], 1)


def mix_heads(nc, c, tag, x, xn_rows, xnT, w_qkv, b_qkv, k_g, k_b, v_g, v_b, w1, b1, w2, b2, out):
    HCOLS = k_g.shape[0]
    H = D // HCOLS
    HB = H // KC
    with Room(nc, tag) as room:
        XT = room.sb("XT", [128, KC, N])
        wkv = room.sb("wkv", [128, KC, 2, H, HCOLS])
        wq = room.sb("wq", [128, KC, H, HCOLS])
        w1s = room.sb("w1s", [128, KC, D])
        w2s = room.sb("w2s", [128, KC, D])
        bkv = room.sb("bkv", [1, 2, H, HCOLS])
        bq = room.sb("bq", [128, KC])
        b1c = room.sb("b1c", [128, KC])
        b2r = room.sb("b2r", [1, D])
        gain = room.sb("gain", [P, 2, 2, HCOLS])
        xs = room.sb("xs", [128, 2, KC, P])
        cen = room.sb("cen", [P, 2, 2 * H, HCOLS])
        sq = room.sb("sq", [P, 2 * H, HCOLS])
        mean = room.sb("mean", [P, 2 * H])
        var = room.sb("var", [P, 2 * H])
        kv = room.sb("kv", [128, KC, 128])
        qT = room.sb("qT", [128, KC, CH])
        retT = room.sb("retT", [128, KC, CH])
        hT = room.sb("hT", [128, KC, CH])
        res = room.sb("res", [P, RING, 2, D])
        xnr = room.sb("xnr", [P, RING, 2, D])
        ps = [room.ps(f"ps{n}", [128, 512]) for n in range(8)]
        psR, psKV = ps[0:2], ps[2:4]
        psQ, psH, psY = ps[4:6], ps[6:8], ps[0]
        names = ("loaded", "step", "xs_ready", "kv_ready", "centred", "var_ready", "sd_ready", "normed", "kv_added", "kv_done",
                 "kv_set", "q_ready", "qT_ready", "ret_ready", "retT_ready", "h_ready", "hT_ready", "y_ready", "done")
        s = {n: room.sem(n) for n in names}
        res_in, res_out = ([room.sem(f"{n}{u}") for u in range(RING)] for n in ("res_in", "res_out"))
        ALL = 16 * (1 + 3 * KC + 2 + 1 + 2 + 2 * HB + 4 + 1)
        with nc.Block() as block:

            @block.sync
            def _(sp):
                def load(dst, src):
                    with nc.allow_non_contiguous_dma(reason="short vectors as columns"):
                        sp.dma_start(dst, src).then_inc(s["loaded"], 16)
                load(XT[:, :, :], xnT)
                parts = w_qkv.rearrange("(k p) (h s c) -> k s p h c", p=128, h=H, s=3)
                bparts = b_qkv.rearrange("(h s c) -> s h c", h=H, s=3)
                for k in range(KC):
                    load(wq[:, k, :, :], parts[k, 0])
                    for n in range(2):
                        load(wkv[:, k, n, :, :], parts[k, 1 + n])
                load(w1s[:, :, :], w1.rearrange("(k p) w -> p k w", p=128))
                load(w2s[:, :, :], w2.rearrange("(k p) w -> p k w", p=128))
                load(b1c[:, :], b1.rearrange("(k p) -> p k", p=128))
                for n in range(2):
                    load(bkv[:, n, :, :], bparts[1 + n].unsqueeze(0))
                    for h in range(HB):
                        sp.dma_start(bq[h * HCOLS:(h + 1) * HCOLS, n:n + 1],
                                     bparts[0, n * HB + h].rearrange("(c a) -> c a", a=1)).then_inc(s["loaded"], 16)
                for n, v in enumerate((k_g, v_g, k_b, v_b)):
                    load(gain[:, n // 2, n % 2, :], v.partition_broadcast(P))
                load(b2r[:, :], b2.rearrange("(a n) -> a n", a=1))
                for i, first in turns(sp, NCH // RING):
                    for u in range(RING):
                        rows = dyn(i * RING + u, first, CH, CH)
                        if not first:
                            sp.wait_ge(res_out[u], i * 16)
                        for dst, src in ((res, x), (xnr, xn_rows)):
                            sp.dma_start(dst[:, u, :, :], src[rows, :].rearrange("(t p) d -> p t d", p=P)).then_inc(res_in[u], 16)

            @block.scalar
            def _(act):
                act.wait_ge(s["loaded"], ALL)
                for i, first in turns(act, NT // 2):
                    for u in range(2):
                        t = i * 2 + u
                        if not first:
                            act.wait_ge(s["kv_ready"], t - 1)
                            act.nop(nofuse=True)
                        act.activation(xs[:, u, :, :], XT[:, :, dyn(t, first, P, P)], ACT.Copy).then_inc(s["xs_ready"], 1)
                        act.wait_ge(s["var_ready"], t + 1)
                        act.activation(var[:, :], var[:, :], ACT.Sqrt).then_inc(s["sd_ready"], 1)
                def store(n, u, at):
                    act.wait_ge(s["done"], n + 1)
                    act.nop(nofuse=True)
                    act.dma_start(out[at, :].rearrange("(t p) d -> p t d", p=P), res[:, u, :, :]).then_inc(res_out[u], 16)

                for i, first in turns(act, NCH // RING):
                    for u in range(RING):
                        n = i * RING + u
                        begun = not (first and u == 0)
                        act.wait_ge(s["q_ready"], n + 1)
                        if begun:
                            act.wait_ge(s["ret_ready"], n)
                        for m in range(KC):
                            act.activation(qT[:, m, :], psQ[m][:, 0:CH], ACT.Identity, bias=bq[:, m:m + 1]).then_inc(s["qT_ready"], 1)
                        act.wait_ge(s["h_ready"], n + 1)
                        if begun:
                            act.wait_ge(s["y_ready"], n)
                        for m in range(KC):
                            act.activation(hT[:, m, :], psH[m][:, 0:CH], ACT.Gelu, bias=b1c[:, m:m + 1]).then_inc(s["hT_ready"], 1)
                        if begun:
                            store(n - 1, (u - 1) % RING, dyn(n - 1, first, CH, CH))
                store(NCH - 1, RING - 1, dyn(NCH - 1, True, CH, CH))
                for u in range(RING):
                    act.wait_ge(res_out[u], 16 * (NCH // RING))

            @block.tensor
            def _(pe):
                pe.wait_ge(s["loaded"], ALL)

                def add_kv(t, u, opens):
                    pe.wait_ge(s["normed"], t + 1)
                    flat = cen[:, u, :, :].rearrange("p g c -> p (g c)")
                    for m in range(KC):
                        mm = pe.matmul(psKV[m][:, 0:128], flat[:, m * 128:(m + 1) * 128], flat[:, D + m * 128:D + (m + 1) * 128],
                                       start=opens, stop=False, skip_group_check=True)
                    mm.then_inc(s["kv_added"], 1)

                for i, first in turns(pe, NT // 2):
                    for u in range(2):
                        t = i * 2 + u
                        pe.wait_ge(s["xs_ready"], t + 1)
                        if not first:
                            pe.wait_ge(s["centred"], t - 1)
                        pe.matmul(psR[u][0:P, :], c["ones"][0:1, 0:P], bkv[:, :, :, :].rearrange("a n h c -> a (n h c)"), start=True, stop=False)
                        for k in range(KC):
                            mm = pe.matmul(psR[u][0:P, :], xs[:, u, k, :], wkv[:, k, :, :, :].rearrange("p n h c -> p (n h c)"),
                                           start=False, stop=(k == KC - 1))
                        mm.then_inc(s["kv_ready"], 1)
                        if not (first and u == 0):
                            add_kv(t - 1, 1 - u, first and u == 1)
                add_kv(NT - 1, 1, False)
                for m in range(KC):
                    mm = pe.matmul(psKV[m][:, 0:128], c["zero"][0:1, :], c["zero"][0:1, :], start=False, stop=True, skip_group_check=True)
                mm.then_inc(s["kv_done"], 1)
                pe.wait_ge(s["kv_set"], 1)

                def finish(n, begun):
                    pe.wait_ge(s["hT_ready"], n * KC + KC)
                    if begun:
                        pe.wait_ge(s["done"], n)
                    for j in range(2):
                        pe.matmul(psY[0:P, j * D:(j + 1) * D], c["ones"][0:1, 0:P], b2r[:, :], start=True, stop=False)
                        for k in range(KC):
                            mm = pe.matmul(psY[0:P, j * D:(j + 1) * D], hT[:, k, j * P:(j + 1) * P], w2s[:, k, :], start=False, stop=(k == KC - 1))
                    mm.then_inc(s["y_ready"], 1)

                for i, first in turns(pe, NCH // RING):
                    for u in range(RING):
                        n = i * RING + u
                        begun = not (first and u == 0)
                        for m in range(KC):
                            for k in range(KC):
                                mm = pe.matmul(psQ[m][:, 0:CH], wq[:, k, m * HB:(m + 1) * HB, :].rearrange("p h c -> p (h c)"),
                                               XT[:, k, dyn(n, first, CH, CH)], start=(k == 0), stop=(k == KC - 1))
                        mm.then_inc(s["q_ready"], 1)
                        pe.wait_ge(s["qT_ready"], n * KC + KC)
                        for m in range(KC):
                            mm = pe.matmul(psKV[m][:, 0:CH], kv[:, m, :], qT[:, m, :], start=True, stop=True)
                        mm.then_inc(s["ret_ready"], 1)
                        if begun:
                            finish(n - 1, not (first and u == 1))
                        pe.wait_ge(s["retT_ready"], n * KC + KC)
                        for m in range(KC):
                            for k in range(KC):
                                mm = pe.matmul(psH[m][:, 0:CH], w1s[:, k, m * 128:(m + 1) * 128], retT[:, k, :], start=(k == 0), stop=(k == KC - 1))
                        mm.then_inc(s["h_ready"], 1)
                finish(NCH - 1, True)

            @block.vector
            def _(dve):
                link = Link(dve, s["step"])
                dve.wait_ge(s["loaded"], ALL)
                link.begin(2 * 9)
                for i, first in turns(dve, NT // 2):
                    link.turn(i)
                    for u in range(2):
                        t = i * 2 + u
                        raw = psR[u][0:P, :].rearrange("p (g c) -> p g c", c=HCOLS)
                        cu = cen[:, u, :, :]
                        dve.wait_ge(s["kv_ready"], t + 1)
                        link(dve.tensor_reduce(mean[:, :], raw, AX, ALU.add))
                        link(dve.tensor_scalar(mean[:, :], mean[:, :], 1.0 / HCOLS, None, ALU.mult))
                        if not first:
                            dve.wait_ge(s["kv_added"], t - 1)
                        dve.tensor_tensor(cu, raw, bc(mean[:, :], 2, HCOLS), ALU.subtract).then_inc(s["centred"], 1)
                        dve.wait_ge(s["centred"], t + 1)
                        link(dve.tensor_tensor(sq[:, :, :], cu, cu, ALU.mult))
                        link(dve.tensor_reduce(mean[:, :], sq[:, :, :], AX, ALU.add))
                        link(dve.tensor_scalar(var[:, :], mean[:, :], 1.0 / HCOLS, 1e-5, ALU.mult, ALU.add))
                        dve.nop().then_inc(s["var_ready"], 1)
                        dve.wait_ge(s["sd_ready"], t + 1)
                        link(dve.reciprocal(mean[:, :], var[:, :]))
                        link(dve.tensor_tensor(cu, cu, bc(mean[:, :], 2, HCOLS), ALU.mult))
                        by_kv = cu.rearrange("p (n h) c -> p n h c", n=2)
                        link.put(dve.tensor_tensor(by_kv[:, 0], by_kv[:, 0], bc(gain[:, 0, 0, :], 1, H), ALU.mult))
                        link(dve.tensor_tensor(by_kv[:, 1], by_kv[:, 1], bc(gain[:, 0, 1, :], 1, H), ALU.mult))
                        dve.tensor_tensor(by_kv[:, 0], by_kv[:, 0], bc(gain[:, 1, 0, :], 1, H), ALU.add)
                        dve.tensor_tensor(by_kv[:, 1], by_kv[:, 1], bc(gain[:, 1, 1, :], 1, H), ALU.add).then_inc(s["normed"], 1)
                link.close(NT // 2)
                link(dve.memset(kv[:, :, :], 0.0))
                dve.wait_ge(s["kv_done"], 1)
                for m in range(KC):
                    for h in range(HB):
                        b = slice(h * HCOLS, (h + 1) * HCOLS)
                        ins = dve.tensor_scalar(kv[b, m, b], psKV[m][b, b], 1.0 / N, None, ALU.mult)
                        link(ins)
                dve.nop().then_inc(s["kv_set"], 1)
                def finish(n, u):
                    dve.wait_ge(s["y_ready"], n + 1)
                    dve.wait_ge(s["step"], n + (link.base + link.k + 1))
                    r = res[:, u, :, :].rearrange("p t d -> p (t d)")
                    dve.tensor_tensor(r, r, psY[0:P, :], ALU.add).then_inc(s["done"], 1)

                for i, first in turns(dve, NCH // RING):
                    for u in range(RING):
                        n = i * RING + u
                        begun = not (first and u == 0)
                        dve.wait_ge(s["ret_ready"], n + 1)
                        if begun:
                            dve.wait_ge(s["h_ready"], n)
                        for m in range(KC):
                            dve.tensor_tensor(retT[:, m, :], psKV[m][:, 0:CH], XT[:, m, dyn(n, first, CH, CH)], ALU.add).then_inc(s["retT_ready"], 1)
                        dve.wait_ge(res_in[u], i * 32 + 32)
                        dve.tensor_tensor(res[:, u, :, :], res[:, u, :, :], xnr[:, u, :, :], ALU.add).then_inc(s["step"], 1)
                        if begun:
                            finish(n - 1, (u - 1) % RING)
                finish(NCH - 1, RING - 1)


def slice_attention(nc, c, tag, x, xnT, W_fx, b_fx, W_x, b_x, W_slice, b_slice, W_q, W_k, W_v, W_out, b_out, temperature,
                    wT_dram, out):
    G = W_slice.shape[1]
    HD = W_slice.shape[0]
    INNER = W_fx.shape[1]
    H = INNER // HD
    M = INNER // 128
    with Room(nc, tag) as room:
        XT = room.sb("XT", [128, KC, N])
        wfx = room.sb("wfx", [128, KC, INNER])
        wx = room.sb("wx", [128, KC, INNER])
        wsl = room.sb("wsl", [128, 128])
        small_w = room.sb("small_w", [HD, 3, HD])
        wout = room.sb("wout", [HD, H, D])
        bfx = room.sb("bfx", [1, INNER])
        bout = room.sb("bout", [1, D])
        bsl = room.sb("bsl", [1, H, G])
        bslr = room.sb("bslr", [1, G])
        bxc = room.sb("bxc", [128, M])
        temp = room.sb("temp", [P, H])
        xs = room.sb("xs", [128, 2, KC, P])
        xm = room.sb("xm", [128, 2, M, P])
        fx = room.sb("fx", [P, 2, INNER])
        w = room.sb("w", [P, 2, H, G])
        mx = room.sb("mx", [P, H])
        wT = room.sb("wT", [128, 2, M, P])
        norm = room.sb("norm", [128, M])
        tok = room.sb("tok", [128, M, HD])
        tokT = room.sb("tokT", [HD, M * 128])
        qk = room.sb("qk", [HD, 2, M * 128])
        at = room.sb("at", [G, H, G])
        am = room.sb("am", [G, H])
        atT = room.sb("atT", [G, H * G])
        val = room.sb("val", [G, H, HD])
        osT = room.sb("osT", [HD, H, G])
        mixm = room.sb("mixm", [128, M, D])
        res = room.sb("res", [P, RING, D])
        wTin = room.sb("wTin", [128, RING, M, P])
        ps = [room.ps(f"ps{n}", [128, 512]) for n in range(8)]
        psX, psL, psF, psT, psTok, psNorm = ps[0:6]
        names = ("loaded", "step", "wsl_zero", "xs_ready", "x_ready", "xm_ready", "l_ready", "shifted", "exped", "w_ready", "f_ready",
                 "fx_ready", "tok_added", "turned", "wT_ready", "tok_done", "stage", "stage_done", "o_ready", "done", "sl_in",
                 "att_shifted", "att_exped", "wT_free")
        s = {n: room.sem(n) for n in names}
        wT_out = room.sem("wT_out")
        res_in, res_out = ([room.sem(f"{n}{u}") for u in range(RING)] for n in ("res_in", "res_out"))
        LOADED = 16 * 12
        with nc.Block() as block:

            @block.sync
            def _(sp):
                def load(dst, src):
                    with nc.allow_non_contiguous_dma(reason="short vectors as columns"):
                        sp.dma_start(dst, src).then_inc(s["loaded"], 16)
                load(XT[:, :, :], xnT)
                load(wfx[:, :, :], W_fx.rearrange("(k p) w -> p k w", p=128))
                load(wx[:, :, :], W_x.rearrange("(k p) w -> p k w", p=128))
                for n, v in enumerate((W_q, W_k, W_v)):
                    load(small_w[:, n, :], v)
                load(wout[:, :, :], W_out.rearrange("(h c) d -> c h d", c=HD))
                load(bfx[:, :], b_fx.rearrange("(a n) -> a n", a=1))
                load(bout[:, :], b_out.rearrange("(a n) -> a n", a=1))
                load(bslr[:, :], b_slice.rearrange("(a n) -> a n", a=1))
                load(bxc[:, :], b_x.rearrange("(m p) -> p m", p=128))
                load(temp[:, :], temperature.rearrange("a h b d -> (a h b d)").partition_broadcast(P))
                sp.wait_ge(s["wsl_zero"], 1)
                sp.dma_start(wsl[0:HD, 0:G], W_slice).then_inc(s["sl_in"], 16)
                sp.dma_start(wsl[HD:128, G:128], W_slice).then_inc(s["sl_in"], 16)
                for i, first in turns(sp, NT // 2):
                    for u in range(2):
                        t = i * 2 + u
                        sp.wait_ge(s["wT_ready"], t + 1)
                        sp.nop(nofuse=True)
                        sp.dma_start(wT_dram[dyn(t, first, 1, 1), :, :].rearrange("t p n -> p (t n)"),
                                     wT[:, u, :, :].rearrange("p m n -> p (m n)")).then_inc(wT_out, 16)
                        sp.wait_ge(wT_out, t * 16 + 16)
                        sp.nop().then_inc(s["wT_free"], 1)
                for i, first in turns(sp, NT // RING):
                    for u in range(RING):
                        t = i * RING + u
                        if not first:
                            sp.wait_ge(res_out[u], i * 16)
                        sp.dma_start(res[:, u, :], x[dyn(t, first, P, P), :]).then_inc(res_in[u], 16)
                        sp.dma_start(wTin[:, u, :, :].rearrange("p m n -> p (m n)"),
                                     wT_dram[dyn(t, first, 1, 1), :, :].rearrange("t p n -> p (t n)")).then_inc(res_in[u], 16)

            @block.gpsimd
            def _(pool):
                pool.memset(wsl[:, :], 0.0).then_inc(s["wsl_zero"], 1)

            @block.scalar
            def _(act):
                act.wait_ge(s["loaded"], LOADED)
                act.nop().then_inc(s["wT_free"], 2)

                def keep(t, u):
                    act.wait_ge(s["turned"], t + 1)
                    act.wait_ge(s["wT_free"], t + 1)
                    act.activation(wT[:, u, :, :].rearrange("p m n -> p (m n)"), psT[:, 0:M * P], ACT.Copy).then_inc(s["wT_ready"], 1)

                for i, first in turns(act, NT // 2):
                    for u in range(2):
                        t = i * 2 + u
                        if not first:
                            act.wait_ge(s["f_ready"], t - 1)
                            act.nop(nofuse=True)
                        act.activation(xs[:, u, :, :], XT[:, :, dyn(t, first, P, P)], ACT.Copy).then_inc(s["xs_ready"], 1)
                        act.wait_ge(s["x_ready"], t + 1)
                        if not first:
                            act.wait_ge(s["l_ready"], t - 1)
                        for m in range(M):
                            act.activation(xm[:, u, m, :], psX[:, m * P:(m + 1) * P], ACT.Identity, bias=bxc[:, m:m + 1])\
                               .then_inc(s["xm_ready"], 1)
                        act.wait_ge(s["f_ready"], t + 1)
                        if not first:
                            act.wait_ge(s["tok_added"], t - 1)
                        act.activation(fx[:, u, :], psF[0:P, :], ACT.Copy).then_inc(s["fx_ready"], 1)
                        act.wait_ge(s["shifted"], t + 1)
                        act.activation(w[:, u, :, :], w[:, u, :, :], ACT.Exp).then_inc(s["exped"], 1)
                        if not (first and u == 0):
                            keep(t - 1, 1 - u)
                keep(NT - 1, 1)
                act.wait_ge(s["att_shifted"], 1)
                act.activation(at[:, :, :], at[:, :, :], ACT.Exp, scale=float(HD) ** -0.5).then_inc(s["att_exped"], 1)
                for i, first in turns(act, NT // RING):
                    for u in range(RING):
                        t = i * RING + u
                        act.wait_ge(s["done"], t + 1)
                        act.dma_start(out[dyn(t, first, P, P), :], res[:, u, :]).then_inc(res_out[u], 16)
                for u in range(RING):
                    act.wait_ge(res_out[u], 16 * (NT // RING))

            @block.tensor
            def _(pe):
                pe.wait_ge(s["loaded"], LOADED)
                pe.wait_ge(s["sl_in"], 32)
                pe.wait_ge(s["stage_done"], 1)

                def gather_tokens(t, u, opens):
                    pe.wait_ge(s["w_ready"], t + 1)
                    pe.wait_ge(s["fx_ready"], t + 1)
                    flat = w[:, u, :, :].rearrange("p h g -> p (h g)")
                    for m in range(M):
                        cols = slice(m * 128, (m + 1) * 128)
                        begin = opens and m == 0
                        pe.matmul(psTok[:, cols], flat[:, cols], fx[:, u, cols], start=begin, stop=False, skip_group_check=True)
                        mm = pe.matmul(psNorm[:, m:m + 1], flat[:, cols], c["ones"][0:P, 0:1], start=begin, stop=False, skip_group_check=True)
                    mm.then_inc(s["tok_added"], 1)
                    if not opens:
                        pe.wait_ge(s["wT_ready"], t)
                    for m in range(M):
                        mm = pe.transpose(psT[:, m * P:(m + 1) * P], flat[:, m * 128:(m + 1) * 128], c["ident"][0:P, 0:P])
                    mm.then_inc(s["turned"], 1)

                for i, first in turns(pe, NT // 2):
                    for u in range(2):
                        t = i * 2 + u
                        begun = not (first and u == 0)
                        if begun:
                            pe.wait_ge(s["xm_ready"], t * M)
                        for m in range(M):
                            for k in range(KC):
                                mm = pe.matmul(psX[:, m * P:(m + 1) * P], wx[:, k, m * 128:(m + 1) * 128], XT[:, k, dyn(t, first, P, P)],
                                               start=(k == 0), stop=(k == KC - 1))
                        mm.then_inc(s["x_ready"], 1)
                        pe.wait_ge(s["xs_ready"], t + 1)
                        if begun:
                            pe.wait_ge(s["fx_ready"], t)
                        pe.matmul(psF[0:P, :], c["ones"][0:1, 0:P], bfx[:, :], start=True, stop=False)
                        for k in range(KC):
                            mm = pe.matmul(psF[0:P, :], xs[:, u, k, :], wfx[:, k, :], start=False, stop=(k == KC - 1))
                        mm.then_inc(s["f_ready"], 1)
                        pe.wait_ge(s["xm_ready"], t * M + M)
                        if begun:
                            pe.wait_ge(s["shifted"], t)
                        for m in range(M):
                            cols = slice(m * 128, (m + 1) * 128)
                            pe.matmul(psL[0:P, cols], c["ones"][0:1, 0:P], bsl[:, :, :].rearrange("a h g -> a (h g)")[:, cols], start=True, stop=False)
                            mm = pe.matmul(psL[0:P, cols], xm[:, u, m, :], wsl[:, :], start=False, stop=True)
                        mm.then_inc(s["l_ready"], 1)
                        if begun:
                            gather_tokens(t - 1, 1 - u, first and u == 1)
                gather_tokens(NT - 1, 1, False)
                pe.matmul(psTok[:, :], c["zero"][0:1, :], bc(c["zero"][0:1, :], 1, 4), start=False, stop=True, skip_group_check=True)
                pe.matmul(psNorm[:, 0:M], c["zero"][0:1, :], c["zero"][0:1, 0:M], start=False, stop=True, skip_group_check=True).then_inc(s["tok_done"], 1)
                pe.wait_ge(s["wT_ready"], NT)
                pe.wait_ge(s["stage_done"], 2)
                for m in range(M):
                    mm = pe.transpose(psX[0:HD, m * 128:(m + 1) * 128], tok[:, m, :], c["ident"][:, :])
                mm.then_inc(s["stage"], 1)
                pe.wait_ge(s["stage_done"], 3)
                for n in range(2):
                    mm = pe.matmul(ps[1 + n][0:HD, :], small_w[:, n, :], tokT[:, :], start=True, stop=True)
                for h in range(H):
                    mm = pe.matmul(psT[0:G, h * HD:(h + 1) * HD], tokT[:, h * G:(h + 1) * G], small_w[:, 2, :], start=True, stop=True)
                mm.then_inc(s["stage"], 1)
                pe.wait_ge(s["stage_done"], 4)
                for h in range(H):
                    mm = pe.matmul(psX[0:G, h * G:(h + 1) * G], qk[:, 0, h * G:(h + 1) * G], qk[:, 1, h * G:(h + 1) * G], start=True, stop=True)
                mm.then_inc(s["stage"], 1)
                pe.wait_ge(s["stage_done"], 5)
                for h in range(H):
                    mm = pe.transpose(psL[0:G, h * G:(h + 1) * G], at[:, h, :], c["ident"][0:G, 0:G])
                mm.then_inc(s["stage"], 1)
                pe.wait_ge(s["stage_done"], 6)
                for h in range(H):
                    mm = pe.matmul(psF[0:HD, h * G:(h + 1) * G], val[:, h, :], atT[:, h * G:(h + 1) * G], start=True, stop=True)
                mm.then_inc(s["stage"], 1)
                pe.wait_ge(s["stage_done"], 7)
                for h in range(H):
                    mm = pe.matmul(ps[4 + h % 2 * 2 + h // 4][0:G, h // 2 % 2 * D:(h // 2 % 2 + 1) * D], osT[:, h, :], wout[:, h, :], start=True, stop=True)
                mm.then_inc(s["stage"], 1)
                pe.wait_ge(s["stage_done"], 8)
                for i, first in turns(pe, NT // RING):
                    for u in range(RING):
                        t = i * RING + u
                        pe.wait_ge(res_in[u], i * 32 + 32)
                        if not first:
                            pe.wait_ge(s["done"], t - (RING - 1))
                        o = ps[u]
                        pe.matmul(o[0:P, 0:D], c["ones"][0:1, 0:P], bout[:, :], start=True, stop=False)
                        for m in range(M):
                            mm = pe.matmul(o[0:P, 0:D], wTin[:, u, m, :], mixm[:, m, :], start=False, stop=(m == M - 1))
                        mm.then_inc(s["o_ready"], 1)

            @block.vector
            def _(dve):
                link = Link(dve, s["step"])
                dve.wait_ge(s["loaded"], LOADED)
                link.put(dve.tensor_copy(bsl[:, :, :], bc(bslr[:, :], 1, H)))
                link(dve.tensor_scalar(temp[:, :], temp[:, :], 0.1, 5.0, ALU.max, ALU.min))
                link(dve.reciprocal(temp[:, :], temp[:, :]))
                dve.nop().then_inc(s["stage_done"], 1)
                link.begin(2 * 4)
                for i, first in turns(dve, NT // 2):
                    link.turn(i)
                    for u in range(2):
                        t = i * 2 + u
                        wu = w[:, u, :, :]
                        dve.wait_ge(s["l_ready"], t + 1)
                        if not first:
                            dve.wait_ge(s["turned"], t - 1)
                        link(dve.tensor_tensor(wu, psL[0:P, :].rearrange("p (h g) -> p h g", g=G), bc(temp[:, :], 2, G), ALU.mult))
                        link(dve.tensor_reduce(mx[:, :], wu, AX, ALU.max))
                        dve.tensor_tensor(wu, wu, bc(mx[:, :], 2, G), ALU.subtract).then_inc(s["shifted"], 1)
                        dve.wait_ge(s["exped"], t + 1)
                        link(dve.tensor_reduce(mx[:, :], wu, AX, ALU.add))
                        link(dve.reciprocal(mx[:, :], mx[:, :]))
                        dve.tensor_tensor(wu, wu, bc(mx[:, :], 2, G), ALU.mult).then_inc(s["w_ready"], 1)
                link.close(NT // 2)
                dve.wait_ge(s["tok_done"], 1)
                link(dve.tensor_scalar(norm[:, :], psNorm[:, 0:M], 1e-5, None, ALU.add))
                link(dve.reciprocal(norm[:, :], norm[:, :]))
                for m in range(M):
                    for a in range(2):
                        r = slice(a * G, (a + 1) * G)
                        link(dve.tensor_scalar(tok[r, m, :], psTok[r, m * 128 + a * HD:m * 128 + (a + 1) * HD], norm[r, m:m + 1], None, ALU.mult))
                dve.nop().then_inc(s["stage_done"], 1)
                dve.wait_ge(s["stage"], 1)
                link(dve.tensor_copy(tokT[:, :], psX[0:HD, :]))
                dve.nop().then_inc(s["stage_done"], 1)
                dve.wait_ge(s["stage"], 2)
                for n in range(2):
                    link(dve.tensor_copy(qk[:, n, :], ps[1 + n][0:HD, :]))
                link(dve.tensor_copy(val[:, :, :], psT[0:G, :].rearrange("k (h c) -> k h c", h=H)))
                dve.nop().then_inc(s["stage_done"], 1)
                dve.wait_ge(s["stage"], 3)
                lg = psX[0:G, :].rearrange("g (h k) -> g h k", h=H)
                link(dve.tensor_reduce(am[:, :], lg, AX, ALU.max))
                link(dve.tensor_tensor(at[:, :, :], lg, bc(am[:, :], 2, G), ALU.subtract))
                dve.nop().then_inc(s["att_shifted"], 1)
                dve.wait_ge(s["att_exped"], 1)
                link(dve.tensor_reduce(am[:, :], at[:, :, :], AX, ALU.add))
                link(dve.reciprocal(am[:, :], am[:, :]))
                link(dve.tensor_tensor(at[:, :, :], at[:, :, :], bc(am[:, :], 2, G), ALU.mult))
                dve.nop().then_inc(s["stage_done"], 1)
                dve.wait_ge(s["stage"], 4)
                link(dve.tensor_copy(atT[:, :], psL[0:G, :]))
                dve.nop().then_inc(s["stage_done"], 1)
                dve.wait_ge(s["stage"], 5)
                link(dve.tensor_copy(osT[:, :, :], psF[0:HD, :].rearrange("c (h g) -> c h g", h=H)))
                dve.nop().then_inc(s["stage_done"], 1)
                dve.wait_ge(s["stage"], 6)
                for a in range(2):
                    for b in range(2):
                        v = ps[4 + a * 2 + b][0:G, :].rearrange("g (m d) -> g m d", m=2)
                        link(dve.tensor_copy(mixm[a * G:(a + 1) * G, 2 * b:2 * b + 2, :], v))
                dve.nop().then_inc(s["stage_done"], 1)
                for i, first in turns(dve, NT // RING):
                    for u in range(RING):
                        t = i * RING + u
                        dve.wait_ge(s["o_ready"], t + 1)
                        dve.wait_ge(res_in[u], i * 32 + 32)
                        dve.tensor_tensor(res[:, u, :], res[:, u, :], ps[u][0:P, 0:D], ALU.add).then_inc(s["done"], 1)


SHARES = (TURNS * 2 // 10, TURNS * 5 // 10)


def program(nc, a, out):
    def dram(name, shape, dt=F32):
        return nc.dram_tensor(name, shape, dt, kind="Internal").ap()

    with Room(nc, "const") as fixed:
        c = constants(nc, fixed)
        H, HC = a["L0_gnn_att_src"].shape
        X = a["L0_ffn_router_w"].shape[0]
        HW = a["L1_gnn_W1"].shape[1]
        xnT = [dram(f"xnT{k}", (128, KC, N)) for k in range(4)]
        xn_rows, mixed0, x1, x2, mixed1, x3, table0 = (
            dram(n, (N, D)) for n in ("xn_rows", "mixed0", "x1", "x2", "mixed1", "x3", "table0"))
        src_part0, dst_part0, logits = dram("src_part0", (N, H)), dram("dst_part0", (N, H)), dram("logits", (N, X))
        src_slots, dst_slots, weights0 = (dram(n, (128, H, TPAD)) for n in ("src_slots", "dst_slots", "weights0"))
        table1, key_part1 = dram("table1", (N, D + 2)), dram("key_part1", (N, 2))
        rec = [dram(f"rec{g}", (TPAD * TILE, 2), I32) for g in range(2)]
        tile_end = [dram(f"tile_end{g}", (1, NT)) for g in range(2)]
        idx = [dram(f"idx{g}", (128, TPAD), I32) for g in range(2)]
        flat_loc = [dram(f"flat_loc{g}", (TPAD * TILE,)) for g in range(2)]
        blk = [dram(f"blk{g}", (1, TPAD), I32) for g in range(2)]
        loc = [dram(f"loc{g}", (128, TPAD)) for g in range(2)]
        blk_off = [dram(f"blk_off{g}", (1, TPAD), I32) for g in range(2)]

        pairs = dram("pairs", (E, 2), I32)
        order_edges(nc, c, "order", a["src"], a["dst"], pairs)
        att = [(a[f"L0_gnn_att_{end}"][h, :], h * HC, n * H + h) for n, end in enumerate(("src", "dst")) for h in range(H)]
        with Room(nc, "by_source") as room1:
            with Room(nc, "by_target") as room0:
                send1, send0 = Sender(nc, room1, rec[1]), Sender(nc, room0, rec[0])
                place_edges(nc, c, "sort0", pairs, 1, send0, tile_end[0])
                project_rows(nc, c, "ln0", a["x"], xnT[0], None, [(a["L0_gnn_W"], 0)], att,
                             [(table0, 0, D), (src_part0, D, H), (dst_part0, D + H, H)],
                             lambda pool: send0.send(pool, 0, SHARES[0]))
                mix_keys(nc, c, "mix0", a["x"], xnT[0], *(a[f"L0_mix_{n}"] for n in (
                    "W_qk", "b_qk", "W_v", "b_v", "gamma", "beta")), mixed0, lambda pool: send0.send(pool, SHARES[0], SHARES[1]))
                place_edges(nc, c, "sort1", pairs, 0, send1, tile_end[1],
                            lambda pool: send0.send(pool, SHARES[1], TURNS))
            lay_slots(nc, c, "slots0", rec[0], tile_end[0], idx[0], loc[0], flat_loc[0], blk[0], blk_off[0], D + H)
            spread_parts(nc, c, "spread0", flat_loc[0], blk[0], dst_part0, dst_slots, (idx[0], src_part0, src_slots))
            softmax_weights(nc, c, "soft", rec[0], src_slots, dst_slots, weights0)
            sum_edges(nc, c, "edges0", idx[0], loc[0], blk_off[0], table0, H, weights0, None,
                      ("relu", mixed0, a["L0_gnn_bias"], x1))
            project_rows(nc, c, "ln1", x1, xnT[1], None, [(a["L0_ffn_router_w"].rearrange("e c -> c e"), 0)], [], [(logits, 0, X)])
            experts(nc, c, "moe", x1, xnT[1], logits, a["L0_ffn_w1"], a["L0_ffn_w2"], a["L0_ffn_w3"], x2,
                    lambda pool: send1.send(pool, 0, TURNS))
        lay_slots(nc, c, "slots1", rec[1], tile_end[1], idx[1], loc[1], flat_loc[1], blk[1], blk_off[1], D + 2)

        halves = [(a[f"L1_gnn_a{n + 1}"][0, end * HW:(end + 1) * HW], n * HW, col) for n in range(2) for end, col in ((1, n), (0, 2 + n))]
        project_rows(nc, c, "ln2", x2, xnT[2], xn_rows, [(a["L1_gnn_W1"], 0), (a["L1_gnn_W2"], HW)], halves,
                     [(table1, 0, D + 2), (key_part1, D + 2, 2)])
        mix_heads(nc, c, "mix1", x2, xn_rows, xnT[2], *(a[f"L1_mix_{n}"] for n in (
            "w_qkv", "b_qkv", "kln_g", "kln_b", "vln_g", "vln_b", "w1", "b1", "w2", "b2")), mixed1)
        sum_edges(nc, c, "edges1", idx[1], loc[1], blk_off[1], table1, 2, None,
                  (flat_loc[1], blk[1], key_part1), ("elu", mixed1, None, x3))
        project_rows(nc, c, "ln3", x3, xnT[3], None, [], [], [])
        slice_attention(nc, c, "slice", x3, xnT[3], *(a[f"L1_ffn_{n}"] for n in (
            "W_fx", "b_fx", "W_x", "b_x", "W_slice", "b_slice", "W_q", "W_k", "W_v", "W_out", "b_out", "temperature")),
            dram("slices", (NT, 128, KC * 2 * P)), out)


def kernel(**inputs):
    import numpy as _np
    import concourse.bacc as _bacc
    from concourse import mybir as _mybir
    from concourse.bass_utils import run_bass_kernel_spmd as _run

    nc = _bacc.Bacc("TRN2", target_bir_lowering=False, num_devices=1)
    arrays, args = {}, {}
    for name in inputs:
        v = _np.ascontiguousarray(inputs[name])
        arrays[f"in_{name}"] = v
        args[name] = nc.dram_tensor(f"in_{name}", v.shape, _mybir.dt.from_np(v.dtype), kind="ExternalInput").ap()
    out = nc.dram_tensor("out_dram", (N, D), F32, kind="ExternalOutput").ap()
    program(nc, args, out)
    r = _run(nc, [arrays], core_ids=[0])
    return r.results[0]["out_dram"]
```
